# Optimizing a Trainium2 kernel written in Bass

```python
import numpy as np
import jax
import jax.numpy as jnp

def _softmax(x, axis=-1):
    return jax.nn.softmax(x, axis=axis)

def _gelu(x):
    return jax.nn.gelu(x, approximate=True)

def _silu(x):
    return jax.nn.silu(x)

def _sigmoid(x):
    return jax.nn.sigmoid(x)

def _layernorm(x, axis=-1, eps=1e-05):
    m = jnp.mean(x, axis=axis, keepdims=True)
    v = jnp.var(x, axis=axis, keepdims=True)
    return (x - m) / jnp.sqrt(v + eps)

def _scatter_add(tgt, idx, src, axis=0):
    return tgt.at[idx].add(src)

def _segment_sum(src, seg, n):
    return jax.ops.segment_sum(src, seg, n)
kernel_name = 'mk_adaln_ffn_d2_seqx_r8_19e266'

def setup_inputs(seed: int=0):
    np.random.seed(seed)
    _w = jnp.asarray

    def _rec_inputs():
        import jax
        import jax.numpy as jnp
        _rk = jax.random.key(seed)
        x = 7.22e-05 + 1 * jax.random.normal(jax.random.fold_in(_rk, 1), (16, 128, 128), jnp.float32)
        _lenS = 128 - jax.random.randint(jax.random.fold_in(_rk, 7), (16,), 0, max(1, 128 // 4) + 1, jnp.int32)
        _lenS2 = 128 - jax.random.randint(jax.random.fold_in(_rk, 8), (16,), 0, max(1, 128 // 4) + 1, jnp.int32)
        fside_BxSxS_0 = 4.13588e-05 + 0.999923 * jax.random.normal(jax.random.fold_in(_rk, 11), (16, 128, 128), jnp.float32)
        itok_B_18_1004 = jax.random.randint(jax.random.fold_in(_rk, 12), (16,), 18, 1005, jnp.int32)
        itok_B_0_2 = jax.random.randint(jax.random.fold_in(_rk, 13), (16,), 0, 3, jnp.int32)
        return (x, fside_BxSxS_0, itok_B_18_1004, itok_B_0_2)
    x, fside_BxSxS_0, itok_B_18_1004, itok_B_0_2 = _rec_inputs()

    def _L0_cond_setup():
        import jax, jax.numpy as jnp
        import numpy as np
        B, L1, L2, DIN, DOUT, H = (8, 128, 128, 128, 128, 16)
        DH = DOUT // H
        SCALE = 1.0 / np.sqrt(DH).astype(np.float32)
        key = jax.random.key(seed)
        ks = jax.random.split(key, 13)
        s = 0.02
        return {'seq1': jax.random.normal(ks[0], (B, L1, DIN), jnp.float32), 'seq2': jax.random.normal(ks[1], (B, L2, DIN), jnp.float32), 'seq_len1': jax.random.randint(ks[2], (B,), 1, L1 + 1, jnp.int32), 'Wq': jax.random.normal(ks[3], (DIN, DOUT), jnp.float32) * s, 'bq': jnp.zeros((DOUT,), jnp.float32), 'Wk': jax.random.normal(ks[4], (DIN, DOUT), jnp.float32) * s, 'bk': jnp.zeros((DOUT,), jnp.float32), 'Wv': jax.random.normal(ks[5], (DIN, DOUT), jnp.float32) * s, 'bv': jnp.zeros((DOUT,), jnp.float32), 'Wo': jax.random.normal(ks[6], (DOUT, DOUT), jnp.float32) * s, 'bo': jnp.zeros((DOUT,), jnp.float32), 'b_prev': jax.random.normal(ks[7], (1, 1, DIN), jnp.float32) * s, 'b_self': jax.random.normal(ks[8], (1, 1, DIN), jnp.float32) * s}
    _L0_cond_all = _L0_cond_setup()
    _L0_cond_in = {k: v for k, v in _L0_cond_all.items() if k in ('Wq', 'bq', 'Wk', 'bk', 'Wv', 'bv', 'Wo', 'bo', 'b_prev', 'b_self')}
    del _L0_cond_all

    def _L0_ffn_setup():
        import jax, jax.numpy as jnp
        import numpy as np
        from jax import lax
        D_MODEL = 128
        D_FF = 512
        NUM_EXPERTS = 24
        TOP_K = 2
        key = jax.random.key(seed)
        ks = jax.random.split(key, 7)
        s1 = 1.0 / np.sqrt(D_MODEL)
        s2 = 1.0 / np.sqrt(D_FF)
        x = jax.random.normal(ks[0], (2, 128, D_MODEL), dtype=jnp.float32)
        gate_w = jax.random.uniform(ks[1], (D_MODEL, NUM_EXPERTS), jnp.float32, -s1, s1)
        gate_b = jax.random.uniform(ks[2], (NUM_EXPERTS,), jnp.float32, -s1, s1)
        w1 = jax.random.uniform(ks[3], (NUM_EXPERTS, D_MODEL, D_FF), jnp.float32, -s1, s1)
        b1 = jax.random.uniform(ks[4], (NUM_EXPERTS, D_FF), jnp.float32, -s1, s1)
        w2 = jax.random.uniform(ks[5], (NUM_EXPERTS, D_FF, D_MODEL), jnp.float32, -s2, s2)
        b2 = jax.random.uniform(ks[6], (NUM_EXPERTS, D_MODEL), jnp.float32, -s2, s2)
        return {'x': x, 'gate_w': gate_w, 'gate_b': gate_b, 'w1': w1, 'b1': b1, 'w2': w2, 'b2': b2}
    _L0_ffn_all = _L0_ffn_setup()
    _L0_ffn_in = {k: v for k, v in _L0_ffn_all.items() if k in ('gate_w', 'gate_b', 'w1', 'b1', 'w2', 'b2')}
    del _L0_ffn_all

    def _L1_cond_setup():
        import jax, jax.numpy as jnp
        import numpy as np
        NEG_INF = -1e+30
        key = jax.random.key(seed)
        k1, k2, k3, k4, k5 = jax.random.split(key, 5)
        B, S, D, A = (16, 128, 128, 32)
        hidden = jax.random.normal(k1, (B, S, D), dtype=jnp.float32)
        W1 = jax.random.normal(k2, (D, A), dtype=jnp.float32) / np.sqrt(D)
        b1 = jax.random.normal(k3, (A,), dtype=jnp.float32) * 0.01
        v = jax.random.normal(k4, (A,), dtype=jnp.float32) / np.sqrt(A)
        prompt_type_ids = jax.random.randint(k5, (B,), 0, 3, dtype=jnp.int32)
        return {'hidden': hidden, 'W1': W1, 'b1': b1, 'v': v, 'prompt_type_ids': prompt_type_ids}
    _L1_cond_all = _L1_cond_setup()
    _L1_cond_in = {k: v for k, v in _L1_cond_all.items() if k in ('W1', 'b1', 'v')}
    del _L1_cond_all

    def _L1_ffn_setup():
        import jax, jax.numpy as jnp
        import numpy as np
        B, S, D = (1, 256, 128)
        E, K, F = (8, 2, 176)
        NS = 2
        SCALE = 2.5

        def _swiglu_mlp(x, wg, wu, wd):
            return jax.nn.silu(x @ wg) * (x @ wu) @ wd
        key = jax.random.key(seed)
        ks = jax.random.split(key, 8)
        s = 0.02
        return {'hidden_states': jax.random.normal(ks[0], (B, S, D), jnp.float32), 'gate_w': jax.random.normal(ks[1], (E, D), jnp.float32) * s, 'w_gate': jax.random.normal(ks[2], (E, D, F), jnp.float32) * s, 'w_up': jax.random.normal(ks[3], (E, D, F), jnp.float32) * s, 'w_down': jax.random.normal(ks[4], (E, F, D), jnp.float32) * s, 'sw_gate': jax.random.normal(ks[5], (D, F * NS), jnp.float32) * s, 'sw_up': jax.random.normal(ks[6], (D, F * NS), jnp.float32) * s, 'sw_down': jax.random.normal(ks[7], (F * NS, D), jnp.float32) * s}
    _L1_ffn_all = _L1_ffn_setup()
    _L1_ffn_in = {k: v for k, v in _L1_ffn_all.items() if k in ('gate_w', 'w_gate', 'w_up', 'w_down', 'sw_gate', 'sw_up', 'sw_down')}
    del _L1_ffn_all
    return {'x': x, 'fside_BxSxS_0': fside_BxSxS_0, 'itok_B_18_1004': itok_B_18_1004, 'itok_B_0_2': itok_B_0_2, 'L0_cond_Wq': _L0_cond_in['Wq'], 'L0_cond_bq': _L0_cond_in['bq'], 'L0_cond_Wk': _L0_cond_in['Wk'], 'L0_cond_bk': _L0_cond_in['bk'], 'L0_cond_Wv': _L0_cond_in['Wv'], 'L0_cond_bv': _L0_cond_in['bv'], 'L0_cond_Wo': _L0_cond_in['Wo'], 'L0_cond_bo': _L0_cond_in['bo'], 'L0_cond_b_prev': _L0_cond_in['b_prev'], 'L0_cond_b_self': _L0_cond_in['b_self'], 'L0_ffn_gate_w': _L0_ffn_in['gate_w'], 'L0_ffn_gate_b': _L0_ffn_in['gate_b'], 'L0_ffn_w1': _L0_ffn_in['w1'], 'L0_ffn_b1': _L0_ffn_in['b1'], 'L0_ffn_w2': _L0_ffn_in['w2'], 'L0_ffn_b2': _L0_ffn_in['b2'], 'L1_cond_W1': _L1_cond_in['W1'], 'L1_cond_b1': _L1_cond_in['b1'], 'L1_cond_v': _L1_cond_in['v'], 'L1_ffn_gate_w': _L1_ffn_in['gate_w'], 'L1_ffn_w_gate': _L1_ffn_in['w_gate'], 'L1_ffn_w_up': _L1_ffn_in['w_up'], 'L1_ffn_w_down': _L1_ffn_in['w_down'], 'L1_ffn_sw_gate': _L1_ffn_in['sw_gate'], 'L1_ffn_sw_up': _L1_ffn_in['sw_up'], 'L1_ffn_sw_down': _L1_ffn_in['sw_down']}

def reference(x, fside_BxSxS_0, itok_B_18_1004, itok_B_0_2, L0_cond_Wq, L0_cond_bq, L0_cond_Wk, L0_cond_bk, L0_cond_Wv, L0_cond_bv, L0_cond_Wo, L0_cond_bo, L0_cond_b_prev, L0_cond_b_self, L0_ffn_gate_w, L0_ffn_gate_b, L0_ffn_w1, L0_ffn_b1, L0_ffn_w2, L0_ffn_b2, L1_cond_W1, L1_cond_b1, L1_cond_v, L1_ffn_gate_w, L1_ffn_w_gate, L1_ffn_w_up, L1_ffn_w_down, L1_ffn_sw_gate, L1_ffn_sw_up, L1_ffn_sw_down):
    import jax
    import jax.numpy as jnp

    def _L0_cond_ref(seq1, seq2, seq_len1, Wq, bq, Wk, bk, Wv, bv, Wo, bo, b_prev, b_self):
        import jax, jax.numpy as jnp
        import numpy as np
        B, L1, L2, DIN, DOUT, H = (8, 128, 128, 128, 128, 16)
        DH = DOUT // H
        SCALE = 1.0 / np.sqrt(DH).astype(np.float32)
        b, l1, _ = seq1.shape
        l2 = seq2.shape[1]
        query = seq2 + b_self
        key = jnp.concatenate([seq1 + b_prev, seq2 + b_self], 1)
        value = jnp.concatenate([seq1, seq2], 1)
        q = (query @ Wq + bq).reshape(b, l2, H, DH).transpose(0, 2, 1, 3)
        k = (key @ Wk + bk).reshape(b, l1 + l2, H, DH).transpose(0, 2, 1, 3)
        v = (value @ Wv + bv).reshape(b, l1 + l2, H, DH).transpose(0, 2, 1, 3)
        score_prev = jnp.einsum('bhqd,bhkd->bhqk', q, k[:, :, :l1]) * SCALE
        score_self = (q * k[:, :, l1:]).sum(-1, keepdims=True) * SCALE
        mask = jnp.arange(l1)[None, :] < seq_len1[:, None]
        score_prev = jnp.where(mask[:, None, None, :], score_prev, -jnp.inf)
        score = jnp.concatenate([score_prev, score_self], -1)
        weights = jax.nn.softmax(score, axis=-1)
        attn = jnp.einsum('bhqk,bhkd->bhqd', weights[..., :-1], v[:, :, :l1])
        attn = attn + weights[..., -1:] * v[:, :, l1:]
        attn = attn.transpose(0, 2, 1, 3).reshape(b, l2, H * DH)
        return attn @ Wo + bo

    def _L0_ffn_ref(x, gate_w, gate_b, w1, b1, w2, b2):
        import jax, jax.numpy as jnp
        import numpy as np
        from jax import lax
        D_MODEL = 128
        D_FF = 512
        NUM_EXPERTS = 24
        TOP_K = 2
        gate_scores = jnp.einsum('bsd,de->bse', x, gate_w) + gate_b
        topk_val, topk_idx = lax.top_k(gate_scores, TOP_K)
        sparse_gates = jax.nn.softmax(topk_val, axis=-1)
        combine = jnp.sum(jax.nn.one_hot(topk_idx, NUM_EXPERTS, dtype=x.dtype) * sparse_gates[..., None], axis=-2)
        h = jax.nn.gelu(jnp.einsum('bsd,edf->besf', x, w1) + b1[None, :, None, :], approximate=False)
        y = jnp.einsum('besf,efd->besd', h, w2) + b2[None, :, None, :]
        out = jnp.einsum('bse,besd->bsd', combine, y)
        return out + x

    def _L1_cond_ref(hidden, W1, b1, v, prompt_type_ids):
        import jax, jax.numpy as jnp
        import numpy as np
        NEG_INF = -1e+30
        B, S, D = hidden.shape
        attn_in = jnp.tanh(jnp.einsum('bsd,da->bsa', hidden, W1) + b1)
        scores = jnp.einsum('bsa,a->bs', attn_in, v)
        idx = jnp.arange(S)
        j = idx[:, None]
        l = idx[None, :]
        prefix_m = l <= j
        postfix_m = l >= j
        cloze_m = l != j
        pt = prompt_type_ids[:, None, None]
        mask = jnp.where(pt == 0, prefix_m[None], jnp.where(pt == 1, postfix_m[None], cloze_m[None]))
        masked_scores = jnp.where(mask, scores[:, None, :], NEG_INF)
        p = jax.nn.softmax(masked_scores, axis=-1)
        cnt = jnp.sum(mask, axis=-1).astype(hidden.dtype)
        pooled = jnp.einsum('bjl,bld->bjd', p, hidden) / cnt[..., None]
        return pooled

    def _L1_ffn_ref(hidden_states, gate_w, w_gate, w_up, w_down, sw_gate, sw_up, sw_down):
        import jax, jax.numpy as jnp
        import numpy as np
        B, S, D = (1, 256, 128)
        E, K, F = (8, 2, 176)
        NS = 2
        SCALE = 2.5

        def _swiglu_mlp(x, wg, wu, wd):
            return jax.nn.silu(x @ wg) * (x @ wu) @ wd
        identity = hidden_states
        x = hidden_states.reshape(-1, hidden_states.shape[-1])
        T = x.shape[0]
        logits = x.astype(jnp.float32) @ gate_w.astype(jnp.float32).T
        scores = jax.nn.softmax(logits, axis=-1)
        topk_w, topk_i = jax.lax.top_k(scores, K)
        topk_w = topk_w / (topk_w.sum(-1, keepdims=True) + 1e-20) * SCALE
        combine = jnp.zeros((T, E), jnp.float32).at[jnp.arange(T)[:, None], topk_i].set(topk_w)
        g = jax.nn.silu(jnp.einsum('td,edf->etf', x, w_gate)) * jnp.einsum('td,edf->etf', x, w_up)
        expert_out = jnp.einsum('etf,efd->etd', g, w_down)
        y = jnp.einsum('te,etd->td', combine, expert_out).astype(x.dtype)
        y = y.reshape(identity.shape)
        return y + _swiglu_mlp(identity, sw_gate, sw_up, sw_down)
    x = x + _L0_ffn_ref(_L0_cond_ref(x, fside_BxSxS_0, itok_B_18_1004, L0_cond_Wq, L0_cond_bq, L0_cond_Wk, L0_cond_bk, L0_cond_Wv, L0_cond_bv, L0_cond_Wo, L0_cond_bo, L0_cond_b_prev, L0_cond_b_self), L0_ffn_gate_w, L0_ffn_gate_b, L0_ffn_w1, L0_ffn_b1, L0_ffn_w2, L0_ffn_b2)
    x = x + _L1_ffn_ref(_L1_cond_ref(x, L1_cond_W1, L1_cond_b1, L1_cond_v, itok_B_0_2), L1_ffn_gate_w, L1_ffn_w_gate, L1_ffn_w_up, L1_ffn_w_down, L1_ffn_sw_gate, L1_ffn_sw_up, L1_ffn_sw_down)
    return x

_drawn_inputs = setup_inputs


def setup_inputs(seed=0):
    import zlib

    import numpy as np

    out = dict(_drawn_inputs(seed))
    spreads = {'L0_cond_bq': (0.0, 0.8),
     'L0_cond_bk': (0.0, 2.0),
     'L0_cond_bv': (0.0, 0.1),
     'L0_cond_bo': (0.0, 0.1)}
    factors = {'fside_BxSxS_0': 8.0,
     'L0_cond_Wq': 8.0,
     'L0_cond_Wk': 8.0,
     'L0_cond_Wv': 6.225,
     'L0_cond_b_prev': 8.0,
     'L0_cond_b_self': 8.0,
     'L0_ffn_gate_b': 3.371,
     'L0_ffn_w1': 4.445,
     'L0_ffn_b1': 5.646,
     'L0_ffn_w2': 3.397,
     'L0_ffn_b2': 8.826,
     'L1_cond_W1': 8.0,
     'L1_cond_b1': 200.0,
     'L1_cond_v': 8.0,
     'L1_ffn_gate_w': 8.0,
     'L1_ffn_w_gate': 8.0,
     'L1_ffn_w_up': 8.0,
     'L1_ffn_w_down': 8.0,
     'L1_ffn_sw_gate': 8.0,
     'L1_ffn_sw_up': 8.0,
     'L1_ffn_sw_down': 8.0}
    for name, (base, spread) in spreads.items():
        noise = np.random.default_rng([zlib.crc32(name.encode()), seed]).standard_normal(out[name].shape)
        drawn = base * np.exp(spread * noise) if base else spread * noise
        out[name] = jnp.asarray(drawn.astype(out[name].dtype))
    for name, factor in factors.items():
        out[name] = (out[name] * factor).astype(out[name].dtype)
    return out
```

```python
from contextlib import ExitStack

import concourse.bass as bass
from concourse import mybir

ALU = mybir.AluOpType
ACT = mybir.ActivationFunctionType
AX_X = mybir.AxisListType.X
F32 = mybir.dt.float32
BF16 = mybir.dt.bfloat16
I32 = mybir.dt.int32
U32 = mybir.dt.uint32

P = 128
B = 16
H = 16
DH = P // H
NG, NJ = 4, 4
SCALE = float(DH) ** -0.5
BIG = 1.0e30

E0, F0 = 24, 512
C0 = F0 // P
REGION = B * P + P
RING = 4
PAD_TILES = RING - 1
MAX_TILES = B * P * 2 // P + E0 + PAD_TILES + 1
XROWS = E0 * REGION + RING * P
YROWS = MAX_TILES * P

E1, F1 = 8, 176
FS = 2 * F1
FE = E1 * F1
NE = FE // P
NSH = [(0, 128), (128, 128), (256, 96)]
NC1 = NE + len(NSH)
A1 = 32
ROUTE_SCALE = 2.5
BLK = 4
NB = B // BLK
W = BLK * P


def attention_moe_kernel(nc, a, out, xs_dram, ys_dram):
    ctx = ExitStack()
    with ctx:
        def sb(name, shape, dt=F32):
            return ctx.enter_context(nc.sbuf_tensor(name, shape, dt))

        def bank(name):
            return ctx.enter_context(nc.psum_tensor(name, [P, 512], F32))

        def sem(name):
            return ctx.enter_context(nc.semaphore(name))

        banks = [bank(f"bank{i}") for i in range(8)]

        ident = sb("ident", [P, P])
        identb = sb("identb", [P, P], BF16)
        before = sb("before", [P, P], BF16)
        onesb = sb("onesb", [P, P], BF16)
        pick_shift = sb("pick_shift", [P, NJ, P], BF16)
        ind = sb("ind", [P, H])
        headmask = sb("headmask", [P, NJ])
        iota_e = sb("iota_e", [P, E0])
        iota_p = sb("iota_p", [P, 1])
        iota_k = sb("iota_k", [P, P])
        region_of = sb("region_of", [P, E0])
        lens_i = sb("lens_i", [P, B], I32)
        lens = sb("lens", [P, B])
        nolen = sb("nolen", [P, B])
        keybias = sb("keybias", [P, B])
        types_i = sb("types_i", [P, B], I32)
        types = sb("types", [P, B])
        is_pre = sb("is_pre", [P, B])
        is_post = sb("is_post", [P, B])
        is_cloze = sb("is_cloze", [P, B])
        count = sb("count", [P, B])
        tmp_b = sb("tmp_b", [P, B])
        tmp_c = sb("tmp_c", [P, B])
        prebias = sb("prebias", [P, P])
        postbias = sb("postbias", [P, P])
        clozebias = sb("clozebias", [P, P])
        poolbias = sb("poolbias", [P, B, P])
        term = sb("term", [P, B, P])
        zrow = sb("zrow", [P, P])
        ones_e = sb("ones_e", [P, E0])
        expert_of = sb("expert_of", [3 * E1, FE], BF16)

        wq, wk, wv, wo = (sb(n, [P, P]) for n in ("wq", "wk", "wv", "wo"))
        cols = sb("cols", [P, 6])
        bvB, boB = sb("bvB", [P, P]), sb("boB", [P, P])
        gate0 = sb("gate0", [P, E0])
        gate0bB = sb("gate0bB", [P, E0])
        cbias = sb("cbias", [P, 3])
        w1c = sb("w1c", [P, A1])
        vcol = sb("vcol", [A1, 1])
        vB = sb("vB", [A1, P])
        gate1 = sb("gate1", [E1, P])
        gate1T = sb("gate1T", [P, E1])
        wg1 = sb("wg1", [P, FE])
        wu1 = sb("wu1", [P, FE])
        wd1 = sb("wd1", [P, NE, P])
        wsg = sb("wsg", [P, FS])
        wsu = sb("wsu", [P, FS])
        wsd = sb("wsd", [P, len(NSH), P])

        xin = [sb(f"xin{i}", [P, P]) for i in range(4)]
        fin = [sb(f"fin{i}", [P, P]) for i in range(4)]
        xfT = [sb(f"xfT{i}", [P, 2 * P]) for i in range(2)]
        kT = [sb(f"kT{i}", [P, P]) for i in range(2)]
        kA = [sb(f"kA{i}", [P, P]) for i in range(2)]
        kd, kv, qb, prod = (sb(n, [P, P]) for n in ("kd", "kv", "qb", "prod"))
        qexp = [sb(f"qexp{i}", [P, NJ, P]) for i in range(2)]
        v9 = [sb(f"v9{i}", [P, H, DH + 1]) for i in range(2)]
        vs = [sb(f"vs{i}", [P, P]) for i in range(2)]
        mx = sb("mx", [P, H])
        mm = sb("mm", [P, H])
        mhl = [sb(f"mhl{i}", [P, NG, 32], BF16) for i in range(2)]
        shT = [sb(f"shT{i}", [P, P], BF16) for i in range(2)]
        sm0 = sb("sm0", [P, H])
        sm = sb("sm", [P, H])
        selfs = sb("selfs", [P, H])
        y_token = sb("y_token", [P, 1])
        ws = [sb(f"ws{i}", [P, H]) for i in range(2)]
        pT = [sb(f"pT{i}", [P, NJ * P]) for i in range(2)]
        den, rec = sb("den", [P, H]), sb("rec", [P, H])
        t1, t2 = sb("t1", [P, P]), sb("t2", [P, P])
        att = [sb(f"att{i}", [P, P]) for i in range(2)]
        attT = [sb(f"attT{i}", [P, P]) for i in range(2)]
        aT = [sb(f"aT{i}", [P, P]) for i in range(2)]
        abuf = [sb(f"abuf{i}", [P, P]) for i in range(4)]
        a_all = sb("a_all", [P, B, P])

        lg = sb("lg", [P, E0])
        top8 = sb("top8", [P, 8])
        topi = sb("topi", [P, 8], U32)
        topf = sb("topf", [P, 2])
        picked = [sb(f"picked{i}", [P, E0], BF16) for i in range(2)]
        onehot = sb("onehot", [P, B, 2, E0])
        gap = sb("gap", [P, B])
        held = sb("held", [P, E0])
        rank = sb("rank", [P, E0])
        rsel = sb("rsel", [P, 2, E0])
        slotf = sb("slotf", [P, B, 2])
        slots = [sb(f"slots{i}", [P, 2], U32) for i in range(4)]
        g1, g2, eg = sb("g1", [P, B]), sb("g2", [P, B]), sb("eg", [P, B])
        ntf = sb("ntf", [P, E0])
        nti = sb("nti", [P, E0], I32)
        incl, excl = sb("incl", [P, E0]), sb("excl", [P, E0])
        below, under = sb("below", [P, E0]), sb("under", [P, E0])
        ej, tj = sb("ej", [P, 1]), sb("tj", [P, 1])
        table = sb("table", [P, 2])
        table_i = sb("table_i", [2, P], I32)
        rounds_f = sb("rounds_f", [P, 1])
        rounds_i = sb("rounds_i", [P, 1], I32)
        rounds = sb("rounds", [P, 1], I32)
        pad_row = sb("pad_row", [P, E0 + RING], F32)
        pad_row_i = sb("pad_row_i", [P, E0 + RING], I32)
        ybase = sb("ybase", [P, E0])
        ysel = sb("ysel", [P, B, 2, E0])
        yoff = sb("yoff", [P, B, 2])
        yslotf = sb("yslotf", [P, B, 2])
        yslot = sb("yslot", [P, B * 2], U32)

        ring = range(RING)
        xt = [sb(f"xt{r}", [P, P]) for r in ring]
        w1 = [sb(f"w1_{r}", [P, F0]) for r in ring]
        w2 = [sb(f"w2_{r}", [P, C0, P]) for r in ring]
        b1 = [sb(f"b1_{r}", [P, C0]) for r in ring]
        b2 = [sb(f"b2_{r}", [P, P]) for r in ring]
        xT = [sb(f"xT{i}", [P, P]) for i in range(2)]
        hT = [sb(f"hT{i}", [P, C0, P]) for i in range(2)]
        yb = [sb(f"yb{r}", [P, P]) for r in ring]

        y1 = [sb(f"y1_{i}", [P, BLK, P]) for i in range(2)]
        y2 = [sb(f"y2_{i}", [P, BLK, P]) for i in range(2)]
        xr = [sb(f"xr{i}", [P, BLK, P]) for i in range(2)]
        mix1 = sb("mix1", [P, BLK, P])
        mix2 = sb("mix2", [P, BLK, P])
        x2 = sb("x2", [P, B, P])
        x2T = sb("x2T", [P, W])
        th = sb("th", [A1, W])
        ms = sb("ms", [P, BLK, P])
        nm = sb("nm", [P, BLK])
        pe_ = sb("pe_", [P, BLK, P])
        psum_ = sb("psum_", [P, BLK])
        sc_, rs_ = sb("sc_", [P, BLK]), sb("rs_", [P, BLK])
        pn = sb("pn", [P, BLK, P])
        pnT = sb("pnT", [P, W])
        plT = [sb(f"plT{i}", [P, W]) for i in range(2)]
        l8 = sb("l8", [P, BLK, E1])
        nl8 = sb("nl8", [P, BLK])
        ls8, e8, pr8 = (sb(n, [P, BLK, E1]) for n in ("ls8", "e8", "pr8"))
        z8, rz8 = sb("z8", [P, BLK]), sb("rz8", [P, BLK])
        top1 = sb("top1", [P, BLK, 8])
        topi1 = sb("topi1", [P, BLK, 8], U32)
        topf1 = sb("topf1", [P, BLK, 2])
        oh1 = sb("oh1", [P, BLK, 2, E1])
        pick1, c8a, c8 = (sb(n, [P, BLK, E1]) for n in ("pick1", "c8a", "c8"))
        s8, r8 = sb("s8", [P, BLK]), sb("r8", [P, BLK])
        c8r, c8s = sb("c8r", [P, BLK, E1]), sb("c8s", [P, BLK, E1])
        cparts = sb("cparts", [P, BLK, 3 * E1], BF16)
        cT = [sb(f"cT{i}", [3 * E1, W], BF16) for i in range(2)]
        sg = [sb(f"sg{i}", [P, W]) for i in range(2)]
        hu = sb("hu", [P, W])
        h1 = sb("h1", [P, NC1, W])
        ob = [sb(f"ob{i}", [P, BLK, P]) for i in range(2)]

        w_att = sem("w_att")
        w_l1 = sem("w_l1")
        pool_const = sem("pool_const")
        dve_const = sem("dve_const")
        cb_in_ps = sem("cb_in_ps")
        cb_ready = sem("cb_ready")
        gT_in_ps = sem("gT_in_ps")
        gT_ready = sem("gT_ready")
        s_in = [sem(f"s_in{i}") for i in range(2)]
        t_in_ps = sem("t_in_ps")
        a_in_ps = sem("a_in_ps")
        y_read = sem("y_read")
        z_read = sem("z_read")
        z_in_ps = sem("z_in_ps")
        x_read = sem("x_read")
        x_in_ps = sem("x_in_ps")
        xfT_ready = sem("xfT_ready")
        kqv_in_ps = sem("kqv_in_ps")
        kT_ready = sem("kT_ready")
        kv_ready = sem("kv_ready")
        kA_ready = sem("kA_ready")
        qk_ready = sem("qk_ready")
        v_ready = sem("v_ready")
        selfA_in_ps = sem("selfA_in_ps")
        reduced = sem("reduced")
        shift_ready = sem("shift_ready")
        shiftT_in_ps = sem("shiftT_in_ps")
        shiftT_ready = sem("shiftT_ready")
        ws_ready = sem("ws_ready")
        scores_in_ps = sem("scores_in_ps")
        exp_done = sem("exp_done")
        pv_done = sem("pv_done")
        att_ready = sem("att_ready")
        att_in_ps = sem("att_in_ps")
        attT_ready = sem("attT_ready")
        out_in_ps = sem("out_in_ps")
        aT_ready = sem("aT_ready")
        a_ready = sem("a_ready")
        a_kept = sem("a_kept")
        logits_in_ps = sem("logits_in_ps")
        picks_ready = sem("picks_ready")
        rank_in_ps = sem("rank_in_ps")
        slots_ready = sem("slots_ready")
        scattered = sem("scattered")
        zeroed = sem("zeroed")
        padded = sem("padded")
        chain_q = sem("chain_q")
        chain_n = sem("chain_n")
        chain_m = sem("chain_m")
        chain_l = sem("chain_l")
        chain_r = sem("chain_r")
        chain_t = sem("chain_t")
        chain_c = sem("chain_c")
        carried = sem("carried")
        chain_x = sem("chain_x")
        chain_h = sem("chain_h")
        table_ready = sem("table_ready")
        table_in_ps = sem("table_in_ps")
        plan_ready = sem("plan_ready")
        gap_exp = sem("gap_exp")
        yslot_ready = sem("yslot_ready")
        tile_in = [sem(f"tile_in{r}") for r in ring]
        xT_in_ps = sem("xT_in_ps")
        xT_ready = sem("xT_ready")
        hid_in_ps = sem("hid_in_ps")
        gelu_done = sem("gelu_done")
        y_in_ps = sem("y_in_ps")
        y_ready = sem("y_ready")
        y_out = [sem(f"y_out{r}") for r in ring]
        gathered = [sem(f"gathered{i}") for i in range(2)]
        xr_in = [sem(f"xr_in{i}") for i in range(2)]
        x2_ready = sem("x2_ready")
        c_pe = sem("c_pe")
        c_act = sem("c_act")
        c_dve = sem("c_dve")
        cond_ready = sem("cond_ready")
        gu_in_ps = sem("gu_in_ps")
        wt_in_ps = sem("wt_in_ps")
        silu_done = sem("silu_done")
        h_ready = sem("h_ready")
        out_acc = sem("out_acc")
        ob_ready = sem("ob_ready")
        ob_out = [sem(f"ob_out{i}") for i in range(2)]

        psB = banks[0:2]
        psA = banks[2:4]
        psY, psZ, psX, psO = banks[4:8]
        ps_ks, ps_q, ps_v, ps_vs = (psY[:, i * P:(i + 1) * P] for i in range(4))
        ps_a, ps_rank, ps_tot = psY[:, 0:128], psY[:, 128:152], psY[:, 152:176]
        ps_lg, ps_self = psY[:, 176:200], psY[:, 200:216]
        ps_k, ps_aT = psZ[:, 0:P], psZ[:, P:2 * P]
        ps_xf, ps_att = psX[:, 0:256], psX[:, 256:384]
        ps_shT = psX[:, 384:448].bitcast(BF16)

        CONSTS = 29
        ALL_CONSTS = CONSTS + 15
        STEPS = B + 3
        ACT_COND, DVE_COND = 6, 5
        LEAD = 6

        def pipeline(eng, step):
            for i in range(LEAD):
                step(i, i % 2, i // 2)
            with eng.Fori(LEAD // 2, B // 2) as n:
                for p in range(2):
                    step(2 * n + p, p, n)
            for i in range(B, STEPS):
                step(i, i % 2, i // 2)

        def known(i):
            return type(i) is int

        def active(i, lag):
            return not known(i) or 0 <= i - lag < B

        def atleast(eng, s, v):
            if not known(v) or v > 0:
                eng.wait_ge(s, v)

        def carry(eng):
            eng.sem_inc(carried, 1)

        PE_STAGES = (0, 1, 2, 4, 5, 6, 9)
        ACT_STAGES = (0, 1, 2, 4, 5, 6)
        DVE_STAGES = (0, 2, 3, 6, 7, 9)

        def beside(cond, stages, c, k):
            for n, at in enumerate(stages):
                if at == c and k < NB:
                    cond(k, n)

        block = ctx.enter_context(nc.Block())

        @block.sync
        def _(sp):
            for dst, name in ((wq, "Wq"), (wk, "Wk"), (wv, "Wv"), (wo, "Wo")):
                sp.dma_start(dst[:, :], a[f"L0_cond_{name}"]).then_inc(w_att, 16)
            for n, ap in enumerate((a["L0_cond_b_prev"].rearrange("a b d -> d (a b)"),
                                    a["L0_cond_b_self"].rearrange("a b d -> d (a b)"),
                                    a["L0_cond_bk"].unsqueeze(1), a["L0_cond_bq"].unsqueeze(1),
                                    a["L0_cond_bo"].unsqueeze(1))):
                sp.dma_start(cols[:, n:n + 1], ap).then_inc(w_att, 16)
            sp.dma_start(cols[0:A1, 5:6], a["L1_cond_b1"].unsqueeze(1)).then_inc(w_att, 16)
            for dst, ap, n in ((bvB, a["L0_cond_bv"], P), (boB, a["L0_cond_bo"], P), (gate0bB, a["L0_ffn_gate_b"], E0),
                               (lens_i, a["itok_B_18_1004"], B), (types_i, a["itok_B_0_2"], B)):
                sp.dma_start(dst[:, :], ap.unsqueeze(0).broadcast_to([P, n])).then_inc(w_att, 16)
            sp.dma_start(gate0[:, :], a["L0_ffn_gate_w"]).then_inc(w_att, 16)

            def load(i, p, n):
                if known(i) and i >= B:
                    return
                if not known(i) or i >= 2:
                    sp.wait_ge(x_in_ps, i - 1)
                sp.dma_start(xin[p][:, :], a["x"][bass.ds(i, 1)].rearrange("o t d -> (o t) d")).then_inc(s_in[p], 16)
                sp.dma_start(fin[p][:, :], a["fside_BxSxS_0"][bass.ds(i, 1)].rearrange("o t d -> (o t) d")).then_inc(s_in[p], 16)

            for i in range(2):
                load(i, i, 0)
            sp.dma_start(w1c[:, :], a["L1_cond_W1"]).then_inc(w_l1, 16)
            sp.dma_start(vcol[:, :], a["L1_cond_v"].unsqueeze(1)).then_inc(w_l1, 16)
            sp.dma_start(gate1[:, :], a["L1_ffn_gate_w"]).then_inc(w_l1, 16)
            sp.dma_start(wg1[:, :].rearrange("d (e f) -> d e f", e=E1), a["L1_ffn_w_gate"].rearrange("e d f -> d e f")).then_inc(w_l1, 16)
            sp.dma_start(wu1[:, :].rearrange("d (e f) -> d e f", e=E1), a["L1_ffn_w_up"].rearrange("e d f -> d e f")).then_inc(w_l1, 16)
            sp.dma_start(wd1[:, :, :], a["L1_ffn_w_down"].rearrange("e f d -> (e f) d").rearrange("(c p) d -> p c d", p=P)).then_inc(w_l1, 16)
            sp.dma_start(wsg[:, :], a["L1_ffn_sw_gate"]).then_inc(w_l1, 16)
            sp.dma_start(wsu[:, :], a["L1_ffn_sw_up"]).then_inc(w_l1, 16)
            for c, (f, m) in enumerate(NSH):
                sp.dma_start(wsd[0:m, c, :], a["L1_ffn_sw_down"][f:f + m, :]).then_inc(w_l1, 16)
            sp.wait_ge(pool_const, 1)
            ys_t = ys_dram.rearrange("(j p) d -> j p d", p=P)
            with sp.Fori(0, MAX_TILES) as j:
                sp.dma_start(ys_t[bass.ds(j, 1)].rearrange("o p d -> (o p) d"), zrow[:, :]).then_inc(zeroed, 16)
            with sp.Fori(1, B // 2) as n:
                for p in range(2):
                    load(2 * n + p, p, n)
            sp.wait_ge(plan_ready, 1)
            with sp.Fori(0, E0 + RING) as e:
                row = sp.value_load(pad_row_i[0:1, bass.ds(e, 1)], min_val=0, max_val=XROWS - P)
                sp.dma_start(xs_dram[bass.ds(row, P)], zrow[:, :]).then_inc(padded, 16)
            sp.wait_ge(scattered, 32 * B)
            sp.wait_ge(padded, 16 * (E0 + RING))
            nr = sp.value_load(rounds[0:1, 0:1], min_val=1, max_val=MAX_TILES // RING)
            w1_d, w2_d = a["L0_ffn_w1"], a["L0_ffn_w2"].rearrange("e (p c) d -> e p c d", c=C0)
            b1_d, b2_d = a["L0_ffn_b1"].rearrange("e (p c) -> e p c", c=C0), a["L0_ffn_b2"]

            def load_tile(j, r, wait):
                if wait is not None:
                    sp.wait_ge(y_ready, wait)
                e = sp.value_load(table_i[0:1, bass.ds(j, 1)], min_val=0, max_val=E0 - 1)
                row = sp.value_load(table_i[1:2, bass.ds(j, 1)], min_val=0, max_val=XROWS - P)
                sp.dma_start(xt[r][:, :], xs_dram[bass.ds(row, P)]).then_inc(tile_in[r], 16)
                sp.dma_start(w1[r][:, :], w1_d[bass.ds(e, 1)].rearrange("o d f -> (o d) f")).then_inc(tile_in[r], 16)
                sp.dma_start(w2[r][:, :, :], w2_d[bass.ds(e, 1)].rearrange("o p c d -> (o p) c d")).then_inc(tile_in[r], 16)
                sp.dma_start(b1[r][:, :], b1_d[bass.ds(e, 1)].rearrange("o p c -> (o p) c")).then_inc(tile_in[r], 16)
                sp.dma_start(b2[r][:, :], b2_d[bass.ds(e, 1)].broadcast_to([P, P])).then_inc(tile_in[r], 16)

            for r in ring:
                load_tile(r, r, None)
            with sp.Fori(1, nr) as n:
                for r in ring:
                    load_tile(RING * n + r, r, RING * n + (r - RING + 1))
            for k in range(NB):
                if k >= 2:
                    sp.wait_ge(x2_ready, k - 1)
                sp.dma_start(xr[k % 2][:, :, :], a["x"][BLK * k:BLK * (k + 1)].rearrange("b t d -> t b d")).then_inc(xr_in[k % 2], 16)
            for k in range(NB):
                sp.wait_ge(ob_ready, k + 1)
                sp.dma_start(out[BLK * k:BLK * (k + 1)].rearrange("b t d -> t b d"), ob[k % 2][:, :, :]).then_inc(ob_out[k % 2], 16)
            for p in range(2):
                sp.wait_ge(ob_out[p], 16 * (NB // 2))

        @block.gpsimd
        def _(pool):
            g = nc.gpsimd

            def select(t, op, pattern, base, mult, fill):
                return g.affine_select(out=t, in_=t, compare_op=op, fill=fill, base=base, pattern=pattern,
                                       channel_multiplier=mult)

            steps = [0]

            def done(ins):
                steps[0] += 1
                ins.then_inc(pool_const, 1)
                pool.wait_ge(pool_const, steps[0])

            done(g.memset(zrow[:, :], 0.0))
            done(g.memset(ident[:, :], 0.0))
            done(select(ident[:, :], ALU.not_equal, [[-1, P]], 0, 1, 1.0))
            done(g.tensor_copy(identb[:, :], ident[:, :]))
            done(g.memset(onesb[:, :], 1.0))
            done(g.memset(before[:, :], 1.0))
            done(select(before[:, :], ALU.is_gt, [[1, P]], 0, -1, 0.0))
            done(g.memset(ind[:, :], SCALE))
            done(select(ind[:, :], ALU.is_ge, [[-DH, H]], 0, 1, 0.0))
            done(select(ind[:, :], ALU.is_ge, [[DH, H]], DH - 1, -1, 0.0))
            done(g.memset(pick_shift[:, :, :], 0.0))
            for g_ in range(NG):
                for part in range(2):
                    done(select(pick_shift[:, :, :], ALU.not_equal, [[-1, NJ], [0, P]], -(32 * g_ + NJ * part), 1, 1.0))
            done(g.memset(mhl[0][:, :, :], 0.0))
            done(g.memset(mhl[1][:, :, :], 0.0))
            done(g.iota(iota_e[:, :], pattern=[[1, E0]], base=0, channel_multiplier=0, allow_small_or_imprecise_dtypes=True))
            done(g.iota(region_of[:, :], pattern=[[REGION, E0]], base=0, channel_multiplier=0, allow_small_or_imprecise_dtypes=True))
            done(g.iota(iota_p[:, :], pattern=[[0, 1]], base=0, channel_multiplier=1, allow_small_or_imprecise_dtypes=True))
            done(g.iota(iota_k[:, :], pattern=[[1, P]], base=0, channel_multiplier=0, allow_small_or_imprecise_dtypes=True))
            done(g.memset(v9[0][:, :, :], 1.0))
            done(g.memset(v9[1][:, :, :], 1.0))
            done(g.memset(held[:, :], 0.0))
            done(g.memset(ones_e[:, :], 1.0))
            assert steps[0] == CONSTS
            done(g.memset(prebias[:, :], 0.0))
            done(select(prebias[:, :], ALU.is_ge, [[-1, P]], 0, 1, -BIG))
            done(g.memset(postbias[:, :], 0.0))
            done(select(postbias[:, :], ALU.is_ge, [[1, P]], 0, -1, -BIG))
            done(g.memset(clozebias[:, :], 0.0))
            done(select(clozebias[:, :], ALU.not_equal, [[-1, P]], 0, 1, -BIG))
            done(g.memset(expert_of[:, :], 0.0))
            for part in range(3):
                v = expert_of[:, :].rearrange("p (e f) -> p e f", e=E1)
                done(select(v, ALU.not_equal, [[-1, E1], [0, F1]], -E1 * part, 1, 1.0))

            pool.wait_ge(chain_c, 11)
            across = lambda t: t[:, :].unsqueeze(1).broadcast_to([P, B, P])
            along = lambda t: t[:, :].unsqueeze(2).broadcast_to([P, B, P])
            done(g.tensor_tensor(poolbias[:, :, :], across(prebias), along(is_pre), ALU.mult))
            for mask, indicator in ((postbias, is_post), (clozebias, is_cloze)):
                done(g.tensor_tensor(term[:, :, :], across(mask), along(indicator), ALU.mult))
                done(g.tensor_tensor(poolbias[:, :, :], poolbias[:, :, :], term[:, :, :], ALU.add))
            assert steps[0] == ALL_CONSTS

            def dispatch(i, p, n):
                if not active(i, 3):
                    return
                q = 1 - p
                pool.wait_ge(slots_ready, i - 2)
                pool.wait_ge(a_ready, i - 2)
                carry(pool)
                for k in range(2):
                    g.indirect_dma_start(xs_dram, bass.IndirectOffsetOnAxis(ap=slots[q][:, k:k + 1], axis=0),
                                         abuf[q][:, :], None).then_inc(scattered, 16)
                pool.wait_ge(scattered, 32 * (i - 2))
                g.tensor_copy(a_all[:, bass.ds(i - 3, 1), :].rearrange("p o d -> p (o d)"), abuf[q][:, :]).then_inc(a_kept, 1)

            pipeline(pool, dispatch)

            for r in ring:
                pool.wait_ge(y_out[r], 16)
            pool.wait_ge(yslot_ready, 1)
            nr = pool.value_load(rounds[0:1, 0:1], min_val=1, max_val=MAX_TILES // RING)
            for r in ring:
                pool.wait_ge(y_out[r], nr * 16)
            carry(pool)
            for k in range(NB):
                if k >= 2:
                    pool.wait_ge(x2_ready, k - 1)
                for t in range(BLK):
                    for s, y in ((0, y1), (1, y2)):
                        n = 2 * (BLK * k + t) + s
                        g.indirect_dma_start(y[k % 2][:, t, :], None, ys_dram,
                                             bass.IndirectOffsetOnAxis(ap=yslot[:, n:n + 1], axis=0)).then_inc(gathered[k % 2], 16)

        @block.tensor
        def _(pe):
            pe.wait_ge(w_att, 16 * 16)
            pe.wait_ge(pool_const, CONSTS)
            for n, (w, c) in enumerate(((wk, 0), (wk, 1), (wq, 1))):
                mm_ = pe.matmul(psY[:, n:n + 1], w[:, :], cols[:, c:c + 1], start=True, stop=True)
            mm_.then_inc(cb_in_ps, 1)
            pe.wait_ge(cb_ready, 1)

            def step(i, p, n):
                if active(i, 0):
                    pe.wait_ge(s_in[p], 32 * (n + 1))
                    m = pe.transpose(ps_xf[:, 0:P], xin[p][:, :], ident[:, :])
                    m = pe.transpose(ps_xf[:, P:2 * P], fin[p][:, :], ident[:, :])
                if active(i, 2):
                    pe.wait_ge(att_ready, i - 1)
                    m = pe.transpose(ps_att, att[p][:, :], ident[:, :])
                if active(i, 0) or active(i, 2):
                    m.then_inc(x_in_ps, 1)
                if not active(i, 0):
                    pe.wait_ge(y_read, i)
                if active(i, 0):
                    pe.wait_ge(x_read, i + 1)
                    atleast(pe, y_read, i)
                    pe.matmul(ps_ks, wk[:, :], xfT[p][:, P:2 * P], start=True, stop=True)
                    pe.matmul(ps_q, wq[:, :], xfT[p][:, P:2 * P], start=True, stop=True)
                    pe.matmul(ps_v, xfT[p][:, 0:P], wv[:, :], start=True, stop=True)
                    pe.matmul(ps_vs, xfT[p][:, P:2 * P], wv[:, :], start=True, stop=True).then_inc(kqv_in_ps, 1)
                if active(i, 0) or active(i, 2):
                    pe.wait_ge(x_read, i + 1)
                    atleast(pe, z_read, i)
                    if active(i, 0):
                        m = pe.matmul(ps_k, wk[:, :], xfT[p][:, 0:P], start=True, stop=True)
                    if active(i, 2):
                        m = pe.matmul(ps_aT, wo[:, :], attT[p][:, :], start=True, stop=True)
                    m.then_inc(z_in_ps, 1)
                if active(i, 1):
                    pe.wait_ge(shift_ready, i)
                    atleast(pe, x_read, i + 1)
                    pe.transpose(ps_shT, mhl[1 - p][:, :, :].rearrange("p g c -> p (g c)"), identb[:, :]).then_inc(shiftT_in_ps, 1)
                    pe.wait_ge(shiftT_ready, i)
                    for g in range(NG + 1):
                        if g < NG:
                            ps = psB[g % 2]
                            atleast(pe, exp_done, 4 * (i - 1) + (g - 1))
                            rows = slice(32 * g, 32 * g + 32)
                            pe.matmul(ps[:, :], kT[1 - p][rows, :], qexp[1 - p][rows, :, :].rearrange("p j t -> p (j t)"),
                                      start=True, stop=False, skip_group_check=True)
                            for j in range(NJ):
                                m = pe.matmul(ps[:, j * P:(j + 1) * P], pick_shift[rows, j, :], shT[1 - p][rows, :],
                                              start=False, stop=(j == NJ - 1), skip_group_check=True)
                            m.then_inc(scores_in_ps, 1)
                        if g > 0:
                            c = g - 1
                            pe.wait_ge(exp_done, 4 * (i - 1) + g)
                            if c == 0:
                                atleast(pe, att_ready, i - 1)
                            for j in range(NJ):
                                h = NJ * c + j
                                m = pe.matmul(psO[:, h * (DH + 1):(h + 1) * (DH + 1)], pT[c % 2][:, j * P:(j + 1) * P],
                                              v9[1 - p][:, h, :], start=True, stop=True)
                            m.then_inc(pv_done, 1)
                if active(i, 0):
                    pe.wait_ge(v_ready, i + 1)
                if active(i, 2):
                    pe.wait_ge(z_read, i + 1)
                    m = pe.matmul(ps_a, attT[p][:, :], wo[:, :], start=True, stop=True)
                    m = pe.matmul(ps_lg, aT[p][:, :], gate0[:, :], start=True, stop=True)
                if active(i, 3):
                    pe.wait_ge(picks_ready, i - 2)
                    pe.matmul(ps_rank, before[:, :], picked[1 - p][:, :], start=True, stop=True)
                    m = pe.matmul(ps_tot, onesb[:, :], picked[1 - p][:, :], start=True, stop=True)
                if active(i, 0):
                    pe.wait_ge(qk_ready, i + 1)
                    m = pe.matmul(ps_self, prod[:, :], ind[:, :], start=True, stop=True)
                if active(i, 0) or active(i, 2) or active(i, 3):
                    m.then_inc(y_in_ps, 1)
                if active(i, 0):
                    pe.wait_ge(kA_ready, i + 1)
                    for g in range(NG):
                        atleast(pe, reduced, 4 * i + (g - 1))
                        rows = slice(32 * g, 32 * g + 32)
                        for j in range(NJ):
                            m = pe.matmul(psA[g % 2][:, j * P:(j + 1) * P], qexp[p][rows, j, :], kA[p][rows, :],
                                          start=True, stop=True)
                        m.then_inc(a_in_ps, 1)

            pipeline(pe, step)

            pe.wait_ge(table_ready, 1)
            pe.wait_ge(y_read, STEPS)
            pe.transpose(psY[0:2, 0:P], table[:, :], ident[:, :]).then_inc(table_in_ps, 1)
            pe.wait_ge(w_l1, 16 * 11)
            pe.transpose(psZ[:, 0:E1], gate1[:, :], ident[0:E1, 0:E1]).then_inc(gT_in_ps, 1)
            pe.wait_ge(plan_ready, 1)
            nr = pe.value_load(rounds[0:1, 0:1], min_val=1, max_val=MAX_TILES // RING)

            def transpose_tile(j, r, n):
                pe.wait_ge(tile_in[r], 80 * (n + 1))
                pe.transpose(banks[4 + r % 2][:, 0:P], xt[r][:, :], ident[:, :]).then_inc(xT_in_ps, 1)

            def up(j, r, first):
                pe.wait_ge(xT_ready, j + 1)
                for c in range(C0):
                    if not first or r > 0:
                        pe.wait_ge(gelu_done, C0 * (j - 1) + (c + 1))
                    pe.matmul(banks[c][:, 0:P], w1[r][:, :].rearrange("d (f c) -> d c f", c=C0)[:, c, :],
                              xT[r % 2][:, :], start=True, stop=True).then_inc(hid_in_ps, 1)

            def down(j, r):
                for c in range(C0):
                    pe.wait_ge(gelu_done, C0 * j + (c + 1))
                    m = pe.matmul(banks[6 + r % 2][:, 0:P], hT[r % 2][:, c, :], w2[r][:, c, :], start=(c == 0), stop=(c == C0 - 1))
                m.then_inc(t_in_ps, 1)

            def round_of_tiles(n, first):
                transpose_tile(RING * n, 0, n)
                for r in ring:
                    if not first or r >= 2:
                        pe.wait_ge(y_ready, RING * n + (r - 1))
                    up(RING * n + r, r, first)
                    if r + 1 < RING:
                        transpose_tile(RING * n + (r + 1), r + 1, n)
                    if r > 0:
                        down(RING * n + (r - 1), r - 1)
                down(RING * n + (RING - 1), RING - 1)

            round_of_tiles(0, True)
            with pe.Fori(1, nr) as n:
                round_of_tiles(n, False)

            pc, pd = banks[6], banks[7]
            steps = [0]

            def signal(ins):
                steps[0] += 1
                ins.then_inc(c_pe, 1)

            def cond(k, stage):
                base_a, base_d = ACT_COND * k, DVE_COND * k
                if stage == 0:
                    pe.wait_ge(x2_ready, k + 1)
                    for t in range(BLK):
                        m = pe.transpose(pc[:, t * P:(t + 1) * P], x2[:, BLK * k + t, :], ident[:, :])
                    signal(m)
                if stage == 1:
                    pe.wait_ge(c_act, base_a + 1)
                    signal(pe.matmul(pd[0:A1, :], w1c[:, :], x2T[:, :], start=True, stop=True))
                if stage == 2:
                    pe.wait_ge(c_act, base_a + 2)
                    signal(pe.matmul(pc[:, :], vB[:, :], th[:, :], start=True, stop=True))
                if stage == 3:
                    pe.wait_ge(c_dve, base_d + 3)
                    for t in range(BLK):
                        m = pe.transpose(pd[:, t * P:(t + 1) * P], pn[:, t, :], ident[:, :])
                    signal(m)
                if stage == 4:
                    pe.wait_ge(c_act, base_a + 4)
                    for t in range(BLK):
                        m = pe.matmul(pc[:, t * P:(t + 1) * P], x2[:, BLK * k + t, :], pnT[:, t * P:(t + 1) * P], start=True, stop=True)
                    signal(m)
                if stage == 5:
                    pe.wait_ge(c_act, base_a + 5)
                    for t in range(BLK):
                        m = pe.matmul(pd[:, t * E1:(t + 1) * E1], plT[k % 2][:, t * P:(t + 1) * P], gate1T[:, :], start=True, stop=True)
                    signal(m)
                if stage == 6:
                    pe.wait_ge(c_dve, base_d + 5)
                    for t in range(BLK):
                        m = pe.transpose(pc[:, :].bitcast(BF16)[0:3 * E1, t * P:(t + 1) * P], cparts[:, t, :], identb[:, :])
                    signal(m)

            def ffn(k):
                x = plT[k % 2]
                pe.wait_ge(cond_ready, k + 1)
                if k == 0:
                    pe.wait_ge(pool_const, ALL_CONSTS)   
                for c in range(NC1):
                    n = NC1 * k + c
                    f, m = (c * P, P) if c < NE else NSH[c - NE]
                    wg, wu = (wg1, wu1) if c < NE else (wsg, wsu)
                    atleast(pe, h_ready, n - 1)
                    pe.matmul(banks[n % 2][0:m, :], wg[:, f:f + m], x[:, :], start=True, stop=True)
                    pe.matmul(banks[2 + n % 2][0:m, :], wu[:, f:f + m], x[:, :], start=True, stop=True).then_inc(gu_in_ps, 1)
                    if c < NE:
                        atleast(pe, h_ready, n)
                        pe.matmul(banks[4][:, :], expert_of[:, f:f + P], cT[k % 2][:, :], start=True, stop=True).then_inc(wt_in_ps, 1)
                    beside(cond, PE_STAGES, c, k + 1)
                for t in range(BLK):
                    pe.wait_ge(h_ready, NC1 * (k + 1))
                    for c in range(NC1):
                        m = P if c < NE else NSH[c - NE][1]
                        wd = wd1[:, c, :] if c < NE else wsd[0:m, c - NE, :]
                        y = pe.matmul(banks[5][:, t * P:(t + 1) * P], h1[0:m, c, t * P:(t + 1) * P], wd, start=(c == 0), stop=(c == NC1 - 1))
                y.then_inc(out_acc, 1)

            pe.wait_ge(gT_ready, 1)
            pe.wait_ge(y_ready, nr * RING)
            for n in range(len(PE_STAGES)):
                cond(0, n)
            for k in range(NB):
                if k >= 1:
                    pe.wait_ge(ob_ready, k)
                ffn(k)

        @block.scalar
        def _(act):
            s = nc.scalar
            act.wait_ge(cb_ready, 1)

            def step(i, p, n):
                if active(i, 1):
                    act.wait_ge(shift_ready, i)
                    atleast(act, att_ready, i - 2)
                    s.activation(ws[1 - p][:, :], sm[:, :], ACT.Exp).then_inc(ws_ready, 1)
                if active(i, 0) or active(i, 2):
                    act.wait_ge(x_in_ps, i + 1)
                    if active(i, 0):
                        atleast(act, kqv_in_ps, i - 1)
                        atleast(act, z_in_ps, i - 1)
                        m = s.activation(xfT[p][:, :], ps_xf, ACT.Identity)
                    if active(i, 2):
                        atleast(act, y_in_ps, i - 2)
                        m = s.activation(attT[p][:, :], ps_att, ACT.Identity)
                    m.then_inc(x_read, 1)
                    act.wait_ge(z_in_ps, i + 1)
                    if active(i, 2):
                        atleast(act, y_in_ps, i - 2)
                        m = s.activation(aT[p][:, :], ps_aT, ACT.Identity, bias=cols[:, 4:5])
                    if active(i, 0):
                        atleast(act, scores_in_ps, 4 * (i - 1))
                        m = s.activation(kT[p][:, :], ps_k, ACT.Identity, bias=cbias[:, 0:1])
                    m.then_inc(z_read, 1)
                if active(i, 1):
                    act.wait_ge(shiftT_in_ps, i)
                    atleast(act, scores_in_ps, 4 * (i - 2))
                    s.activation(shT[1 - p][:, :], ps_shT, ACT.Identity).then_inc(shiftT_ready, 1)
                for g in range(NG):
                    if active(i, 1):
                        act.wait_ge(scores_in_ps, 4 * (i - 1) + (g + 1))
                        atleast(act, pv_done, 4 * (i - 1) + (g - 1))
                        carry(act)
                        kb = keybias[:, bass.ds(i - 1, 1)]
                        s.activation(pT[g % 2][:, :], psB[g % 2][:, :], ACT.Exp, bias=kb).then_inc(exp_done, 1)
                    if g == 0 and active(i, 0):
                        act.wait_ge(kv_ready, i + 1)
                        act.wait_ge(z_read, i + 1)
                        atleast(act, a_in_ps, 4 * (i - 1))
                        s.activation(kA[p][:, :], kv[:, :], ACT.Identity, bias=kT[p][:, 0:1]).then_inc(kA_ready, 1)

            pipeline(act, step)

            act.wait_ge(chain_l, 6 * B)
            s.activation(eg[:, :], gap[:, :], ACT.Exp).then_inc(gap_exp, 1)
            act.wait_ge(plan_ready, 1)
            nr = act.value_load(rounds[0:1, 0:1], min_val=1, max_val=MAX_TILES // RING)
            ys_t = ys_dram.rearrange("(j p) d -> j p d", p=P)
            act.wait_ge(zeroed, 16 * MAX_TILES)

            def send(j, r):
                act.wait_ge(y_ready, j + 1)
                act.dma_start(ys_t[bass.ds(j, 1)].rearrange("o p d -> (o p) d"), yb[r][:, :]).then_inc(y_out[r], 16)

            def round_of_tiles(n, first):
                for r in ring:
                    j = RING * n + r
                    for c in range(C0):
                        act.wait_ge(hid_in_ps, C0 * j + (c + 1))
                        if c == 0:
                            act.wait_ge(tile_in[r], 80 * (n + 1))
                            if not first or r >= 2:
                                act.wait_ge(t_in_ps, RING * n + (r - 1))
                        s.activation(hT[r % 2][:, c, :], banks[c][:, 0:P], ACT.Gelu,
                                     bias=b1[r][:, c:c + 1]).then_inc(gelu_done, 1)
                    if r > 0:
                        send(RING * n + (r - 1), r - 1)
                send(RING * n + (RING - 1), RING - 1)

            round_of_tiles(0, True)
            with act.Fori(1, nr) as n:
                round_of_tiles(n, False)

            pc, pd = banks[6], banks[7]

            def cond(k, stage):
                bp, bd = 7 * k, DVE_COND * k
                if stage == 0:
                    act.wait_ge(c_pe, bp + 1)
                    s.activation(x2T[:, :], pc[:, :], ACT.Identity).then_inc(c_act, 1)
                if stage == 1:
                    act.wait_ge(c_pe, bp + 2)
                    s.activation(th[:, :], pd[0:A1, :], ACT.Tanh, bias=cols[0:A1, 5:6]).then_inc(c_act, 1)
                if stage == 2:
                    act.wait_ge(c_dve, bd + 2)
                    for t in range(BLK):
                        m = s.activation(pe_[:, t, :], ms[:, t, :], ACT.Exp, bias=nm[:, t:t + 1], accum_out=psum_[:, t:t + 1])
                    m.then_inc(c_act, 1)
                if stage == 3:
                    act.wait_ge(c_pe, bp + 4)
                    s.activation(pnT[:, :], pd[:, :], ACT.Identity).then_inc(c_act, 1)
                if stage == 4:
                    act.wait_ge(c_pe, bp + 5)
                    atleast(act, out_acc, k - 1)
                    s.activation(plT[k % 2][:, :], pc[:, :], ACT.Identity).then_inc(c_act, 1)
                if stage == 5:
                    act.wait_ge(c_dve, bd + 4)
                    s.activation(e8[:, :, :].rearrange("p b e -> p (b e)"), ls8[:, :, :].rearrange("p b e -> p (b e)"), ACT.Exp).then_inc(c_act, 1)

            def ffn(k):
                for c in range(NC1):
                    n = NC1 * k + c
                    m = P if c < NE else NSH[c - NE][1]
                    act.wait_ge(gu_in_ps, n + 1)
                    atleast(act, h_ready, n - 1)
                    s.activation(sg[n % 2][0:m, :], banks[n % 2][0:m, :], ACT.Silu).then_inc(silu_done, 1)
                    beside(cond, ACT_STAGES, c, k + 1)

            for n in range(len(ACT_STAGES)):
                cond(0, n)
            for k in range(NB):
                ffn(k)

        @block.vector
        def _(dve):
            v = nc.vector

            class Chain:

                def __init__(self, s, per):
                    self.s, self.per, self.k, self.base = s, per, 0, 0

                def start(self, b):
                    self.base, self.k = self.per * b, 0

                def add(self, ins):
                    self.k += 1
                    assert self.k <= self.per
                    ins.then_inc(self.s, 1)

                def link(self, ins):
                    self.add(ins)
                    dve.wait_ge(self.s, self.base + self.k)

                def join(self):
                    dve.wait_ge(self.s, self.base + self.k)

            cc = Chain(chain_c, 22)
            cc.start(0)
            dve.wait_ge(w_att, 16 * 16)
            dve.wait_ge(pool_const, CONSTS)
            cc.add(v.tensor_copy(lens[:, :], lens_i[:, :]))
            cc.link(v.tensor_copy(types[:, :], types_i[:, :]))
            cc.add(v.tensor_scalar(nolen[:, :], lens[:, :], 1.0, -BIG, ALU.is_lt, ALU.mult))
            cc.add(v.tensor_scalar(keybias[:, :], lens[:, :], iota_p[:, 0:1], -BIG, ALU.is_le, ALU.mult))
            cc.add(v.tensor_reduce(headmask[:, :], ind[:, :].rearrange("p (g j) -> p j g", g=NG), AX_X, ALU.add))
            cc.add(v.tensor_scalar(is_pre[:, :], types[:, :], 0.0, None, ALU.is_equal))
            cc.link(v.tensor_scalar(is_post[:, :], types[:, :], 1.0, None, ALU.is_equal))
            cc.link(v.tensor_tensor(tmp_b[:, :], is_pre[:, :], is_post[:, :], ALU.add))
            cc.link(v.tensor_scalar(is_cloze[:, :], tmp_b[:, :], -1.0, 1.0, ALU.mult, ALU.add))
            cc.add(v.tensor_scalar(tmp_c[:, 0:1], iota_p[:, 0:1], 1.0, None, ALU.add))
            cc.link(v.tensor_scalar(tmp_c[:, 1:2], iota_p[:, 0:1], -1.0, float(P), ALU.mult, ALU.add))
            cc.link(v.tensor_scalar(count[:, :], is_cloze[:, :], float(P - 1), None, ALU.mult))
            cc.link(v.scalar_tensor_tensor(out=count[:, :], in0=is_pre[:, :], scalar=tmp_c[:, 0:1], in1=count[:, :], op0=ALU.mult, op1=ALU.add))
            cc.link(v.scalar_tensor_tensor(out=count[:, :], in0=is_post[:, :], scalar=tmp_c[:, 1:2], in1=count[:, :], op0=ALU.mult, op1=ALU.add))
            dve.wait_ge(cb_in_ps, 1)
            cc.add(v.tensor_tensor(cbias[:, 0:1], psY[:, 0:1], cols[:, 2:3], ALU.add))
            cc.add(v.tensor_tensor(cbias[:, 1:2], psY[:, 1:2], cols[:, 2:3], ALU.add))
            cc.join()
            v.tensor_tensor(cbias[:, 2:3], psY[:, 2:3], cols[:, 3:4], ALU.add).then_inc(cb_ready, 1)
            dve.wait_ge(cb_ready, 1)

            cq, cn, cm, cl, cr = (Chain(x, y) for x, y in ((chain_q, 2), (chain_n, 4), (chain_m, 4), (chain_l, 6), (chain_r, 5)))

            def step(i, p, n):
                if active(i, 0):
                    cq.start(i)
                    dve.wait_ge(kqv_in_ps, i + 1)
                    cq.link(v.tensor_scalar(qb[:, :], ps_q, cbias[:, 2:3], None, ALU.add))
                    v.scalar_tensor_tensor(out=prod[:, :], in0=ps_ks, scalar=cbias[:, 1:2], in1=qb[:, :], op0=ALU.add, op1=ALU.mult)
                    atleast(dve, scores_in_ps, 4 * (i - 1))
                    for j in range(NJ):
                        ins = v.tensor_scalar(qexp[p][:, j, :], qb[:, :], headmask[:, j:j + 1], None, ALU.mult)
                    ins.then_inc(qk_ready, 1)
                    dve.wait_ge(z_read, i + 1)
                    cq.link(v.tensor_scalar(kd[:, :], kT[p][:, :], kT[p][:, 0:1], None, ALU.subtract))
                    atleast(dve, kA_ready, i)
                    v.scalar_tensor_tensor(out=kv[:, :], in0=iota_k[:, :], scalar=lens[:, bass.ds(i, 1)], in1=kd[:, :],
                                           op0=ALU.is_lt, op1=ALU.mult).then_inc(kv_ready, 1)
                    atleast(dve, pv_done, 4 * (i - 1))
                    v.tensor_tensor(v9[p][:, :, 0:DH], ps_v.rearrange("p (h d) -> p h d", h=H),
                                    bvB[:, :].rearrange("p (h d) -> p h d", h=H), ALU.add)
                    v.tensor_tensor(vs[p][:, :], ps_vs, bvB[:, :], ALU.add).then_inc(v_ready, 1)
                if active(i, 1):
                    b = i - 1
                    cn.start(b)
                    dve.wait_ge(pv_done, 4 * (b + 1))
                    dve.wait_ge(ws_ready, b + 1)
                    o = psO[:, 0:H * (DH + 1)].rearrange("p (h d) -> p h d", h=H)
                    wb = ws[1 - p][:, :].unsqueeze(2).broadcast_to([P, H, DH])
                    cn.link(v.tensor_tensor(den[:, :], o[:, :, DH:DH + 1].rearrange("p h o -> p (h o)"), ws[1 - p][:, :], ALU.add))
                    cn.add(v.reciprocal(rec[:, :], den[:, :]))
                    dve.wait_ge(v_ready, b + 1)
                    hd = lambda t: t[:, :].rearrange("p (h d) -> p h d", h=H)
                    cn.link(v.tensor_tensor(hd(t1), hd(vs[1 - p]), wb, ALU.mult))
                    cn.link(v.tensor_tensor(hd(t2), hd(t1), o[:, :, 0:DH], ALU.add))
                    atleast(dve, x_in_ps, i - 1)
                    v.tensor_tensor(hd(att[1 - p]), hd(t2), rec[:, :].unsqueeze(2).broadcast_to([P, H, DH]), ALU.mult).then_inc(att_ready, 1)
                if active(i, 0) or active(i, 2) or active(i, 3):
                    dve.wait_ge(y_in_ps, i + 1)
                if active(i, 3):
                    cr.start(i - 3)
                    m = v.tensor_tensor(rank[:, :], ps_rank, held[:, :], ALU.add)
                    cr.add(m)
                    m = v.tensor_tensor(held[:, :], ps_tot, held[:, :], ALU.add)
                    cr.add(m)
                if active(i, 2):
                    cl.start(i - 2)
                    m = v.tensor_tensor(lg[:, :], ps_lg, gate0bB[:, :], ALU.add)
                    cl.add(m)
                    atleast(dve, a_kept, i - 3)
                    m = v.tensor_tensor(abuf[p][:, :], ps_a, boB[:, :], ALU.add)
                    m.then_inc(a_ready, 1)
                if active(i, 0):
                    cm.start(i)
                    v.tensor_copy(selfs[:, :], ps_self).then_inc(y_read, 1)
                elif active(i, 3):
                    v.tensor_copy(y_token[:, :], ps_rank[:, 0:1]).then_inc(y_read, 1)
                if active(i, 0):
                    for g in range(NG):
                        dve.wait_ge(a_in_ps, 4 * i + (g + 1))
                        v.tensor_reduce(mx[:, NJ * g:NJ * g + NJ], psA[g % 2][:, :].rearrange("p (j k) -> p j k", j=NJ), AX_X,
                                        ALU.max).then_inc(reduced, 1)
                    dve.wait_ge(reduced, 4 * (i + 1))
                    dve.wait_ge(y_read, i + 1)
                    cm.link(v.scalar_tensor_tensor(out=mm[:, :], in0=mx[:, :], scalar=nolen[:, bass.ds(i, 1)], in1=selfs[:, :],
                                                   op0=ALU.add, op1=ALU.max))
                    atleast(dve, shiftT_in_ps, i - 1)
                    hi, lo = mhl[p][:, :, 0:NJ], mhl[p][:, :, NJ:2 * NJ]
                    gj = lambda t: t[:, :].rearrange("p (g j) -> p g j", g=NG)
                    cm.link(v.tensor_scalar(hi, gj(mm), -1.0, None, ALU.mult))
                    cm.link(v.scalar_tensor_tensor(out=lo, in0=gj(mm), scalar=-1.0, in1=hi, op0=ALU.mult, op1=ALU.subtract))
                    cm.link(v.tensor_tensor(gj(sm0), gj(selfs), hi, ALU.add))
                    atleast(dve, ws_ready, i)
                    v.tensor_tensor(gj(sm), gj(sm0), lo, ALU.add).then_inc(shift_ready, 1)
                if active(i, 3):
                    b = i - 3
                    cr.join()
                    cr.link(v.tensor_tensor(rank[:, :], rank[:, :], region_of[:, :], ALU.add))
                    cr.link(v.tensor_tensor(rsel[:, :, :], onehot[:, bass.ds(b, 1), :, :].rearrange("p o k e -> p (o k) e"),
                                            rank[:, :].unsqueeze(1).broadcast_to([P, 2, E0]), ALU.mult))
                    sl = slotf[:, bass.ds(b, 1), :].rearrange("p o k -> p (o k)")
                    cr.link(v.tensor_reduce(sl, rsel[:, :, :], AX_X, ALU.add))
                    atleast(dve, a_kept, i - 4)
                    carry(dve)
                    v.tensor_copy(slots[1 - p][:, :], sl).then_inc(slots_ready, 1)
                if active(i, 2):
                    b = i - 2
                    cl.join()
                    carry(dve)
                    cl.link(v.max(top8[:, :], lg[:, :]))
                    carry(dve)
                    cl.link(v.max_index(topi[:, :], top8[:, :], lg[:, :]))
                    cl.link(v.tensor_copy(topf[:, :], topi[:, 0:2]))
                    cl.add(v.tensor_tensor(gap[:, bass.ds(b, 1)], top8[:, 1:2], top8[:, 0:1], ALU.subtract))
                    oh = onehot[:, bass.ds(b, 1), :, :].rearrange("p o k e -> p (o k) e")
                    cl.link(v.tensor_tensor(oh, iota_e[:, :].unsqueeze(1).broadcast_to([P, 2, E0]),
                                            topf[:, :].unsqueeze(2).broadcast_to([P, 2, E0]), ALU.is_equal))
                    atleast(dve, y_in_ps, i - 1)
                    v.tensor_tensor(picked[p][:, :], onehot[:, bass.ds(b, 1), 0, :].rearrange("p o e -> p (o e)"),
                                    onehot[:, bass.ds(b, 1), 1, :].rearrange("p o e -> p (o e)"), ALU.add).then_inc(picks_ready, 1)

            pipeline(dve, step)

            ct = Chain(chain_t, 40)
            ct.start(0)
            cr.start(B - 1)
            cr.k = 5
            cr.join()
            ct.link(v.tensor_scalar(nti[:, :], held[:, :], float(P - 1), None, ALU.add))
            ct.link(v.tensor_scalar(nti[:, :], nti[:, :], 7, None, ALU.arith_shift_right))
            ct.link(v.tensor_copy(ntf[:, :], nti[:, :]))
            ct.link(v.tensor_tensor_scan(incl[:, :], ones_e[:, :], ntf[:, :], 0.0, ALU.mult, ALU.add))
            ct.add(v.tensor_tensor(excl[:, :], incl[:, :], ntf[:, :], ALU.subtract))
            ct.link(v.tensor_scalar(below[:, :], incl[:, :], iota_p[:, 0:1], None, ALU.is_le))
            ct.add(v.tensor_reduce(ej[:, :], below[:, :], AX_X, ALU.add))
            ct.link(v.tensor_tensor(under[:, :], below[:, :], incl[:, :], ALU.mult))
            ct.link(v.tensor_reduce(tj[:, :], under[:, :], AX_X, ALU.max))
            ct.link(v.tensor_tensor(tj[:, :], iota_p[:, :], tj[:, :], ALU.subtract))
            ct.link(v.tensor_scalar(tj[:, :], tj[:, :], float(P), None, ALU.mult))
            ct.link(v.scalar_tensor_tensor(out=tj[:, :], in0=ej[:, :], scalar=float(REGION), in1=tj[:, :], op0=ALU.mult, op1=ALU.add))
            ct.add(v.tensor_scalar(table[:, 1:2], tj[:, :], float(XROWS - P), None, ALU.min))
            ct.add(v.tensor_scalar(table[:, 0:1], ej[:, :], float(E0 - 1), None, ALU.min))
            ct.add(v.tensor_scalar(rounds_i[:, :], incl[:, E0 - 1:E0], float(RING - 1), None, ALU.add))
            ct.add(v.tensor_tensor(pad_row[:, 0:E0], held[:, :], region_of[:, :], ALU.add))
            for r in ring:
                ct.add(v.memset(pad_row[:, E0 + r:E0 + r + 1], float(E0 * REGION + r * P)))
            ct.join()
            v.engine_nop().then_inc(table_ready, 1)
            ct.add(v.tensor_scalar(rounds[:, :], rounds_i[:, :], 2, None, ALU.arith_shift_right))
            ct.add(v.tensor_copy(pad_row_i[:, :], pad_row[:, :]))
            dve.wait_ge(table_in_ps, 1)
            ct.link(v.tensor_copy(table_i[:, :], psY[0:2, 0:P]))
            v.engine_nop().then_inc(plan_ready, 1)
            dve.wait_ge(gap_exp, 1)
            ct.link(v.tensor_scalar(g1[:, :], eg[:, :], 1.0, None, ALU.add))
            ct.link(v.reciprocal(g1[:, :], g1[:, :]))
            ct.link(v.tensor_tensor(g2[:, :], g1[:, :], eg[:, :], ALU.mult))
            ct.link(v.scalar_tensor_tensor(out=ybase[:, :], in0=excl[:, :], scalar=float(P), in1=region_of[:, :], op0=ALU.mult, op1=ALU.subtract))
            ct.link(v.tensor_tensor(ysel[:, :, :, :].rearrange("p b k e -> p (b k) e"), onehot[:, :, :, :].rearrange("p b k e -> p (b k) e"),
                                    ybase[:, :].unsqueeze(1).broadcast_to([P, 2 * B, E0]), ALU.mult))
            ct.link(v.tensor_reduce(yoff[:, :, :].rearrange("p b k -> p (b k)"), ysel[:, :, :, :].rearrange("p b k e -> p (b k) e"), AX_X, ALU.add))
            ct.link(v.tensor_tensor(yslotf[:, :, :], slotf[:, :, :], yoff[:, :, :], ALU.add))
            ct.link(v.tensor_copy(yslot[:, :], yslotf[:, :, :].rearrange("p b k -> p (b k)")))
            v.engine_nop().then_inc(yslot_ready, 1)
            dve.wait_ge(gT_in_ps, 1)
            ct.add(v.tensor_copy(gate1T[:, :], psZ[:, 0:E1]))
            ct.link(v.tensor_scalar(vB[:, :], onesb[0:A1, :], vcol[:, 0:1], None, ALU.mult))
            v.engine_nop().then_inc(gT_ready, 1)

            nr = dve.value_load(rounds[0:1, 0:1], min_val=1, max_val=MAX_TILES // RING)

            def take_xT(j, r, first):
                dve.wait_ge(xT_in_ps, j + 1)
                if not first or r >= 2:
                    dve.wait_ge(hid_in_ps, C0 * (j - 1))
                v.tensor_copy(xT[r % 2][:, :], banks[4 + r % 2][:, 0:P]).then_inc(xT_ready, 1)

            def take_y(j, r, n, first):
                dve.wait_ge(t_in_ps, j + 1)
                if not first:
                    dve.wait_ge(y_out[r], 16 * n)
                v.tensor_tensor(yb[r][:, :], banks[6 + r % 2][:, 0:P], b2[r][:, :], ALU.add).then_inc(y_ready, 1)

            def round_of_tiles(n, first):
                take_xT(RING * n, 0, first)
                for r in ring:
                    if r + 1 < RING:
                        take_xT(RING * n + (r + 1), r + 1, first)
                    if r > 0:
                        take_y(RING * n + (r - 1), r - 1, n, first)
                take_y(RING * n + (RING - 1), RING - 1, n, first)

            round_of_tiles(0, True)
            with dve.Fori(1, nr) as n:
                round_of_tiles(n, False)

            pc, pd = banks[6], banks[7]
            cx = Chain(chain_x, 1000)

            def cond(k, stage):
                bp, ba = 7 * k, ACT_COND * k
                blk = slice(BLK * k, BLK * (k + 1))
                if stage == 0:
                    dve.wait_ge(gathered[k % 2], 16 * 2 * BLK * (k // 2 + 1))
                    dve.wait_ge(xr_in[k % 2], 16 * (k // 2 + 1))
                    for t in range(BLK):
                        b = BLK * k + t
                        cx.add(v.scalar_tensor_tensor(out=mix1[:, t, :], in0=y1[k % 2][:, t, :], scalar=g1[:, b:b + 1], in1=xr[k % 2][:, t, :],
                                                      op0=ALU.mult, op1=ALU.add))
                    cx.join()
                    for t in range(BLK):
                        b = BLK * k + t
                        cx.add(v.scalar_tensor_tensor(out=mix2[:, t, :], in0=y2[k % 2][:, t, :], scalar=g2[:, b:b + 1], in1=mix1[:, t, :],
                                                      op0=ALU.mult, op1=ALU.add))
                    cx.join()
                    if k == 0:
                        dve.wait_ge(a_kept, B)
                    v.tensor_tensor(x2[:, blk, :], mix2[:, :, :], a_all[:, blk, :], ALU.add).then_inc(x2_ready, 1)
                    v.engine_nop().then_inc(c_dve, 1)
                if stage == 1:
                    dve.wait_ge(c_pe, bp + 3)
                    if k == 0:
                        dve.wait_ge(pool_const, ALL_CONSTS)
                    cx.link(v.tensor_tensor(ms[:, :, :], pc[:, :].rearrange("p (b l) -> p b l", b=BLK), poolbias[:, blk, :], ALU.add))
                    v.tensor_reduce(nm[:, :], ms[:, :, :], AX_X, ALU.max, negate=True).then_inc(c_dve, 1)
                if stage == 2:
                    dve.wait_ge(c_act, ba + 3)
                    cx.link(v.tensor_tensor(sc_[:, :], psum_[:, :], count[:, blk], ALU.mult))
                    cx.link(v.reciprocal(rs_[:, :], sc_[:, :]))
                    v.tensor_tensor(pn[:, :, :], pe_[:, :, :], rs_[:, :].unsqueeze(2).broadcast_to([P, BLK, P]), ALU.mult).then_inc(c_dve, 1)
                if stage == 3:
                    dve.wait_ge(c_pe, bp + 6)
                    cx.link(v.tensor_copy(l8[:, :, :].rearrange("p b e -> p (b e)"), pd[:, 0:BLK * E1]))
                    cx.link(v.tensor_reduce(nl8[:, :], l8[:, :, :], AX_X, ALU.max))
                    v.tensor_tensor(ls8[:, :, :], l8[:, :, :], nl8[:, :].unsqueeze(2).broadcast_to([P, BLK, E1]), ALU.subtract).then_inc(c_dve, 1)
                if stage == 4:
                    dve.wait_ge(c_act, ba + 6)
                    cx.link(v.tensor_reduce(z8[:, :], e8[:, :, :], AX_X, ALU.add))
                    cx.link(v.reciprocal(rz8[:, :], z8[:, :]))
                    cx.link(v.tensor_tensor(pr8[:, :, :], e8[:, :, :], rz8[:, :].unsqueeze(2).broadcast_to([P, BLK, E1]), ALU.mult))
                    for t in range(BLK):
                        cx.add(v.max(top1[:, t, :], pr8[:, t, :]))
                    cx.join()
                    for t in range(BLK):
                        cx.add(v.max_index(topi1[:, t, :], top1[:, t, :], pr8[:, t, :]))
                    cx.join()
                    cx.link(v.tensor_copy(topf1[:, :, :], topi1[:, :, 0:2]))
                    for s in range(2):
                        cx.add(v.tensor_tensor(oh1[:, :, s, :], iota_e[:, 0:E1].unsqueeze(1).broadcast_to([P, BLK, E1]),
                                               topf1[:, :, s:s + 1].broadcast_to([P, BLK, E1]), ALU.is_equal))
                    cx.add(v.tensor_tensor(s8[:, :], top1[:, :, 0:1].rearrange("p b o -> p (b o)"), top1[:, :, 1:2].rearrange("p b o -> p (b o)"), ALU.add))
                    cx.join()
                    cx.add(v.tensor_tensor(pick1[:, :, :], oh1[:, :, 0, :], oh1[:, :, 1, :], ALU.add))
                    cx.link(v.tensor_scalar(s8[:, :], s8[:, :], 1e-20, None, ALU.add))
                    cx.add(v.tensor_tensor(c8a[:, :, :], pick1[:, :, :], pr8[:, :, :], ALU.mult))
                    cx.link(v.reciprocal(r8[:, :], s8[:, :]))
                    cx.link(v.tensor_scalar(r8[:, :], r8[:, :], ROUTE_SCALE, None, ALU.mult))
                    cx.link(v.tensor_tensor(c8[:, :, :], c8a[:, :, :], r8[:, :].unsqueeze(2).broadcast_to([P, BLK, E1]), ALU.mult))
                    parts = [cparts[:, :, E1 * n:E1 * (n + 1)] for n in range(3)]
                    cx.link(v.tensor_copy(parts[0], c8[:, :, :]))
                    cx.link(v.tensor_tensor(c8r[:, :, :], c8[:, :, :], parts[0], ALU.subtract))
                    cx.link(v.tensor_copy(parts[1], c8r[:, :, :]))
                    cx.link(v.tensor_tensor(c8s[:, :, :], c8r[:, :, :], parts[1], ALU.subtract))
                    v.tensor_copy(parts[2], c8s[:, :, :]).then_inc(c_dve, 1)
                if stage == 5:
                    dve.wait_ge(c_pe, bp + 7)
                    atleast(dve, out_acc, k - 1)
                    v.tensor_copy(cT[k % 2][:, :], pc[:, :].bitcast(BF16)[0:3 * E1, 0:W]).then_inc(cond_ready, 1)

            def ffn(k):
                for c in range(NC1):
                    n = NC1 * k + c
                    m = P if c < NE else NSH[c - NE][1]
                    dve.wait_ge(silu_done, n + 1)
                    dve.wait_ge(gu_in_ps, n + 1)
                    atleast(dve, out_acc, k)
                    if c < NE:
                        atleast(dve, h_ready, n)
                        cf[0] += 1
                        v.tensor_tensor(hu[:, :], sg[n % 2][:, :], banks[2 + n % 2][:, :], ALU.mult).then_inc(chain_h, 1)
                        dve.wait_ge(chain_h, cf[0])
                        dve.wait_ge(wt_in_ps, NE * k + c + 1)
                        v.tensor_tensor(h1[:, c, :], hu[:, :], banks[4][:, :], ALU.mult).then_inc(h_ready, 1)
                    else:
                        v.tensor_tensor(h1[0:m, c, :], sg[n % 2][0:m, :], banks[2 + n % 2][0:m, :], ALU.mult).then_inc(h_ready, 1)
                    beside(cond, DVE_STAGES, c, k + 1)
                dve.wait_ge(out_acc, k + 1)
                if k >= 2:
                    dve.wait_ge(ob_out[k % 2], 16 * (k // 2))
                v.tensor_tensor(ob[k % 2][:, :, :], banks[5][:, :].rearrange("p (b d) -> p b d", b=BLK), x2[:, BLK * k:BLK * (k + 1), :],
                                ALU.add).then_inc(ob_ready, 1)

            cf = [0]
            for n in range(len(DVE_STAGES)):
                cond(0, n)
            for k in range(NB):
                ffn(k)


_INS = ['x', 'fside_BxSxS_0', 'itok_B_18_1004', 'itok_B_0_2', 'L0_cond_Wq', 'L0_cond_bq', 'L0_cond_Wk', 'L0_cond_bk', 'L0_cond_Wv',
        'L0_cond_bv', 'L0_cond_Wo', 'L0_cond_bo', 'L0_cond_b_prev', 'L0_cond_b_self', 'L0_ffn_gate_w', 'L0_ffn_gate_b', 'L0_ffn_w1',
        'L0_ffn_b1', 'L0_ffn_w2', 'L0_ffn_b2', 'L1_cond_W1', 'L1_cond_b1', 'L1_cond_v', 'L1_ffn_gate_w', 'L1_ffn_w_gate', 'L1_ffn_w_up',
        'L1_ffn_w_down', 'L1_ffn_sw_gate', 'L1_ffn_sw_up', 'L1_ffn_sw_down']


def kernel(**inputs):
    import numpy as _np
    import concourse.bacc as _bacc
    from concourse import mybir as _mybir
    from concourse.bass_utils import run_bass_kernel_spmd as _run

    nc = _bacc.Bacc("TRN2", target_bir_lowering=False, num_devices=1)
    arrays, aps = {}, {}
    for name in _INS:
        v = _np.ascontiguousarray(inputs[name])
        arrays[f"in_{name}_dram"] = v
        aps[name] = nc.dram_tensor(f"in_{name}_dram", v.shape, _mybir.dt.from_np(v.dtype), kind="ExternalInput").ap()
    out = nc.dram_tensor("out_0_dram", (B, P, P), F32, kind="ExternalOutput").ap()
    xs = nc.dram_tensor("dispatched_tokens", (XROWS, P), F32, kind="Internal").ap()
    ys = nc.dram_tensor("expert_outputs", (YROWS, P), F32, kind="Internal").ap()
    attention_moe_kernel(nc, aps, out, xs, ys)
    r = _run(nc, [arrays], core_ids=[0])
    return r.results[0]["out_0_dram"]
```

```python
from contextlib import ExitStack

import concourse.bass as bass
from concourse import mybir

ALU = mybir.AluOpType
ACT = mybir.ActivationFunctionType
AX_X = mybir.AxisListType.X
F32 = mybir.dt.float32
BF16 = mybir.dt.bfloat16
I32 = mybir.dt.int32
U32 = mybir.dt.uint32

P = 128
B = 16
H = 16
DH = P // H
NG, NJ = 4, 4
SCALE = float(DH) ** -0.5
BIG = 1.0e30

E0, F0 = 24, 512
C0 = F0 // P
RUNS = B + 1
REGION = RUNS * P
RING = 4
PAD_TILES = RING - 1
ZERO_TILES = 12
MIN_TILES = B * P * 2 // P
MAX_TILES = B * P * 2 // P + E0 + PAD_TILES + 1
YROWS = MAX_TILES * P

E1, F1 = 8, 176
FS = 2 * F1
FE = E1 * F1
NE = FE // P
NSH = [(0, 128), (128, 128), (256, 96)]
NC1 = NE + len(NSH)
A1 = 32
ROUTE_SCALE = 2.5
BLK = 4
NB = B // BLK
W = BLK * P


def attention_moe_kernel(nc, a, out, at_dram, ids_dram, ys_dram):
    ctx = ExitStack()
    with ctx:
        def sb(name, shape, dt=F32):
            return ctx.enter_context(nc.sbuf_tensor(name, shape, dt))

        def bank(name):
            return ctx.enter_context(nc.psum_tensor(name, [P, 512], F32))

        def sem(name):
            return ctx.enter_context(nc.semaphore(name))

        banks = [bank(f"bank{i}") for i in range(8)]

        ident = sb("ident", [P, P])
        identb = sb("identb", [P, P], BF16)
        before = sb("before", [P, P], BF16)
        onesb = sb("onesb", [P, P], BF16)
        pick_shift = sb("pick_shift", [P, H, P], BF16)
        ind = sb("ind", [P, H])
        headmask = sb("headmask", [P, NJ])
        iota_e = sb("iota_e", [P, E0])
        iota_p = sb("iota_p", [P, 1])
        iota_k = sb("iota_k", [P, P])
        region_of = sb("region_of", [P, E0])
        lens_i = sb("lens_i", [P, B], I32)
        lens = sb("lens", [P, B])
        nolen = sb("nolen", [P, B])
        keybias = sb("keybias", [P, B])
        types_i = sb("types_i", [P, B], I32)
        types = sb("types", [P, B])
        is_pre = sb("is_pre", [P, B])
        is_post = sb("is_post", [P, B])
        is_cloze = sb("is_cloze", [P, B])
        count = sb("count", [P, B])
        tmp_b = sb("tmp_b", [P, B])
        tmp_c = sb("tmp_c", [P, B])
        prebias = sb("prebias", [P, P])
        postbias = sb("postbias", [P, P])
        clozebias = sb("clozebias", [P, P])
        poolbias = sb("poolbias", [P, B, P])
        h1 = sb("h1", [P, NC1, W])
        h1_flat = h1[:, :, :].rearrange("p c w -> p (c w)")
        term = h1_flat[:, 0:B * P].rearrange("p (b l) -> p b l", b=B)
        b2_all = h1_flat[:, B * P:(B + E0) * P].rearrange("p (e d) -> p e d", e=E0)
        b1_all = h1_flat[:, (B + E0) * P:(B + E0) * P + E0 * C0].rearrange("p (e c) -> p e c", e=E0)
        zrow = sb("zrow", [P, P])
        ones_e = sb("ones_e", [P, E0])
        expert_of = sb("expert_of", [3 * E1, FE], BF16)

        wq, wk, wv, wo = (sb(n, [P, P]) for n in ("wq", "wk", "wv", "wo"))
        cols = sb("cols", [P, 6])
        bvB, boB = sb("bvB", [P, P]), sb("boB", [P, P])
        gate0 = sb("gate0", [P, E0])
        gate0bB = sb("gate0bB", [P, E0])
        cbias = sb("cbias", [P, 3])
        w1c = sb("w1c", [P, A1])
        vcol = sb("vcol", [A1, 1])
        vB = sb("vB", [A1, P])
        gate1 = sb("gate1", [E1, P])
        gate1T = sb("gate1T", [P, E1])
        wg1 = sb("wg1", [P, FE])
        wu1 = sb("wu1", [P, FE])
        wd1 = sb("wd1", [P, NE, P])
        wsg = sb("wsg", [P, FS])
        wsu = sb("wsu", [P, FS])
        wsd = sb("wsd", [P, len(NSH), P])

        xin = [sb(f"xin{i}", [P, P]) for i in range(2)]
        fin = [sb(f"fin{i}", [P, P]) for i in range(2)]
        xfT = [sb(f"xfT{i}", [P, 2 * P]) for i in range(2)]
        kT = [sb(f"kT{i}", [P, P]) for i in range(2)]
        kA = [sb(f"kA{i}", [P, P]) for i in range(2)]
        kd, kv, qb, prod = (sb(n, [P, P]) for n in ("kd", "kv", "qb", "prod"))
        qexp = [sb(f"qexp{i}", [P, H, P]) for i in range(2)]
        v9 = [sb(f"v9{i}", [P, H, DH + 1]) for i in range(2)]
        vs = [sb(f"vs{i}", [P, P]) for i in range(2)]
        mx = sb("mx", [P, H])
        mm = sb("mm", [P, H])
        mhl = [sb(f"mhl{i}", [P, NG, 32], BF16) for i in range(2)]
        shT = [sb(f"shT{i}", [P, P], BF16) for i in range(2)]
        sm0 = sb("sm0", [P, H])
        sm = sb("sm", [P, H])
        selfs = sb("selfs", [P, H])
        y_token = sb("y_token", [P, 1])
        ws = [sb(f"ws{i}", [P, H]) for i in range(2)]
        pT = [sb(f"pT{i}", [P, NJ * P]) for i in range(2)]
        den, rec = sb("den", [P, H]), sb("rec", [P, H])
        t1, t2 = sb("t1", [P, P]), sb("t2", [P, P])
        att = [sb(f"att{i}", [P, P]) for i in range(2)]
        attT = [sb(f"attT{i}", [P, P]) for i in range(2)]
        aT = [sb(f"aT{i}", [P, P]) for i in range(2)]
        a_all = sb("a_all", [P, B, P])

        lg = sb("lg", [P, E0])
        top8 = sb("top8", [P, 8])
        topi = sb("topi", [P, 8], U32)
        topf = sb("topf", [P, 2])
        picked = [sb(f"picked{i}", [P, E0], BF16) for i in range(2)]
        onehot = sb("onehot", [P, B, 2, E0])
        gap = sb("gap", [P, B])
        held = sb("held", [P, E0])
        rank = sb("rank", [P, E0])
        rsel = sb("rsel", [P, 2, E0])
        slotf = sb("slotf", [P, B, 2])
        slots = [sb(f"slots{i}", [P, 2], U32) for i in range(2)]
        gelu_warm = sb("gelu_warm", [P, 1])
        g1, g2, eg = sb("g1", [P, B]), sb("g2", [P, B]), sb("eg", [P, B])
        ntf = sb("ntf", [P, E0])
        nti = sb("nti", [P, E0], I32)
        incl, excl = sb("incl", [P, E0]), sb("excl", [P, E0])
        below, under = sb("below", [P, E0]), sb("under", [P, E0])
        ej, tj = sb("ej", [P, 1]), sb("tj", [P, 1])
        table = sb("table", [P, 2])
        table_i = sb("table_i", [1, P], I32)
        rounds_f = sb("rounds_f", [P, 1])
        rounds_i = sb("rounds_i", [P, 1], I32)
        rounds = sb("rounds", [P, 1], I32)
        tile_list = sb("tile_list", [P, 1], U32)
        tile_ids = sb("tile_ids", [P, P])
        tile_rows = sb("tile_rows", [P, P], U32)
        tok = [sb(f"tok{i}", [P, 1]) for i in range(2)]
        row_r = [sb(f"row_r{r}", [P, 1], U32) for r in range(RING)]
        ybase = sb("ybase", [P, E0])
        ysel = sb("ysel", [P, B, 2, E0])
        yoff = sb("yoff", [P, B, 2])
        yslotf = sb("yslotf", [P, B, 2])
        yslot = sb("yslot", [P, B * 2], U32)

        ring = range(RING)
        xt = [sb(f"xt{r}", [P, P]) for r in ring]
        w1 = [sb(f"w1_{r}", [P, F0]) for r in ring]
        w2 = [sb(f"w2_{r}", [P, C0, P]) for r in ring]
        b1 = [sb(f"b1_{r}", [P, C0]) for r in ring]
        b2 = [sb(f"b2_{r}", [P, P]) for r in ring]
        xT = [sb(f"xT{i}", [P, P]) for i in range(2)]
        hT = [sb(f"hT{i}", [P, C0, P]) for i in range(2)]
        yb = [sb(f"yb{r}", [P, P]) for r in ring]

        y1 = [qexp[0][:, BLK * i:BLK * (i + 1), :] for i in range(2)]
        y2 = [qexp[0][:, BLK * (2 + i):BLK * (3 + i), :] for i in range(2)]
        mix1, mix2, ms, pe_ = (qexp[1][:, BLK * i:BLK * (i + 1), :] for i in range(4))
        xr = [sb(f"xr{i}", [P, BLK, P]) for i in range(2)]
        mix1p, mix2p = (t[:, :].rearrange("p (b d) -> p b d", b=BLK) for t in w1[0:2])
        x2 = sb("x2", [P, B, P])
        x2T = sb("x2T", [P, W])
        th = sb("th", [A1, W])
        nm = sb("nm", [P, BLK])
        psum_ = sb("psum_", [P, BLK])
        sc_, rs_ = sb("sc_", [P, BLK]), sb("rs_", [P, BLK])
        pn = sb("pn", [P, BLK, P])
        pnT = sb("pnT", [P, W])
        plT = [sb(f"plT{i}", [P, W]) for i in range(2)]
        l8 = sb("l8", [P, BLK, E1])
        nl8 = sb("nl8", [P, BLK])
        ls8, e8, pr8 = (sb(n, [P, BLK, E1]) for n in ("ls8", "e8", "pr8"))
        z8, rz8 = sb("z8", [P, BLK]), sb("rz8", [P, BLK])
        top1 = sb("top1", [P, BLK, 8])
        topi1 = sb("topi1", [P, BLK, 8], U32)
        topf1 = sb("topf1", [P, BLK, 2])
        oh1 = sb("oh1", [P, BLK, 2, E1])
        pick1, c8a, c8 = (sb(n, [P, BLK, E1]) for n in ("pick1", "c8a", "c8"))
        s8, r8 = sb("s8", [P, BLK]), sb("r8", [P, BLK])
        c8r, c8s = sb("c8r", [P, BLK, E1]), sb("c8s", [P, BLK, E1])
        cparts = sb("cparts", [P, BLK, 3 * E1], BF16)
        cT = [sb(f"cT{i}", [3 * E1, W], BF16) for i in range(2)]
        sg = [sb(f"sg{i}", [P, W]) for i in range(2)]
        hu = sb("hu", [P, W])
        ob = [sb(f"ob{i}", [P, BLK, P]) for i in range(2)]

        w_att = sem("w_att")
        w_rest = sem("w_rest")
        w_l1 = sem("w_l1")
        pool_const = sem("pool_const")
        dve_const = sem("dve_const")
        cb_in_ps = sem("cb_in_ps")
        cb_ready = sem("cb_ready")
        gT_in_ps = sem("gT_in_ps")
        gT_ready = sem("gT_ready")
        s_in = [sem(f"s_in{i}") for i in range(2)]
        t_in_ps = sem("t_in_ps")
        a_in_ps = sem("a_in_ps")
        y_read = sem("y_read")
        z_read = sem("z_read")
        z_in_ps = sem("z_in_ps")
        x_read = sem("x_read")
        x_in_ps = sem("x_in_ps")
        xfT_ready = sem("xfT_ready")
        kqv_in_ps = sem("kqv_in_ps")
        kT_ready = sem("kT_ready")
        kv_ready = sem("kv_ready")
        kA_ready = sem("kA_ready")
        prod_ready = sem("prod_ready")
        qexp_dve = sem("qexp_dve")
        qexp_pool = sem("qexp_pool")
        self_in_ps = sem("self_in_ps")
        self_read = sem("self_read")
        v_ready = sem("v_ready")
        reduced = sem("reduced")
        shift_ready = sem("shift_ready")
        shiftT_in_ps = sem("shiftT_in_ps")
        shiftT_ready = sem("shiftT_ready")
        ws_ready = sem("ws_ready")
        scores_in_ps = sem("scores_in_ps")
        exp_done = sem("exp_done")
        pv_done = sem("pv_done")
        att_ready = sem("att_ready")
        att_in_ps = sem("att_in_ps")
        attT_ready = sem("attT_ready")
        aT_in_ps = sem("aT_in_ps")
        aT_ready = sem("aT_ready")
        a_ready = sem("a_ready")
        a_stored = sem("a_stored")
        tok_next = sem("tok_next")
        listed = sem("listed")
        logits_in_ps = sem("logits_in_ps")
        picks_ready = sem("picks_ready")
        rank_in_ps = sem("rank_in_ps")
        slots_ready = sem("slots_ready")
        scattered = sem("scattered")
        zeroed = sem("zeroed")
        rows_in = sem("rows_in")
        rows_in_ps = sem("rows_in_ps")
        rows_ready = sem("rows_ready")
        copied = sem("copied")
        xt_in = [sem(f"xt_in{r}") for r in range(RING)]
        chain_q = sem("chain_q")
        chain_n = sem("chain_n")
        chain_m = sem("chain_m")
        chain_l = sem("chain_l")
        chain_r = sem("chain_r")
        chain_t = sem("chain_t")
        chain_c = sem("chain_c")
        carried = sem("carried")
        chain_x = sem("chain_x")
        chain_h = sem("chain_h")
        table_ready = sem("table_ready")
        table_in_ps = sem("table_in_ps")
        plan_ready = sem("plan_ready")
        gap_exp = sem("gap_exp")
        yslot_ready = sem("yslot_ready")
        biases_in = sem("biases_in")
        b1_ready = sem("b1_ready")
        b2_ready = sem("b2_ready")
        tile_in = [sem(f"tile_in{r}") for r in ring]
        xT_in_ps = sem("xT_in_ps")
        xT_ready = sem("xT_ready")
        hid_in_ps = sem("hid_in_ps")
        gelu_done = sem("gelu_done")
        y_in_ps = sem("y_in_ps")
        y_ready = sem("y_ready")
        y_out = [sem(f"y_out{r}") for r in ring]
        gathered = [sem(f"gathered{i}") for i in range(2)]
        xr_in = [sem(f"xr_in{i}") for i in range(2)]
        x2_ready = sem("x2_ready")
        x2_first = sem("x2_first")
        mix_step = sem("mix_step")
        c_pe = sem("c_pe")
        c_act = sem("c_act")
        c_dve = sem("c_dve")
        cond_ready = sem("cond_ready")
        gu_in_ps = sem("gu_in_ps")
        wt_in_ps = sem("wt_in_ps")
        silu_done = sem("silu_done")
        h_ready = sem("h_ready")
        out_acc = sem("out_acc")
        ob_ready = sem("ob_ready")
        ob_out = [sem(f"ob_out{i}") for i in range(2)]

        psB = banks[0:2]
        psA = banks[2:4]
        psY, psZ, psX, psO = banks[4:8]
        ps_ks, ps_q, ps_v, ps_vs = (psY[:, i * P:(i + 1) * P] for i in range(4))
        ps_a, ps_rank, ps_tot = psY[:, 0:128], psY[:, 128:152], psY[:, 152:176]
        ps_lg = psY[:, 176:200]
        ps_self = psO[:, H * (DH + 1):H * (DH + 2)]
        ps_k, ps_aT = psZ[:, 0:P], psZ[:, P:2 * P]
        ps_xf, ps_att = psX[:, 0:256], psX[:, 256:384]
        ps_shT = psX[:, 384:448].bitcast(BF16)

        FIRST_CONSTS = 8
        CONSTS = 23
        ALL_CONSTS = CONSTS + 15
        CHAIN_TYPES = 9
        STEPS = B + 4
        ACT_COND, DVE_COND = 6, 5
        LEAD = 6

        def pipeline(eng, step):
            for i in range(LEAD):
                step(i, i % 2, i // 2)
            with eng.Fori(LEAD // 2, B // 2) as n:
                for p in range(2):
                    step(2 * n + p, p, n)
            for i in range(B, STEPS):
                step(i, i % 2, i // 2)

        def known(i):
            return type(i) is int

        def active(i, lag):
            return not known(i) or 0 <= i - lag < B

        def upto(v):
            return min(v, B) if known(v) else v

        def atleast(eng, s, v):
            if not known(v) or v > 0:
                eng.wait_ge(s, v)

        def mixed(eng, k):
            eng.wait_ge(x2_ready if k > 0 else x2_first, max(k, 1))

        def carry(eng):
            eng.sem_inc(carried, 1)

        PE_STAGES = (0, 1, 2, 4, 5, 6, 9)
        ACT_STAGES = (0, 1, 2, 4, 5, 6)
        DVE_STAGES = (0, 2, 3, 6, 7, 9)

        def beside(cond, stages, c, k):
            for n, at in enumerate(stages):
                if at == c and k < NB:
                    cond(k, n)

        block = ctx.enter_context(nc.Block())

        @block.sync
        def _(sp):
            def load(i, p, n):
                if known(i) and i >= B:
                    return
                if not known(i) or i >= 2:
                    sp.wait_ge(x_in_ps, i - 1)
                sp.dma_start(xin[p][:, :], a["x"][bass.ds(i, 1)].rearrange("o t d -> (o t) d")).then_inc(s_in[p], 16)
                sp.dma_start(fin[p][:, :], a["fside_BxSxS_0"][bass.ds(i, 1)].rearrange("o t d -> (o t) d")).then_inc(s_in[p], 16)

            load(0, 0, 0)
            for dst, name in ((wq, "Wq"), (wk, "Wk")):
                sp.dma_start(dst[:, :], a[f"L0_cond_{name}"]).then_inc(w_att, 16)
            for n, ap in enumerate((a["L0_cond_b_prev"].rearrange("a b d -> d (a b)"),
                                    a["L0_cond_b_self"].rearrange("a b d -> d (a b)"),
                                    a["L0_cond_bk"].unsqueeze(1), a["L0_cond_bq"].unsqueeze(1))):
                sp.dma_start(cols[:, n:n + 1], ap).then_inc(w_att, 16)
            sp.dma_start(lens_i[:, :], a["itok_B_18_1004"].unsqueeze(0).broadcast_to([P, B])).then_inc(w_att, 16)
            sp.dma_start(wv[:, :], a["L0_cond_Wv"]).then_inc(w_att, 16)
            sp.dma_start(bvB[:, :], a["L0_cond_bv"].unsqueeze(0).broadcast_to([P, P])).then_inc(w_att, 16)
            load(1, 1, 0)
            sp.dma_start(types_i[:, :], a["itok_B_0_2"].unsqueeze(0).broadcast_to([P, B])).then_inc(w_rest, 16)
            sp.dma_start(wo[:, :], a["L0_cond_Wo"]).then_inc(w_rest, 16)
            sp.dma_start(cols[:, 4:5], a["L0_cond_bo"].unsqueeze(1)).then_inc(w_rest, 16)
            sp.dma_start(cols[0:A1, 5:6], a["L1_cond_b1"].unsqueeze(1)).then_inc(w_rest, 16)
            for dst, ap, n in ((boB, a["L0_cond_bo"], P), (gate0bB, a["L0_ffn_gate_b"], E0)):
                sp.dma_start(dst[:, :], ap.unsqueeze(0).broadcast_to([P, n])).then_inc(w_rest, 16)
            sp.dma_start(gate0[:, :], a["L0_ffn_gate_w"]).then_inc(w_rest, 16)
            sp.wait_ge(pool_const, FIRST_CONSTS)
            for part in range(RUNS * E0 // (P // 2)):
                sp.dma_start(ids_dram[(P // 2) * part:(P // 2) * (part + 1), :], zrow[0:P // 2, :]).then_inc(listed, 16)
            sp.dma_start(ids_dram[(P // 2) * (part + 1):, :], zrow[0:RUNS * E0 % (P // 2), :]).then_inc(listed, 16)
            for i in range(2, LEAD):
                load(i, i % 2, i // 2)
            sp.dma_start(w1c[:, :], a["L1_cond_W1"]).then_inc(w_l1, 16)
            sp.dma_start(vcol[:, :], a["L1_cond_v"].unsqueeze(1)).then_inc(w_l1, 16)
            sp.dma_start(gate1[:, :], a["L1_ffn_gate_w"]).then_inc(w_l1, 16)
            sp.dma_start(wg1[:, :].rearrange("d (e f) -> d e f", e=E1), a["L1_ffn_w_gate"].rearrange("e d f -> d e f")).then_inc(w_l1, 16)
            sp.dma_start(wu1[:, :].rearrange("d (e f) -> d e f", e=E1), a["L1_ffn_w_up"].rearrange("e d f -> d e f")).then_inc(w_l1, 16)
            sp.dma_start(wd1[:, :, :], a["L1_ffn_w_down"].rearrange("e f d -> (e f) d").rearrange("(c p) d -> p c d", p=P)).then_inc(w_l1, 16)
            sp.dma_start(wsg[:, :], a["L1_ffn_sw_gate"]).then_inc(w_l1, 16)
            sp.dma_start(wsu[:, :], a["L1_ffn_sw_up"]).then_inc(w_l1, 16)
            for c, (f, m) in enumerate(NSH):
                sp.dma_start(wsd[0:m, c, :], a["L1_ffn_sw_down"][f:f + m, :]).then_inc(w_l1, 16)
            sp.dma_start(b1_all, a["L0_ffn_b1"].rearrange("e (p c) -> p e c", c=C0)).then_inc(biases_in, 16)
            sp.dma_start(b2_all, a["L0_ffn_b2"].unsqueeze(0).broadcast_to([P, E0, P])).then_inc(biases_in, 16)
            ys_t = ys_dram.rearrange("(j p) d -> p j d", p=P)
            for j in range(0, MAX_TILES, ZERO_TILES):
                sp.dma_start(ys_t[:, j:j + ZERO_TILES, :], zrow[:, :].unsqueeze(1).broadcast_to([P, ZERO_TILES, P])).then_inc(zeroed, 16)

            def store(i):
                sp.wait_ge(a_ready, i - 3)
                sp.dma_start(at_dram[bass.ds(i - 4, 1)].rearrange("o t d -> (o t) d"),
                             a_all[:, bass.ds(i - 4, 1), :].rearrange("p o d -> p (o d)")).then_inc(a_stored, 16)

            for i in range(4, LEAD):
                store(i)
            with sp.Fori(LEAD // 2, B // 2) as n:
                for p in range(2):
                    load(2 * n + p, p, n)
                    store(2 * n + p)
            for i in range(B, STEPS):
                store(i)
            sp.wait_ge(plan_ready, 1)
            nl = sp.value_load(rounds[0:1, 0:1], min_val=MIN_TILES // RING - 1, max_val=MAX_TILES // RING - 1)
            w1_d, w2_d = a["L0_ffn_w1"], a["L0_ffn_w2"].rearrange("e (p c) d -> e p c d", c=C0)

            def load_tile(j, r, wait):
                if wait is not None:
                    sp.wait_ge(y_ready, wait)
                e = sp.value_load(table_i[0:1, bass.ds(j, 1)], min_val=0, max_val=E0 - 1)
                sp.dma_start(w1[r][:, :], w1_d[bass.ds(e, 1)].rearrange("o d f -> (o d) f")).then_inc(tile_in[r], 16)
                sp.dma_start(w2[r][:, :, :], w2_d[bass.ds(e, 1)].rearrange("o p c d -> (o p) c d")).then_inc(tile_in[r], 16)

            for r in ring:
                load_tile(r, r, None)
            with sp.Fori(1, nl + 1) as n:
                for r in ring:
                    load_tile(RING * n + r, r, RING * n + (r - RING + 1))
            for k in range(NB):
                if k >= 2:
                    mixed(sp, k - 2)
                sp.dma_start(xr[k % 2][:, :, :], a["x"][BLK * k:BLK * (k + 1)].rearrange("b t d -> t b d")).then_inc(xr_in[k % 2], 16)
            for k in range(NB):
                sp.wait_ge(ob_ready, k + 1)
                sp.dma_start(out[BLK * k:BLK * (k + 1)].rearrange("b t d -> t b d"), ob[k % 2][:, :, :]).then_inc(ob_out[k % 2], 16)
            for p in range(2):
                sp.wait_ge(ob_out[p], 16 * (NB // 2))

        @block.gpsimd
        def _(pool):
            g = nc.gpsimd

            def select(t, op, pattern, base, mult, fill):
                return g.affine_select(out=t, in_=t, compare_op=op, fill=fill, base=base, pattern=pattern,
                                       channel_multiplier=mult)

            steps = [0]

            def done(ins):
                steps[0] += 1
                ins.then_inc(pool_const, 1)
                pool.wait_ge(pool_const, steps[0])

            done(g.memset(ident[:, :], 0.0))
            done(select(ident[:, :], ALU.not_equal, [[-1, P]], 0, 1, 1.0))
            done(g.memset(ind[:, :], SCALE))
            done(select(ind[:, :], ALU.is_ge, [[-DH, H]], 0, 1, 0.0))
            done(select(ind[:, :], ALU.is_ge, [[DH, H]], DH - 1, -1, 0.0))
            done(g.iota(iota_p[:, :], pattern=[[0, 1]], base=0, channel_multiplier=1, allow_small_or_imprecise_dtypes=True))
            done(g.iota(iota_k[:, :], pattern=[[1, P]], base=0, channel_multiplier=0, allow_small_or_imprecise_dtypes=True))
            done(g.memset(zrow[:, :], 0.0))
            assert steps[0] == FIRST_CONSTS
            done(g.memset(mhl[0][:, :, :], 0.0))
            done(g.memset(mhl[1][:, :, :], 0.0))
            done(g.tensor_copy(identb[:, :], ident[:, :]))
            done(g.memset(pick_shift[:, :, :], 0.0))
            for part in range(2):
                v = pick_shift[:, :, :].rearrange("p (g j) q -> p g j q", g=NG)
                done(select(v, ALU.not_equal, [[-32, NG], [-1, NJ], [0, P]], -NJ * part, 1, 1.0))
            done(g.memset(onesb[:, :], 1.0))
            done(g.memset(before[:, :], 1.0))
            done(select(before[:, :], ALU.is_gt, [[1, P]], 0, -1, 0.0))
            done(g.iota(iota_e[:, :], pattern=[[1, E0]], base=0, channel_multiplier=0, allow_small_or_imprecise_dtypes=True))
            done(g.iota(region_of[:, :], pattern=[[REGION, E0]], base=0, channel_multiplier=0, allow_small_or_imprecise_dtypes=True))
            done(g.memset(held[:, :], 0.0))
            done(g.memset(ones_e[:, :], 1.0))
            for i in range(2):
                done(g.iota(tok[i][:, :], pattern=[[0, 1]], base=i * P, channel_multiplier=1, allow_small_or_imprecise_dtypes=True))
            assert steps[0] == CONSTS

            def second_layer_constants(i):
                across = lambda t: t[:, :].unsqueeze(1).broadcast_to([P, B, P])
                along = lambda t: t[:, :].unsqueeze(2).broadcast_to([P, B, P])
                if i == 0:
                    done(g.memset(prebias[:, :], 0.0))
                    done(select(prebias[:, :], ALU.is_ge, [[-1, P]], 0, 1, -BIG))
                    done(g.memset(postbias[:, :], 0.0))
                    done(select(postbias[:, :], ALU.is_ge, [[1, P]], 0, -1, -BIG))
                    done(g.memset(clozebias[:, :], 0.0))
                    done(select(clozebias[:, :], ALU.not_equal, [[-1, P]], 0, 1, -BIG))
                if i == 1:
                    done(g.memset(expert_of[:, :], 0.0))
                    for part in range(3):
                        v = expert_of[:, :].rearrange("p (e f) -> p e f", e=E1)
                        done(select(v, ALU.not_equal, [[-1, E1], [0, F1]], -E1 * part, 1, 1.0))
                if i == 2:
                    pool.wait_ge(chain_c, CHAIN_TYPES)
                    done(g.tensor_tensor(poolbias[:, :, :], across(prebias), along(is_pre), ALU.mult))
                if i == 3:
                    done(g.tensor_tensor(term, across(postbias), along(is_post), ALU.mult))
                if i == 4:
                    done(g.tensor_tensor(poolbias[:, :, :], poolbias[:, :, :], term, ALU.add))
                if i == 5:
                    done(g.tensor_tensor(term, across(clozebias), along(is_cloze), ALU.mult))
                    done(g.tensor_tensor(poolbias[:, :, :], poolbias[:, :, :], term, ALU.add))
                    assert steps[0] == ALL_CONSTS

            def expand(i, p):
                if not active(i, 0):
                    return
                if known(i) and i == 0:
                    pool.wait_ge(dve_const, 4)
                pool.wait_ge(chain_q, 2 * i + 1)
                atleast(pool, scores_in_ps, 4 * (i - 1))
                for g_ in range(2, NG):
                    rows = slice(32 * g_, 32 * g_ + 32)
                    g.tensor_tensor(qexp[p][rows, NJ * g_:NJ * (g_ + 1), :], qb[rows, :].unsqueeze(1).broadcast_to([32, NJ, P]),
                                    headmask[rows, :].unsqueeze(2).broadcast_to([32, NJ, P]), ALU.mult).then_inc(qexp_pool, 1)
                    pool.wait_ge(qexp_pool, 2 * i + (g_ - 1))

            def dispatch(i, p, n):
                expand(i, p)
                if known(i):
                    second_layer_constants(i)
                if not active(i, 4):
                    return
                pool.wait_ge(slots_ready, i - 3)
                if known(i) and i == 4:
                    pool.wait_ge(listed, 16 * (RUNS * E0 // (P // 2) + 1))
                carry(pool)
                for k in range(2):
                    g.indirect_dma_start(ids_dram.rearrange("r (t o) -> (r t) o", o=1), bass.IndirectOffsetOnAxis(ap=slots[p][:, k:k + 1], axis=0),
                                         tok[p][:, :], None).then_inc(scattered, 16)
                pool.wait_ge(scattered, 32 * (i - 3))
                carry(pool)
                g.tensor_scalar(tok[p][:, :], tok[p][:, :], float(2 * P), None, ALU.add).then_inc(tok_next, 1)
                pool.wait_ge(tok_next, i - 3)

            pipeline(pool, dispatch)

            pool.wait_ge(plan_ready, 1)
            pool.wait_ge(scattered, 32 * B)
            g.indirect_dma_start(tile_ids[:, :], None, ids_dram,
                                 bass.IndirectOffsetOnAxis(ap=tile_list[:, 0:1], axis=0)).then_inc(rows_in, 16)

            def gather_tile(j, r, wait):
                if wait is not None:
                    pool.wait_ge(xT_in_ps, wait)
                g.tensor_copy(row_r[r][:, :], tile_rows[:, bass.ds(j, 1)]).then_inc(copied, 1)
                pool.wait_ge(copied, j + 1)
                carry(pool)
                g.indirect_dma_start(xt[r][:, :], None, at_dram.rearrange("b t d -> (b t) d"),
                                     bass.IndirectOffsetOnAxis(ap=row_r[r][:, 0:1], axis=0)).then_inc(xt_in[r], 16)

            pool.wait_ge(rows_ready, 1)
            pool.wait_ge(a_stored, 16 * B)
            for r in ring:
                gather_tile(r, r, None)
            nl = pool.value_load(rounds[0:1, 0:1], min_val=MIN_TILES // RING - 1, max_val=MAX_TILES // RING - 1)
            with pool.Fori(1, nl + 1) as n:
                for r in ring:
                    gather_tile(RING * n + r, r, RING * n + (r - RING + 1))
            gather_tile(RING * nl + RING, 0, RING * nl + 1)

            for r in ring:
                pool.wait_ge(y_out[r], 16)
            pool.wait_ge(yslot_ready, 1)
            for r in ring:
                pool.wait_ge(y_out[r], nl * 16 + 16)
            carry(pool)
            for k in range(NB):
                if k >= 2:
                    mixed(pool, k - 2)
                for t in range(BLK):
                    for s, y in ((0, y1), (1, y2)):
                        n = 2 * (BLK * k + t) + s
                        g.indirect_dma_start(y[k % 2][:, t, :], None, ys_dram,
                                             bass.IndirectOffsetOnAxis(ap=yslot[:, n:n + 1], axis=0)).then_inc(gathered[k % 2], 16)
                if k > 0:
                    blk = slice(BLK * k, BLK * (k + 1))
                    pool.wait_ge(gathered[k % 2], 16 * 2 * BLK * (k // 2 + 1))
                    pool.wait_ge(xr_in[k % 2], 16 * (k // 2 + 1))
                    pool.wait_ge(a_ready, B)
                    gates = lambda t: t[:, blk].unsqueeze(2).broadcast_to([P, BLK, P])
                    for n, (o, x, y, op) in enumerate(((mix1p, y1[k % 2], gates(g1), ALU.mult), (mix2p, y2[k % 2], gates(g2), ALU.mult),
                                                       (mix1p, mix1p, xr[k % 2][:, :, :], ALU.add), (mix2p, mix2p, a_all[:, blk, :], ALU.add))):
                        g.tensor_tensor(o, x, y, op).then_inc(mix_step, 1)
                        pool.wait_ge(mix_step, 4 * (k - 1) + n + 1)
                    g.tensor_tensor(x2[:, blk, :], mix1p, mix2p, ALU.add).then_inc(x2_ready, 1)
                    pool.wait_ge(x2_ready, k)

        @block.tensor
        def _(pe):
            pe.wait_ge(w_att, 16 * 9)
            pe.wait_ge(pool_const, FIRST_CONSTS)
            for n, (w, c) in enumerate(((wk, 0), (wk, 1), (wq, 1))):
                mm_ = pe.matmul(psY[:, n:n + 1], w[:, :], cols[:, c:c + 1], start=True, stop=True)
            mm_.then_inc(cb_in_ps, 1)

            def shifted_scores(i, p, g):
                if not active(i, 2):
                    return
                ps = psB[g % 2]
                atleast(pe, exp_done, 4 * (i - 2) + (g - 1))
                pe.matmul(ps[:, :], kT[p][:, :], qexp[p][:, NJ * g:NJ * (g + 1), :].rearrange("p j t -> p (j t)"),
                          start=True, stop=False, skip_group_check=True)
                for j in range(NJ):
                    m = pe.matmul(ps[:, j * P:(j + 1) * P], pick_shift[:, NJ * g + j, :], shT[p][:, :],
                                  start=False, stop=(j == NJ - 1), skip_group_check=True)
                m.then_inc(scores_in_ps, 1)

            def weighted_values(i, p, g):
                if not active(i, 2):
                    return
                pe.wait_ge(exp_done, 4 * (i - 2) + (g + 1))
                if g == 0:
                    atleast(pe, att_ready, i - 2)
                    pe.wait_ge(self_read, upto(i))
                for j in range(NJ):
                    h = NJ * g + j
                    m = pe.matmul(psO[:, h * (DH + 1):(h + 1) * (DH + 1)], pT[g % 2][:, j * P:(j + 1) * P],
                                  v9[p][:, h, :], start=True, stop=True)
                m.then_inc(pv_done, 1)

            def max_scores(i, p, g):
                if not active(i, 1):
                    return
                if g == 0:
                    pe.wait_ge(kA_ready, i)
                    pe.wait_ge(qexp_dve, i)
                if g == 2:
                    pe.wait_ge(qexp_pool, 2 * i)
                atleast(pe, reduced, 4 * (i - 1) + (g - 1))
                for j in range(NJ):
                    m = pe.matmul(psA[g % 2][:, j * P:(j + 1) * P], qexp[1 - p][:, NJ * g + j, :], kA[1 - p][:, :], start=True, stop=True)
                m.then_inc(a_in_ps, 1)

            def step(i, p, n):
                if known(i) and i == 2:
                    pe.wait_ge(pool_const, CONSTS)
                if known(i) and i == 3:
                    pe.wait_ge(w_rest, 16 * 7)
                if active(i, 2):
                    pe.wait_ge(shift_ready, i - 1)
                    pe.wait_ge(x_read, i)
                    pe.transpose(ps_shT, mhl[p][:, :, :].rearrange("p g c -> p (g c)"), identb[:, :]).then_inc(shiftT_in_ps, 1)
                    pe.wait_ge(shiftT_ready, i - 1)
                shifted_scores(i, p, 0)
                if active(i, 0) or active(i, 3):
                    if not active(i, 2):
                        atleast(pe, x_read, i)
                    if active(i, 0):
                        pe.wait_ge(s_in[p], 32 * (n + 1))
                        m = pe.transpose(ps_xf[:, 0:P], xin[p][:, :], ident[:, :])
                        m = pe.transpose(ps_xf[:, P:2 * P], fin[p][:, :], ident[:, :])
                    if active(i, 3):
                        pe.wait_ge(att_ready, i - 2)
                        m = pe.transpose(ps_att, att[1 - p][:, :], ident[:, :])
                    m.then_inc(x_in_ps, 1)
                if active(i, 1):
                    pe.wait_ge(prod_ready, i)
                    atleast(pe, att_ready, i - 2)
                    pe.matmul(ps_self, prod[:, :], ind[:, :], start=True, stop=True).then_inc(self_in_ps, 1)
                shifted_scores(i, p, 1)
                if active(i, 3):
                    pe.wait_ge(x_read, i + 1)
                    pe.wait_ge(z_read, upto(i))
                    pe.matmul(ps_aT, wo[:, :], attT[1 - p][:, :], start=True, stop=True).then_inc(aT_in_ps, 1)
                weighted_values(i, p, 0)
                max_scores(i, p, 0)
                if active(i, 3) or active(i, 4):
                    pe.wait_ge(v_ready, upto(i))
                    atleast(pe, y_read, i - 3)
                    if active(i, 3):
                        pe.wait_ge(aT_ready, i - 2)
                        m = pe.matmul(ps_a, attT[1 - p][:, :], wo[:, :], start=True, stop=True)
                        m = pe.matmul(ps_lg, aT[1 - p][:, :], gate0[:, :], start=True, stop=True)
                    if active(i, 4):
                        pe.wait_ge(picks_ready, i - 3)
                        pe.matmul(ps_rank, before[:, :], picked[p][:, :], start=True, stop=True)
                        m = pe.matmul(ps_tot, onesb[:, :], picked[p][:, :], start=True, stop=True)
                    m.then_inc(y_in_ps, 1)
                shifted_scores(i, p, 2)
                weighted_values(i, p, 1)
                max_scores(i, p, 1)
                shifted_scores(i, p, 3)
                max_scores(i, p, 2)
                weighted_values(i, p, 2)
                max_scores(i, p, 3)
                weighted_values(i, p, 3)
                if active(i, 0):
                    if known(i) and i == 0:
                        pe.wait_ge(cb_ready, 1)
                    pe.wait_ge(x_read, i + 1)
                    if known(i) and 0 < i < 3:
                        pe.wait_ge(v_ready, i)
                        pe.wait_ge(z_read, i)
                    atleast(pe, y_read, i - 2)
                    pe.matmul(ps_q, wq[:, :], xfT[p][:, P:2 * P], start=True, stop=True)
                    pe.matmul(ps_ks, wk[:, :], xfT[p][:, P:2 * P], start=True, stop=True)
                    pe.matmul(ps_v, xfT[p][:, 0:P], wv[:, :], start=True, stop=True)
                    pe.matmul(ps_vs, xfT[p][:, P:2 * P], wv[:, :], start=True, stop=True).then_inc(kqv_in_ps, 1)
                    atleast(pe, aT_ready, i - 2)
                    pe.matmul(ps_k, wk[:, :], xfT[p][:, 0:P], start=True, stop=True).then_inc(z_in_ps, 1)

            pipeline(pe, step)

            pe.wait_ge(table_ready, 1)
            pe.wait_ge(y_read, STEPS - 3)
            pe.transpose(psY[0:1, 0:P], table[:, 0:1], ident[:, :]).then_inc(table_in_ps, 1)
            pe.wait_ge(x_read, STEPS - 1)
            pe.wait_ge(rows_in, 16)
            pe.transpose(psX[:, 0:P], tile_ids[:, :], ident[:, :]).then_inc(rows_in_ps, 1)
            pe.wait_ge(w_l1, 16 * 11)
            pe.transpose(psZ[:, 0:E1], gate1[:, :], ident[0:E1, 0:E1]).then_inc(gT_in_ps, 1)
            pe.wait_ge(plan_ready, 1)
            nl = pe.value_load(rounds[0:1, 0:1], min_val=MIN_TILES // RING - 1, max_val=MAX_TILES // RING - 1)

            def transpose_tile(j, r, n):
                pe.wait_ge(xt_in[r], 16 * (n + 1))
                pe.transpose(banks[4 + r % 2][:, 0:P], xt[r][:, :], ident[:, :]).then_inc(xT_in_ps, 1)

            def up(j, r, n, first):
                pe.wait_ge(tile_in[r], 32 * (n + 1))
                pe.wait_ge(xT_ready, j + 1)
                for c in range(C0):
                    if not first or r > 0:
                        pe.wait_ge(gelu_done, C0 * (j - 1) + (c + 1))
                    pe.matmul(banks[c][:, 0:P], w1[r][:, :].rearrange("d (f c) -> d c f", c=C0)[:, c, :],
                              xT[r % 2][:, :], start=True, stop=True).then_inc(hid_in_ps, 1)

            def down(j, r):
                for c in range(C0):
                    pe.wait_ge(gelu_done, C0 * j + (c + 1))
                    m = pe.matmul(banks[6 + r % 2][:, 0:P], hT[r % 2][:, c, :], w2[r][:, c, :], start=(c == 0), stop=(c == C0 - 1))
                m.then_inc(t_in_ps, 1)

            def round_of_tiles(n, first):
                for r in ring:
                    j = RING * n + r
                    up(j, r, n, first)
                    transpose_tile(j + 1, (r + 1) % RING, n + (r + 1) // RING)
                    if r > 0 or not first:
                        if not first or r >= 3:
                            pe.wait_ge(y_ready, j - 2)
                        down(j - 1, (r - 1) % RING)

            transpose_tile(0, 0, 0)
            round_of_tiles(0, True)
            with pe.Fori(1, nl + 1) as n:
                round_of_tiles(n, False)
            pe.wait_ge(y_ready, nl * RING + (RING - 2))
            down(nl * RING + (RING - 1), RING - 1)

            pc, pd = banks[6], banks[7]
            steps = [0]

            def signal(ins):
                steps[0] += 1
                ins.then_inc(c_pe, 1)

            def cond(k, stage):
                base_a, base_d = ACT_COND * k, DVE_COND * k
                if stage == 0:
                    mixed(pe, k)
                    for t in range(BLK):
                        m = pe.transpose(pc[:, t * P:(t + 1) * P], x2[:, BLK * k + t, :], ident[:, :])
                    signal(m)
                if stage == 1:
                    pe.wait_ge(c_act, base_a + 1)
                    signal(pe.matmul(pd[0:A1, :], w1c[:, :], x2T[:, :], start=True, stop=True))
                if stage == 2:
                    pe.wait_ge(c_act, base_a + 2)
                    signal(pe.matmul(pc[:, :], vB[:, :], th[:, :], start=True, stop=True))
                if stage == 3:
                    pe.wait_ge(c_dve, base_d + 3)
                    for t in range(BLK):
                        m = pe.transpose(pd[:, t * P:(t + 1) * P], pn[:, t, :], ident[:, :])
                    signal(m)
                if stage == 4:
                    pe.wait_ge(c_act, base_a + 4)
                    for t in range(BLK):
                        m = pe.matmul(pc[:, t * P:(t + 1) * P], x2[:, BLK * k + t, :], pnT[:, t * P:(t + 1) * P], start=True, stop=True)
                    signal(m)
                if stage == 5:
                    pe.wait_ge(c_act, base_a + 5)
                    for t in range(BLK):
                        m = pe.matmul(pd[:, t * E1:(t + 1) * E1], plT[k % 2][:, t * P:(t + 1) * P], gate1T[:, :], start=True, stop=True)
                    signal(m)
                if stage == 6:
                    pe.wait_ge(c_dve, base_d + 5)
                    for t in range(BLK):
                        m = pe.transpose(pc[:, :].bitcast(BF16)[0:3 * E1, t * P:(t + 1) * P], cparts[:, t, :], identb[:, :])
                    signal(m)

            def ffn(k):
                x = plT[k % 2]
                pe.wait_ge(cond_ready, k + 1)
                if k == 0:
                    pe.wait_ge(pool_const, ALL_CONSTS)   
                for c in range(NC1):
                    n = NC1 * k + c
                    f, m = (c * P, P) if c < NE else NSH[c - NE]
                    wg, wu = (wg1, wu1) if c < NE else (wsg, wsu)
                    atleast(pe, h_ready, n - 1)
                    pe.matmul(banks[n % 2][0:m, :], wg[:, f:f + m], x[:, :], start=True, stop=True)
                    pe.matmul(banks[2 + n % 2][0:m, :], wu[:, f:f + m], x[:, :], start=True, stop=True).then_inc(gu_in_ps, 1)
                    if c < NE:
                        atleast(pe, h_ready, n)
                        pe.matmul(banks[4][:, :], expert_of[:, f:f + P], cT[k % 2][:, :], start=True, stop=True).then_inc(wt_in_ps, 1)
                    beside(cond, PE_STAGES, c, k + 1)
                atleast(pe, ob_ready, k)
                for t in range(BLK):
                    pe.wait_ge(h_ready, NC1 * (k + 1))
                    for c in range(NC1):
                        m = P if c < NE else NSH[c - NE][1]
                        wd = wd1[:, c, :] if c < NE else wsd[0:m, c - NE, :]
                        y = pe.matmul(banks[5][:, t * P:(t + 1) * P], h1[0:m, c, t * P:(t + 1) * P], wd, start=(c == 0), stop=(c == NC1 - 1))
                y.then_inc(out_acc, 1)

            pe.wait_ge(gT_ready, 1)
            pe.wait_ge(y_ready, nl * RING + RING)
            for n in range(len(PE_STAGES)):
                cond(0, n)
            for k in range(NB):
                ffn(k)

        @block.scalar
        def _(act):
            s = nc.scalar

            def weights(i, p, g):
                if not active(i, 2):
                    return
                act.wait_ge(scores_in_ps, 4 * (i - 2) + (g + 1))
                atleast(act, pv_done, 4 * (i - 2) + (g - 1))
                carry(act)
                kb = keybias[:, bass.ds(i - 2, 1)]
                s.activation(pT[g % 2][:, :], psB[g % 2][:, :], ACT.Exp, bias=kb).then_inc(exp_done, 1)

            def step(i, p, n):
                if active(i, 2):
                    act.wait_ge(shiftT_in_ps, i - 1)
                    atleast(act, scores_in_ps, 4 * (i - 3))
                    s.activation(shT[p][:, :], ps_shT, ACT.Identity).then_inc(shiftT_ready, 1)
                    atleast(act, att_ready, i - 3)
                    s.activation(ws[p][:, :], sm[:, :], ACT.Exp).then_inc(ws_ready, 1)
                weights(i, p, 0)
                if active(i, 0) or active(i, 3):
                    act.wait_ge(x_in_ps, i + 1)
                    if active(i, 0):
                        atleast(act, kqv_in_ps, i - 1)
                        atleast(act, z_in_ps, i - 1)
                        m = s.activation(xfT[p][:, :], ps_xf, ACT.Identity)
                    if active(i, 3):
                        atleast(act, y_in_ps, i - 4)
                        m = s.activation(attT[1 - p][:, :], ps_att, ACT.Identity)
                    m.then_inc(x_read, 1)
                weights(i, p, 1)
                if known(i) and i == 3:
                    act.wait_ge(w_rest, 16 * 7)
                if active(i, 3):
                    act.wait_ge(aT_in_ps, i - 2)
                    s.activation(aT[1 - p][:, :], ps_aT, ACT.Identity, bias=cols[:, 4:5]).then_inc(aT_ready, 1)
                if active(i, 1):
                    act.wait_ge(kv_ready, i)
                    act.wait_ge(z_read, i)
                    atleast(act, a_in_ps, 4 * (i - 2))
                    s.activation(kA[1 - p][:, :], kv[:, :], ACT.Identity, bias=kT[1 - p][:, 0:1]).then_inc(kA_ready, 1)
                weights(i, p, 2)
                weights(i, p, 3)
                if known(i) and i == 0:
                    act.wait_ge(cb_ready, 1)
                if active(i, 0):
                    act.wait_ge(z_in_ps, i + 1)
                    atleast(act, scores_in_ps, 4 * (i - 1))
                    s.activation(kT[p][:, :], ps_k, ACT.Identity, bias=cbias[:, 0:1]).then_inc(z_read, 1)

            pipeline(act, step)

            act.wait_ge(chain_l, 6 * B)
            s.activation(eg[:, :], gap[:, :], ACT.Exp).then_inc(gap_exp, 1)
            act.wait_ge(gap_exp, 1)
            s.activation(gelu_warm[:, :], eg[:, 0:1], ACT.Gelu)
            act.wait_ge(plan_ready, 1)
            nl = act.value_load(rounds[0:1, 0:1], min_val=MIN_TILES // RING - 1, max_val=MAX_TILES // RING - 1)
            ys_t = ys_dram.rearrange("(j p) d -> j p d", p=P)
            act.wait_ge(zeroed, 16 * (MAX_TILES // ZERO_TILES))

            def send(j, r):
                act.wait_ge(y_ready, j + 1)
                act.dma_start(ys_t[bass.ds(j, 1)].rearrange("o p d -> (o p) d"), yb[r][:, :]).then_inc(y_out[r], 16)

            def round_of_tiles(n, first):
                for r in ring:
                    j = RING * n + r
                    for c in range(C0):
                        act.wait_ge(hid_in_ps, C0 * j + (c + 1))
                        if c == 0:
                            act.wait_ge(b1_ready, j + 1)
                            if not first or r >= 2:
                                act.wait_ge(t_in_ps, RING * n + (r - 1))
                        s.activation(hT[r % 2][:, c, :], banks[c][:, 0:P], ACT.Gelu,
                                     bias=b1[r][:, c:c + 1]).then_inc(gelu_done, 1)
                    if r > 0 or not first:
                        send(j - 1, (r - 1) % RING)

            round_of_tiles(0, True)
            with act.Fori(1, nl + 1) as n:
                round_of_tiles(n, False)
            send(nl * RING + (RING - 1), RING - 1)

            pc, pd = banks[6], banks[7]

            def cond(k, stage):
                bp, bd = 7 * k, DVE_COND * k
                if stage == 0:
                    act.wait_ge(c_pe, bp + 1)
                    s.activation(x2T[:, :], pc[:, :], ACT.Identity).then_inc(c_act, 1)
                if stage == 1:
                    act.wait_ge(c_pe, bp + 2)
                    s.activation(th[:, :], pd[0:A1, :], ACT.Tanh, bias=cols[0:A1, 5:6]).then_inc(c_act, 1)
                if stage == 2:
                    act.wait_ge(c_dve, bd + 2)
                    for t in range(BLK):
                        m = s.activation(pe_[:, t, :], ms[:, t, :], ACT.Exp, bias=nm[:, t:t + 1], accum_out=psum_[:, t:t + 1])
                    m.then_inc(c_act, 1)
                if stage == 3:
                    act.wait_ge(c_pe, bp + 4)
                    s.activation(pnT[:, :], pd[:, :], ACT.Identity).then_inc(c_act, 1)
                if stage == 4:
                    act.wait_ge(c_pe, bp + 5)
                    atleast(act, out_acc, k - 1)
                    s.activation(plT[k % 2][:, :], pc[:, :], ACT.Identity).then_inc(c_act, 1)
                if stage == 5:
                    act.wait_ge(c_dve, bd + 4)
                    s.activation(e8[:, :, :].rearrange("p b e -> p (b e)"), ls8[:, :, :].rearrange("p b e -> p (b e)"), ACT.Exp).then_inc(c_act, 1)

            def ffn(k):
                for c in range(NC1):
                    n = NC1 * k + c
                    m = P if c < NE else NSH[c - NE][1]
                    act.wait_ge(gu_in_ps, n + 1)
                    atleast(act, h_ready, n - 1)
                    s.activation(sg[n % 2][0:m, :], banks[n % 2][0:m, :], ACT.Silu).then_inc(silu_done, 1)
                    beside(cond, ACT_STAGES, c, k + 1)

            for n in range(len(ACT_STAGES)):
                cond(0, n)
            for k in range(NB):
                ffn(k)

        @block.vector
        def _(dve):
            v = nc.vector

            class Chain:

                def __init__(self, s, per):
                    self.s, self.per, self.k, self.base = s, per, 0, 0

                def start(self, b):
                    self.base, self.k = self.per * b, 0

                def add(self, ins):
                    self.k += 1
                    assert self.k <= self.per
                    ins.then_inc(self.s, 1)

                def link(self, ins):
                    self.add(ins)
                    dve.wait_ge(self.s, self.base + self.k)

                def join(self):
                    dve.wait_ge(self.s, self.base + self.k)

            cc = Chain(chain_c, 22)
            cc.start(0)
            for t in qexp:
                v.memset(t[:, :, :], 0.0).then_inc(dve_const, 1)
            for t in v9:
                v.memset(t[:, :, :], 1.0).then_inc(dve_const, 1)
            dve.wait_ge(dve_const, 4)
            dve.wait_ge(w_att, 16 * 9)
            dve.wait_ge(pool_const, FIRST_CONSTS)
            dve.wait_ge(cb_in_ps, 1)
            v.tensor_tensor(cbias[:, 0:1], psY[:, 0:1], cols[:, 2:3], ALU.add)
            v.tensor_tensor(cbias[:, 1:2], psY[:, 1:2], cols[:, 2:3], ALU.add)
            v.tensor_tensor(cbias[:, 2:3], psY[:, 2:3], cols[:, 3:4], ALU.add).then_inc(cb_ready, 1)
            dve.wait_ge(cb_ready, 1)
            cc.link(v.tensor_copy(lens[:, :], lens_i[:, :]))
            cc.add(v.tensor_scalar(nolen[:, :], lens[:, :], 1.0, -BIG, ALU.is_lt, ALU.mult))
            cc.add(v.tensor_scalar(keybias[:, :], lens[:, :], iota_p[:, 0:1], -BIG, ALU.is_le, ALU.mult))
            cc.link(v.tensor_reduce(headmask[:, :], ind[:, :].rearrange("p (g j) -> p j g", g=NG), AX_X, ALU.add))

            def types_constants():
                dve.wait_ge(w_rest, 16 * 7)
                cc.link(v.tensor_copy(types[:, :], types_i[:, :]))
                cc.add(v.tensor_scalar(is_pre[:, :], types[:, :], 0.0, None, ALU.is_equal))
                cc.link(v.tensor_scalar(is_post[:, :], types[:, :], 1.0, None, ALU.is_equal))
                cc.link(v.tensor_tensor(tmp_b[:, :], is_pre[:, :], is_post[:, :], ALU.add))
                cc.link(v.tensor_scalar(is_cloze[:, :], tmp_b[:, :], -1.0, 1.0, ALU.mult, ALU.add))
                assert cc.k == CHAIN_TYPES
                cc.add(v.tensor_scalar(tmp_c[:, 0:1], iota_p[:, 0:1], 1.0, None, ALU.add))
                cc.link(v.tensor_scalar(tmp_c[:, 1:2], iota_p[:, 0:1], -1.0, float(P), ALU.mult, ALU.add))
                cc.link(v.tensor_scalar(count[:, :], is_cloze[:, :], float(P - 1), None, ALU.mult))
                cc.link(v.scalar_tensor_tensor(out=count[:, :], in0=is_pre[:, :], scalar=tmp_c[:, 0:1], in1=count[:, :], op0=ALU.mult, op1=ALU.add))
                cc.link(v.scalar_tensor_tensor(out=count[:, :], in0=is_post[:, :], scalar=tmp_c[:, 1:2], in1=count[:, :], op0=ALU.mult, op1=ALU.add))

            cq, cn, cm, cl, cr = (Chain(x, y) for x, y in ((chain_q, 2), (chain_n, 4), (chain_m, 4), (chain_l, 6), (chain_r, 5)))

            def maximum(i, g):
                if not active(i, 1):
                    return
                dve.wait_ge(a_in_ps, 4 * (i - 1) + (g + 1))
                v.tensor_reduce(mx[:, NJ * g:NJ * g + NJ], psA[g % 2][:, :].rearrange("p (j k) -> p j k", j=NJ), AX_X,
                                ALU.max).then_inc(reduced, 1)

            def step(i, p, n):
                if known(i) and i == 1:
                    types_constants()
                    dve.wait_ge(pool_const, CONSTS)
                if active(i, 1):
                    dve.wait_ge(self_in_ps, i)
                    v.tensor_copy(selfs[:, :], ps_self).then_inc(self_read, 1)
                maximum(i, 0)
                if active(i, 3) or active(i, 4):
                    dve.wait_ge(y_in_ps, i - 2)
                if active(i, 3):
                    cl.start(i - 3)
                    cl.add(v.tensor_tensor(lg[:, :], ps_lg, gate0bB[:, :], ALU.add))
                    v.tensor_tensor(a_all[:, bass.ds(i - 3, 1), :].rearrange("p o d -> p (o d)"), ps_a, boB[:, :], ALU.add).then_inc(a_ready, 1)
                    if not active(i, 4):
                        v.tensor_copy(y_token[:, :], ps_lg[:, 0:1]).then_inc(y_read, 1)
                if active(i, 4):
                    cr.start(i - 4)
                    cr.add(v.tensor_tensor(rank[:, :], ps_rank, held[:, :], ALU.add))
                    cr.link(v.tensor_tensor(held[:, :], ps_tot, held[:, :], ALU.add))
                    v.tensor_copy(y_token[:, :], ps_rank[:, 0:1]).then_inc(y_read, 1)
                    b = i - 4
                    cr.link(v.tensor_tensor(rank[:, :], rank[:, :], region_of[:, :], ALU.add))
                    cr.link(v.tensor_tensor(rsel[:, :, :], onehot[:, bass.ds(b, 1), :, :].rearrange("p o k e -> p (o k) e"),
                                            rank[:, :].unsqueeze(1).broadcast_to([P, 2, E0]), ALU.mult))
                    sl = slotf[:, bass.ds(b, 1), :].rearrange("p o k -> p (o k)")
                    cr.link(v.tensor_reduce(sl, rsel[:, :, :], AX_X, ALU.add))
                    atleast(dve, scattered, 32 * (i - 5))
                    carry(dve)
                    v.tensor_copy(slots[p][:, :], sl).then_inc(slots_ready, 1)
                maximum(i, 1)
                if active(i, 3):
                    b = i - 3
                    cl.join()
                    carry(dve)
                    cl.link(v.max(top8[:, :], lg[:, :]))
                    carry(dve)
                    cl.link(v.max_index(topi[:, :], top8[:, :], lg[:, :]))
                    cl.link(v.tensor_copy(topf[:, :], topi[:, 0:2]))
                    cl.add(v.tensor_tensor(gap[:, bass.ds(b, 1)], top8[:, 1:2], top8[:, 0:1], ALU.subtract))
                    oh = onehot[:, bass.ds(b, 1), :, :].rearrange("p o k e -> p (o k) e")
                    cl.link(v.tensor_tensor(oh, iota_e[:, :].unsqueeze(1).broadcast_to([P, 2, E0]),
                                            topf[:, :].unsqueeze(2).broadcast_to([P, 2, E0]), ALU.is_equal))
                    atleast(dve, y_in_ps, i - 3)
                    v.tensor_tensor(picked[1 - p][:, :], onehot[:, bass.ds(b, 1), 0, :].rearrange("p o e -> p (o e)"),
                                    onehot[:, bass.ds(b, 1), 1, :].rearrange("p o e -> p (o e)"), ALU.add).then_inc(picks_ready, 1)
                maximum(i, 2)
                maximum(i, 3)
                if active(i, 1):
                    cm.start(i - 1)
                    dve.wait_ge(reduced, 4 * i)
                    dve.wait_ge(self_read, i)
                    cm.link(v.scalar_tensor_tensor(out=mm[:, :], in0=mx[:, :], scalar=nolen[:, bass.ds(i - 1, 1)], in1=selfs[:, :],
                                                   op0=ALU.add, op1=ALU.max))
                    atleast(dve, shiftT_in_ps, i - 2)
                    hi, lo = mhl[1 - p][:, :, 0:NJ], mhl[1 - p][:, :, NJ:2 * NJ]
                    gj = lambda t: t[:, :].rearrange("p (g j) -> p g j", g=NG)
                    cm.link(v.tensor_scalar(hi, gj(mm), -1.0, None, ALU.mult))
                    cm.link(v.scalar_tensor_tensor(out=lo, in0=gj(mm), scalar=-1.0, in1=hi, op0=ALU.mult, op1=ALU.subtract))
                    cm.link(v.tensor_tensor(gj(sm0), gj(selfs), hi, ALU.add))
                    atleast(dve, ws_ready, i - 1)
                    v.tensor_tensor(gj(sm), gj(sm0), lo, ALU.add).then_inc(shift_ready, 1)
                if active(i, 2):
                    cn.start(i - 2)
                    dve.wait_ge(pv_done, 4 * (i - 1))
                    dve.wait_ge(ws_ready, i - 1)
                    o = psO[:, 0:H * (DH + 1)].rearrange("p (h d) -> p h d", h=H)
                    wb = ws[p][:, :].unsqueeze(2).broadcast_to([P, H, DH])
                    cn.link(v.tensor_tensor(den[:, :], o[:, :, DH:DH + 1].rearrange("p h o -> p (h o)"), ws[p][:, :], ALU.add))
                    cn.add(v.reciprocal(rec[:, :], den[:, :]))
                    dve.wait_ge(v_ready, i - 1)
                    hd = lambda t: t[:, :].rearrange("p (h d) -> p h d", h=H)
                    cn.link(v.tensor_tensor(hd(t1), hd(vs[p]), wb, ALU.mult))
                    cn.link(v.tensor_tensor(hd(t2), hd(t1), o[:, :, 0:DH], ALU.add))
                    atleast(dve, x_in_ps, i)
                    v.tensor_tensor(hd(att[p]), hd(t2), rec[:, :].unsqueeze(2).broadcast_to([P, H, DH]), ALU.mult).then_inc(att_ready, 1)
                if active(i, 0):
                    cq.start(i)
                    dve.wait_ge(kqv_in_ps, i + 1)
                    atleast(dve, qexp_pool, 2 * i)
                    cq.link(v.tensor_scalar(qb[:, :], ps_q, cbias[:, 2:3], None, ALU.add))
                    v.scalar_tensor_tensor(out=prod[:, :], in0=ps_ks, scalar=cbias[:, 1:2], in1=qb[:, :],
                                           op0=ALU.add, op1=ALU.mult).then_inc(prod_ready, 1)
                    dve.wait_ge(z_read, i + 1)
                    cq.link(v.tensor_scalar(kd[:, :], kT[p][:, :], kT[p][:, 0:1], None, ALU.subtract))
                    atleast(dve, kA_ready, i)
                    v.scalar_tensor_tensor(out=kv[:, :], in0=iota_k[:, :], scalar=lens[:, bass.ds(i, 1)], in1=kd[:, :],
                                           op0=ALU.is_lt, op1=ALU.mult).then_inc(kv_ready, 1)
                    atleast(dve, scores_in_ps, 4 * (i - 1))
                    for g in range(2):
                        rows = slice(32 * g, 32 * g + 32)
                        ins = v.tensor_tensor(qexp[p][rows, NJ * g:NJ * (g + 1), :], qb[rows, :].unsqueeze(1).broadcast_to([32, NJ, P]),
                                              headmask[rows, :].unsqueeze(2).broadcast_to([32, NJ, P]), ALU.mult)
                    ins.then_inc(qexp_dve, 1)
                    atleast(dve, pv_done, 4 * (i - 1))
                    v.tensor_tensor(v9[p][:, :, 0:DH], ps_v.rearrange("p (h d) -> p h d", h=H),
                                    bvB[:, :].rearrange("p (h d) -> p h d", h=H), ALU.add)
                    v.tensor_tensor(vs[p][:, :], ps_vs, bvB[:, :], ALU.add).then_inc(v_ready, 1)

            pipeline(dve, step)

            ct = Chain(chain_t, 40)
            ct.start(0)
            cr.start(B - 1)
            cr.k = 5
            cr.join()
            ct.link(v.tensor_scalar(nti[:, :], held[:, :], float(P - 1), None, ALU.add))
            ct.link(v.tensor_scalar(nti[:, :], nti[:, :], 7, None, ALU.arith_shift_right))
            ct.link(v.tensor_copy(ntf[:, :], nti[:, :]))
            ct.link(v.tensor_tensor_scan(incl[:, :], ones_e[:, :], ntf[:, :], 0.0, ALU.mult, ALU.add))
            ct.add(v.tensor_tensor(excl[:, :], incl[:, :], ntf[:, :], ALU.subtract))
            ct.link(v.tensor_scalar(below[:, :], incl[:, :], iota_p[:, 0:1], None, ALU.is_le))
            ct.add(v.tensor_reduce(ej[:, :], below[:, :], AX_X, ALU.add))
            ct.link(v.tensor_tensor(under[:, :], below[:, :], incl[:, :], ALU.mult))
            ct.link(v.tensor_reduce(tj[:, :], under[:, :], AX_X, ALU.max))
            ct.link(v.tensor_tensor(tj[:, :], iota_p[:, :], tj[:, :], ALU.subtract))
            ct.link(v.scalar_tensor_tensor(out=tj[:, :], in0=ej[:, :], scalar=float(RUNS), in1=tj[:, :], op0=ALU.mult, op1=ALU.add))
            ct.add(v.tensor_scalar(table[:, 0:1], ej[:, :], float(E0 - 1), None, ALU.min))
            ct.add(v.tensor_scalar(tile_list[:, :], tj[:, :], float(E0 * RUNS - 1), None, ALU.min))
            ct.link(v.tensor_scalar(rounds_i[:, :], incl[:, E0 - 1:E0], -1.0, None, ALU.add))
            v.engine_nop().then_inc(table_ready, 1)
            ct.add(v.tensor_scalar(rounds[:, :], rounds_i[:, :], 2, None, ALU.arith_shift_right))
            dve.wait_ge(table_in_ps, 1)
            ct.link(v.tensor_copy(table_i[:, :], psY[0:1, 0:P]))
            v.engine_nop().then_inc(plan_ready, 1)
            dve.wait_ge(gap_exp, 1)
            ct.link(v.tensor_scalar(g1[:, :], eg[:, :], 1.0, None, ALU.add))
            ct.link(v.reciprocal(g1[:, :], g1[:, :]))
            ct.link(v.tensor_tensor(g2[:, :], g1[:, :], eg[:, :], ALU.mult))
            ct.link(v.scalar_tensor_tensor(out=ybase[:, :], in0=excl[:, :], scalar=float(P), in1=region_of[:, :], op0=ALU.mult, op1=ALU.subtract))
            ct.link(v.tensor_tensor(ysel[:, :, :, :].rearrange("p b k e -> p (b k) e"), onehot[:, :, :, :].rearrange("p b k e -> p (b k) e"),
                                    ybase[:, :].unsqueeze(1).broadcast_to([P, 2 * B, E0]), ALU.mult))
            ct.link(v.tensor_reduce(yoff[:, :, :].rearrange("p b k -> p (b k)"), ysel[:, :, :, :].rearrange("p b k e -> p (b k) e"), AX_X, ALU.add))
            ct.link(v.tensor_tensor(yslotf[:, :, :], slotf[:, :, :], yoff[:, :, :], ALU.add))
            ct.link(v.tensor_copy(yslot[:, :], yslotf[:, :, :].rearrange("p b k -> p (b k)")))
            v.engine_nop().then_inc(yslot_ready, 1)
            dve.wait_ge(rows_in_ps, 1)
            v.tensor_copy(tile_rows[:, :], psX[:, 0:P]).then_inc(rows_ready, 1)
            dve.wait_ge(gT_in_ps, 1)
            ct.add(v.tensor_copy(gate1T[:, :], psZ[:, 0:E1]))
            ct.link(v.tensor_scalar(vB[:, :], onesb[0:A1, :], vcol[:, 0:1], None, ALU.mult))
            v.engine_nop().then_inc(gT_ready, 1)

            nl = dve.value_load(rounds[0:1, 0:1], min_val=MIN_TILES // RING - 1, max_val=MAX_TILES // RING - 1)

            def take_xT(j, r, first):
                dve.wait_ge(xT_in_ps, j + 1)
                if not first or j >= 2:
                    dve.wait_ge(hid_in_ps, C0 * (j - 1))
                v.tensor_copy(xT[r % 2][:, :], banks[4 + r % 2][:, 0:P]).then_inc(xT_ready, 1)
                e = dve.value_load(table_i[0:1, bass.ds(j, 1)], min_val=0, max_val=E0 - 1)
                if not first or j >= RING:
                    dve.wait_ge(gelu_done, C0 * (j - RING + 1))
                carry(dve)
                v.tensor_scalar(b1[r][:, :], b1_all[:, bass.ds(e, 1), :].rearrange("p o c -> p (o c)"), 1.0, None, ALU.mult).then_inc(b1_ready, 1)
                v.tensor_scalar(b2[r][:, :], b2_all[:, bass.ds(e, 1), :].rearrange("p o d -> p (o d)"), 1.0, None, ALU.mult).then_inc(b2_ready, 1)

            def take_y(j, r, n):
                dve.wait_ge(t_in_ps, j + 1)
                dve.wait_ge(b2_ready, j + 1)
                atleast(dve, y_out[r], 16 * n)
                v.tensor_tensor(yb[r][:, :], banks[6 + r % 2][:, 0:P], b2[r][:, :], ALU.add).then_inc(y_ready, 1)

            def round_of_tiles(n):
                first = known(n) and n == 0
                for r in ring:
                    j = RING * n + r
                    take_xT(j + 1, (r + 1) % RING, first)
                    if r > 0 or not first:
                        take_y(j - 1, (r - 1) % RING, n - 1 if r == 0 else n)

            dve.wait_ge(biases_in, 32)
            take_xT(0, 0, True)
            round_of_tiles(0)
            round_of_tiles(1)
            with dve.Fori(2, nl + 1) as n:
                round_of_tiles(n)
            take_y(nl * RING + (RING - 1), RING - 1, nl)

            pc, pd = banks[6], banks[7]
            cx = Chain(chain_x, 1000)

            def cond(k, stage):
                bp, ba = 7 * k, ACT_COND * k
                blk = slice(BLK * k, BLK * (k + 1))
                if stage == 0 and k > 0:
                    v.engine_nop().then_inc(c_dve, 1)
                if stage == 0 and k == 0:
                    dve.wait_ge(gathered[k % 2], 16 * 2 * BLK * (k // 2 + 1))
                    dve.wait_ge(xr_in[k % 2], 16 * (k // 2 + 1))
                    for t in range(BLK):
                        b = BLK * k + t
                        cx.add(v.scalar_tensor_tensor(out=mix1[:, t, :], in0=y1[k % 2][:, t, :], scalar=g1[:, b:b + 1], in1=xr[k % 2][:, t, :],
                                                      op0=ALU.mult, op1=ALU.add))
                    cx.join()
                    for t in range(BLK):
                        b = BLK * k + t
                        cx.add(v.scalar_tensor_tensor(out=mix2[:, t, :], in0=y2[k % 2][:, t, :], scalar=g2[:, b:b + 1], in1=mix1[:, t, :],
                                                      op0=ALU.mult, op1=ALU.add))
                    cx.join()
                    dve.wait_ge(a_ready, B)
                    v.tensor_tensor(x2[:, blk, :], mix2[:, :, :], a_all[:, blk, :], ALU.add).then_inc(x2_first, 1)
                    v.engine_nop().then_inc(c_dve, 1)
                if stage == 1:
                    dve.wait_ge(c_pe, bp + 3)
                    if k == 0:
                        dve.wait_ge(pool_const, ALL_CONSTS)
                    cx.link(v.tensor_tensor(ms[:, :, :], pc[:, :].rearrange("p (b l) -> p b l", b=BLK), poolbias[:, blk, :], ALU.add))
                    v.tensor_reduce(nm[:, :], ms[:, :, :], AX_X, ALU.max, negate=True).then_inc(c_dve, 1)
                if stage == 2:
                    dve.wait_ge(c_act, ba + 3)
                    cx.link(v.tensor_tensor(sc_[:, :], psum_[:, :], count[:, blk], ALU.mult))
                    cx.link(v.reciprocal(rs_[:, :], sc_[:, :]))
                    v.tensor_tensor(pn[:, :, :], pe_[:, :, :], rs_[:, :].unsqueeze(2).broadcast_to([P, BLK, P]), ALU.mult).then_inc(c_dve, 1)
                if stage == 3:
                    dve.wait_ge(c_pe, bp + 6)
                    cx.link(v.tensor_copy(l8[:, :, :].rearrange("p b e -> p (b e)"), pd[:, 0:BLK * E1]))
                    cx.link(v.tensor_reduce(nl8[:, :], l8[:, :, :], AX_X, ALU.max))
                    v.tensor_tensor(ls8[:, :, :], l8[:, :, :], nl8[:, :].unsqueeze(2).broadcast_to([P, BLK, E1]), ALU.subtract).then_inc(c_dve, 1)
                if stage == 4:
                    dve.wait_ge(c_act, ba + 6)
                    cx.link(v.tensor_reduce(z8[:, :], e8[:, :, :], AX_X, ALU.add))
                    cx.link(v.reciprocal(rz8[:, :], z8[:, :]))
                    cx.link(v.tensor_tensor(pr8[:, :, :], e8[:, :, :], rz8[:, :].unsqueeze(2).broadcast_to([P, BLK, E1]), ALU.mult))
                    for t in range(BLK):
                        cx.add(v.max(top1[:, t, :], pr8[:, t, :]))
                    cx.join()
                    for t in range(BLK):
                        cx.add(v.max_index(topi1[:, t, :], top1[:, t, :], pr8[:, t, :]))
                    cx.join()
                    cx.link(v.tensor_copy(topf1[:, :, :], topi1[:, :, 0:2]))
                    for s in range(2):
                        cx.add(v.tensor_tensor(oh1[:, :, s, :], iota_e[:, 0:E1].unsqueeze(1).broadcast_to([P, BLK, E1]),
                                               topf1[:, :, s:s + 1].broadcast_to([P, BLK, E1]), ALU.is_equal))
                    cx.add(v.tensor_tensor(s8[:, :], top1[:, :, 0:1].rearrange("p b o -> p (b o)"), top1[:, :, 1:2].rearrange("p b o -> p (b o)"), ALU.add))
                    cx.join()
                    cx.add(v.tensor_tensor(pick1[:, :, :], oh1[:, :, 0, :], oh1[:, :, 1, :], ALU.add))
                    cx.link(v.tensor_scalar(s8[:, :], s8[:, :], 1e-20, None, ALU.add))
                    cx.add(v.tensor_tensor(c8a[:, :, :], pick1[:, :, :], pr8[:, :, :], ALU.mult))
                    cx.link(v.reciprocal(r8[:, :], s8[:, :]))
                    cx.link(v.tensor_scalar(r8[:, :], r8[:, :], ROUTE_SCALE, None, ALU.mult))
                    cx.link(v.tensor_tensor(c8[:, :, :], c8a[:, :, :], r8[:, :].unsqueeze(2).broadcast_to([P, BLK, E1]), ALU.mult))
                    parts = [cparts[:, :, E1 * n:E1 * (n + 1)] for n in range(3)]
                    cx.link(v.tensor_copy(parts[0], c8[:, :, :]))
                    cx.link(v.tensor_tensor(c8r[:, :, :], c8[:, :, :], parts[0], ALU.subtract))
                    cx.link(v.tensor_copy(parts[1], c8r[:, :, :]))
                    cx.link(v.tensor_tensor(c8s[:, :, :], c8r[:, :, :], parts[1], ALU.subtract))
                    v.tensor_copy(parts[2], c8s[:, :, :]).then_inc(c_dve, 1)
                if stage == 5:
                    dve.wait_ge(c_pe, bp + 7)
                    atleast(dve, out_acc, k - 1)
                    v.tensor_copy(cT[k % 2][:, :], pc[:, :].bitcast(BF16)[0:3 * E1, 0:W]).then_inc(cond_ready, 1)

            def ffn(k):
                for c in range(NC1):
                    n = NC1 * k + c
                    m = P if c < NE else NSH[c - NE][1]
                    dve.wait_ge(silu_done, n + 1)
                    dve.wait_ge(gu_in_ps, n + 1)
                    atleast(dve, out_acc, k)
                    if c < NE:
                        atleast(dve, h_ready, n)
                        cf[0] += 1
                        v.tensor_tensor(hu[:, :], sg[n % 2][:, :], banks[2 + n % 2][:, :], ALU.mult).then_inc(chain_h, 1)
                        dve.wait_ge(chain_h, cf[0])
                        dve.wait_ge(wt_in_ps, NE * k + c + 1)
                        v.tensor_tensor(h1[:, c, :], hu[:, :], banks[4][:, :], ALU.mult).then_inc(h_ready, 1)
                    else:
                        v.tensor_tensor(h1[0:m, c, :], sg[n % 2][0:m, :], banks[2 + n % 2][0:m, :], ALU.mult).then_inc(h_ready, 1)
                    beside(cond, DVE_STAGES, c, k + 1)
                dve.wait_ge(out_acc, k + 1)
                if k >= 2:
                    dve.wait_ge(ob_out[k % 2], 16 * (k // 2))
                v.tensor_tensor(ob[k % 2][:, :, :], banks[5][:, :].rearrange("p (b d) -> p b d", b=BLK), x2[:, BLK * k:BLK * (k + 1), :],
                                ALU.add).then_inc(ob_ready, 1)

            cf = [0]
            for n in range(len(DVE_STAGES)):
                cond(0, n)
            for k in range(NB):
                ffn(k)


_INS = ['x', 'fside_BxSxS_0', 'itok_B_18_1004', 'itok_B_0_2', 'L0_cond_Wq', 'L0_cond_bq', 'L0_cond_Wk', 'L0_cond_bk', 'L0_cond_Wv',
        'L0_cond_bv', 'L0_cond_Wo', 'L0_cond_bo', 'L0_cond_b_prev', 'L0_cond_b_self', 'L0_ffn_gate_w', 'L0_ffn_gate_b', 'L0_ffn_w1',
        'L0_ffn_b1', 'L0_ffn_w2', 'L0_ffn_b2', 'L1_cond_W1', 'L1_cond_b1', 'L1_cond_v', 'L1_ffn_gate_w', 'L1_ffn_w_gate', 'L1_ffn_w_up',
        'L1_ffn_w_down', 'L1_ffn_sw_gate', 'L1_ffn_sw_up', 'L1_ffn_sw_down']


def kernel(**inputs):
    import numpy as _np
    import concourse.bacc as _bacc
    from concourse import mybir as _mybir
    from concourse.bass_utils import run_bass_kernel_spmd as _run

    nc = _bacc.Bacc("TRN2", target_bir_lowering=False, num_devices=1)
    arrays, aps = {}, {}
    for name in _INS:
        v = _np.ascontiguousarray(inputs[name])
        arrays[f"in_{name}_dram"] = v
        aps[name] = nc.dram_tensor(f"in_{name}_dram", v.shape, _mybir.dt.from_np(v.dtype), kind="ExternalInput").ap()
    out = nc.dram_tensor("out_0_dram", (B, P, P), F32, kind="ExternalOutput").ap()
    at = nc.dram_tensor("attention_output", (B, P, P), F32, kind="Internal").ap()
    ids = nc.dram_tensor("expert_tokens", (E0 * RUNS, P), F32, kind="Internal").ap()
    ys = nc.dram_tensor("expert_outputs", (YROWS, P), F32, kind="Internal").ap()
    attention_moe_kernel(nc, aps, out, at, ids, ys)
    r = _run(nc, [arrays], core_ids=[0])
    return r.results[0]["out_0_dram"]
```

```python
from contextlib import ExitStack

import concourse.bass as bass
from concourse import mybir

ALU = mybir.AluOpType
ACT = mybir.ActivationFunctionType
AX_X = mybir.AxisListType.X
F32 = mybir.dt.float32
BF16 = mybir.dt.bfloat16
I32 = mybir.dt.int32
U32 = mybir.dt.uint32

P = 128
B = 16
H = 16
DH = P // H
NG, NJ = 4, 4
SCALE = float(DH) ** -0.5
BIG = 1.0e30

E0, F0 = 24, 512
C0 = F0 // P
RUNS = B + 1
REGION = RUNS * P
RING = 4
PAD_TILES = RING - 1
ZERO_TILES = 12
MIN_TILES = B * P * 2 // P
MAX_TILES = B * P * 2 // P + E0 + PAD_TILES + 1
YROWS = MAX_TILES * P

E1, F1 = 8, 176
FS = 2 * F1
FE = E1 * F1
NE = FE // P
NSH = [(0, 128), (128, 128), (256, 96)]
NC1 = NE + len(NSH)
A1 = 32
ROUTE_SCALE = 2.5
BLK = 4
NB = B // BLK
W = BLK * P


def attention_moe_kernel(nc, a, out, at_dram, ids_dram, ys_dram):
    ctx = ExitStack()
    with ctx:
        def sb(name, shape, dt=F32):
            return ctx.enter_context(nc.sbuf_tensor(name, shape, dt))

        def bank(name):
            return ctx.enter_context(nc.psum_tensor(name, [P, 512], F32))

        def sem(name):
            return ctx.enter_context(nc.semaphore(name))

        banks = [bank(f"bank{i}") for i in range(8)]

        ident = sb("ident", [P, P])
        identb = sb("identb", [P, P], BF16)
        before = sb("before", [P, P], BF16)
        onesb = sb("onesb", [P, P], BF16)
        ind = sb("ind", [P, H])
        headmask = sb("headmask", [P, NJ])
        iota_e = sb("iota_e", [P, E0])
        iota_p = sb("iota_p", [P, 1])
        iota_k = sb("iota_k", [P, P])
        region_of = sb("region_of", [P, E0])
        lens_i = sb("lens_i", [P, B], I32)
        lens = sb("lens", [P, B])
        nolen = sb("nolen", [P, B])
        keymask = sb("keymask", [P, B])
        types_i = sb("types_i", [P, B], I32)
        types = sb("types", [P, B])
        is_pre = sb("is_pre", [P, B])
        is_post = sb("is_post", [P, B])
        is_cloze = sb("is_cloze", [P, B])
        count = sb("count", [P, B])
        tmp_b = sb("tmp_b", [P, B])
        tmp_c = sb("tmp_c", [P, B])
        prebias = sb("prebias", [P, P])
        postbias = sb("postbias", [P, P])
        clozebias = sb("clozebias", [P, P])
        poolbias = sb("poolbias", [P, B, P])
        h1 = sb("h1", [P, NC1, W])
        h1_flat = h1[:, :, :].rearrange("p c w -> p (c w)")
        term = h1_flat[:, 0:B * P].rearrange("p (b l) -> p b l", b=B)
        b2_all = h1_flat[:, B * P:(B + E0) * P].rearrange("p (e d) -> p e d", e=E0)
        b1_all = h1_flat[:, (B + E0) * P:(B + E0) * P + E0 * C0].rearrange("p (e c) -> p e c", e=E0)
        zrow = sb("zrow", [P, P])
        ones_e = sb("ones_e", [P, E0])
        expert_of = sb("expert_of", [3 * E1, FE], BF16)

        wq, wk, wv, wo = (sb(n, [P, P]) for n in ("wq", "wk", "wv", "wo"))
        cols = sb("cols", [P, 7])
        boB = sb("boB", [P, P])
        gate0 = sb("gate0", [P, E0])
        gate0bB = sb("gate0bB", [P, E0])
        cbias = sb("cbias", [P, 3])
        w1c = sb("w1c", [P, A1])
        vcol = sb("vcol", [A1, 1])
        vB = sb("vB", [A1, P])
        gate1 = sb("gate1", [E1, P])
        gate1T = sb("gate1T", [P, E1])
        wg1 = sb("wg1", [P, FE])
        wu1 = sb("wu1", [P, FE])
        wd1 = sb("wd1", [P, NE, P])
        wsg = sb("wsg", [P, FS])
        wsu = sb("wsu", [P, FS])
        wsd = sb("wsd", [P, len(NSH), P])

        xin = [sb(f"xin{i}", [P, P]) for i in range(2)]
        fin = [sb(f"fin{i}", [P, P]) for i in range(2)]
        xfT = [sb(f"xfT{i}", [P, 2 * P]) for i in range(2)]
        kT = [sb(f"kT{i}", [P, P]) for i in range(2)]
        kA = [sb(f"kA{i}", [P, P]) for i in range(2)]
        kd, kv, qb, prod = (sb(n, [P, P]) for n in ("kd", "kv", "qb", "prod"))
        qexp = [sb(f"qexp{i}", [P, H, P]) for i in range(2)]
        ones_h = sb("ones_h", [P, H, 1])
        v9 = [sb(f"v9{i}", [P, H, DH + 1]) for i in range(2)]
        vs = [sb(f"vs{i}", [P, P]) for i in range(2)]
        mx = sb("mx", [P, H])
        mm = sb("mm", [P, H])
        top = sb("top", [P, H])
        sm = sb("sm", [P, H])
        selfs = [sb(f"selfs{i}", [P, H]) for i in range(2)]
        y_token = sb("y_token", [P, 1])
        ws = [sb(f"ws{i}", [P, H]) for i in range(2)]
        ps = [sb(f"ps{i}", [P, NJ, P]) for i in range(2)]
        pT = [sb(f"pT{i}", [P, NJ * P]) for i in range(2)]
        den, rec = sb("den", [P, H]), sb("rec", [P, H])
        t1, t2 = sb("t1", [P, P]), sb("t2", [P, P])
        att = [sb(f"att{i}", [P, P]) for i in range(2)]
        attT = [sb(f"attT{i}", [P, P]) for i in range(2)]
        aT = [sb(f"aT{i}", [P, P]) for i in range(2)]
        a_all = sb("a_all", [P, B, P])

        lg = sb("lg", [P, E0])
        top8 = sb("top8", [P, 8])
        topi = sb("topi", [P, 8], U32)
        topf = sb("topf", [P, 2])
        picked = [sb(f"picked{i}", [P, E0], BF16) for i in range(2)]
        onehot = sb("onehot", [P, B, 2, E0])
        gap = sb("gap", [P, B])
        held = sb("held", [P, E0])
        rank = sb("rank", [P, E0])
        rsel = sb("rsel", [P, 2, E0])
        slotf = sb("slotf", [P, B, 2])
        slots = [sb(f"slots{i}", [P, 2], U32) for i in range(2)]
        gelu_warm = sb("gelu_warm", [P, 1])
        g1, g2, eg = sb("g1", [P, B]), sb("g2", [P, B]), sb("eg", [P, B])
        ntf = sb("ntf", [P, E0])
        nti = sb("nti", [P, E0], I32)
        incl, excl = sb("incl", [P, E0]), sb("excl", [P, E0])
        below, under = sb("below", [P, E0]), sb("under", [P, E0])
        ej, tj = sb("ej", [P, 1]), sb("tj", [P, 1])
        table = sb("table", [P, 2])
        table_i = sb("table_i", [1, P], I32)
        rounds_f = sb("rounds_f", [P, 1])
        rounds_i = sb("rounds_i", [P, 1], I32)
        rounds = sb("rounds", [P, 1], I32)
        tile_list = sb("tile_list", [P, 1], U32)
        tile_ids = sb("tile_ids", [P, P])
        tile_rows = sb("tile_rows", [P, P], U32)
        tok = [sb(f"tok{i}", [P, 1]) for i in range(2)]
        row_r = [sb(f"row_r{r}", [P, 1], U32) for r in range(RING)]
        ybase = sb("ybase", [P, E0])
        ysel = sb("ysel", [P, B, 2, E0])
        yoff = sb("yoff", [P, B, 2])
        yslotf = sb("yslotf", [P, B, 2])
        yslot = sb("yslot", [P, B * 2], U32)

        ring = range(RING)
        xt = [sb(f"xt{r}", [P, P]) for r in ring]
        w1 = [sb(f"w1_{r}", [P, F0]) for r in ring]
        w2 = [sb(f"w2_{r}", [P, C0, P]) for r in ring]
        b1 = [sb(f"b1_{r}", [P, C0]) for r in ring]
        b2 = [sb(f"b2_{r}", [P, P]) for r in ring]
        xT = [sb(f"xT{i}", [P, P]) for i in range(2)]
        hT = [sb(f"hT{i}", [P, C0, P]) for i in range(2)]
        yb = [sb(f"yb{r}", [P, P]) for r in ring]

        y1 = [qexp[0][:, BLK * i:BLK * (i + 1), :] for i in range(2)]
        y2 = [qexp[0][:, BLK * (2 + i):BLK * (3 + i), :] for i in range(2)]
        mix1, mix2, ms, pe_ = (qexp[1][:, BLK * i:BLK * (i + 1), :] for i in range(4))
        xr = [sb(f"xr{i}", [P, BLK, P]) for i in range(2)]
        mix1p, mix2p = (t[:, :].rearrange("p (b d) -> p b d", b=BLK) for t in w1[0:2])
        x2 = sb("x2", [P, B, P])
        x2T = sb("x2T", [P, W])
        th = sb("th", [A1, W])
        nm = sb("nm", [P, BLK])
        psum_ = sb("psum_", [P, BLK])
        sc_, rs_ = sb("sc_", [P, BLK]), sb("rs_", [P, BLK])
        pn = sb("pn", [P, BLK, P])
        pnT = sb("pnT", [P, W])
        plT = [sb(f"plT{i}", [P, W]) for i in range(2)]
        l8 = sb("l8", [P, BLK, E1])
        nl8 = sb("nl8", [P, BLK])
        ls8, e8, pr8 = (sb(n, [P, BLK, E1]) for n in ("ls8", "e8", "pr8"))
        z8, rz8 = sb("z8", [P, BLK]), sb("rz8", [P, BLK])
        top1 = sb("top1", [P, BLK, 8])
        topi1 = sb("topi1", [P, BLK, 8], U32)
        topf1 = sb("topf1", [P, BLK, 2])
        oh1 = sb("oh1", [P, BLK, 2, E1])
        pick1, c8a, c8 = (sb(n, [P, BLK, E1]) for n in ("pick1", "c8a", "c8"))
        s8, r8 = sb("s8", [P, BLK]), sb("r8", [P, BLK])
        c8r, c8s = sb("c8r", [P, BLK, E1]), sb("c8s", [P, BLK, E1])
        cparts = sb("cparts", [P, BLK, 3 * E1], BF16)
        cT = [sb(f"cT{i}", [3 * E1, W], BF16) for i in range(2)]
        sg = [sb(f"sg{i}", [P, W]) for i in range(2)]
        hu = sb("hu", [P, W])
        ob = [sb(f"ob{i}", [P, BLK, P]) for i in range(2)]

        w_att = sem("w_att")
        w_rest = sem("w_rest")
        w_l1 = sem("w_l1")
        pool_const = sem("pool_const")
        dve_const = sem("dve_const")
        cb_in_ps = sem("cb_in_ps")
        cb_ready = sem("cb_ready")
        gT_in_ps = sem("gT_in_ps")
        gT_ready = sem("gT_ready")
        s_in = [sem(f"s_in{i}") for i in range(2)]
        t_in_ps = sem("t_in_ps")
        a_in_ps = sem("a_in_ps")
        y_read = sem("y_read")
        z_read = sem("z_read")
        z_in_ps = sem("z_in_ps")
        x_read = sem("x_read")
        x_in_ps = sem("x_in_ps")
        xfT_ready = sem("xfT_ready")
        kqv_in_ps = sem("kqv_in_ps")
        kT_ready = sem("kT_ready")
        kv_ready = sem("kv_ready")
        kA_ready = sem("kA_ready")
        prod_ready = sem("prod_ready")
        qexp_pool = sem("qexp_pool")
        self_in_ps = sem("self_in_ps")
        self_read = sem("self_read")
        v_ready = sem("v_ready")
        shift_ready = sem("shift_ready")
        ws_ready = sem("ws_ready")
        sub_done = sem("sub_done")
        exp_done = sem("exp_done")
        pT_in_ps = sem("pT_in_ps")
        pT_ready = sem("pT_ready")
        pv_done = sem("pv_done")
        att_ready = sem("att_ready")
        att_in_ps = sem("att_in_ps")
        attT_ready = sem("attT_ready")
        aT_in_ps = sem("aT_in_ps")
        aT_ready = sem("aT_ready")
        a_ready = sem("a_ready")
        a_stored = sem("a_stored")
        tok_next = sem("tok_next")
        listed = sem("listed")
        logits_in_ps = sem("logits_in_ps")
        picks_ready = sem("picks_ready")
        rank_in_ps = sem("rank_in_ps")
        slots_ready = sem("slots_ready")
        scattered = sem("scattered")
        zeroed = sem("zeroed")
        rows_in = sem("rows_in")
        rows_in_ps = sem("rows_in_ps")
        rows_ready = sem("rows_ready")
        copied = sem("copied")
        xt_in = [sem(f"xt_in{r}") for r in range(RING)]
        chain_q = sem("chain_q")
        chain_n = sem("chain_n")
        chain_m = sem("chain_m")
        chain_l = sem("chain_l")
        chain_r = sem("chain_r")
        chain_t = sem("chain_t")
        chain_c = sem("chain_c")
        carried = sem("carried")
        chain_x = sem("chain_x")
        chain_h = sem("chain_h")
        table_ready = sem("table_ready")
        table_in_ps = sem("table_in_ps")
        plan_ready = sem("plan_ready")
        gap_exp = sem("gap_exp")
        yslot_ready = sem("yslot_ready")
        biases_in = sem("biases_in")
        b1_ready = sem("b1_ready")
        b2_ready = sem("b2_ready")
        tile_in = [sem(f"tile_in{r}") for r in ring]
        xT_in_ps = sem("xT_in_ps")
        xT_ready = sem("xT_ready")
        hid_in_ps = sem("hid_in_ps")
        gelu_done = sem("gelu_done")
        y_in_ps = sem("y_in_ps")
        y_ready = sem("y_ready")
        y_out = [sem(f"y_out{r}") for r in ring]
        gathered = [sem(f"gathered{i}") for i in range(2)]
        xr_in = [sem(f"xr_in{i}") for i in range(2)]
        x2_ready = sem("x2_ready")
        x2_first = sem("x2_first")
        mix_step = sem("mix_step")
        c_pe = sem("c_pe")
        c_act = sem("c_act")
        c_dve = sem("c_dve")
        cond_ready = sem("cond_ready")
        gu_in_ps = sem("gu_in_ps")
        wt_in_ps = sem("wt_in_ps")
        silu_done = sem("silu_done")
        h_ready = sem("h_ready")
        out_acc = sem("out_acc")
        ob_ready = sem("ob_ready")
        ob_out = [sem(f"ob_out{i}") for i in range(2)]

        psT = banks[0:2]
        psA = banks[2:4]
        psY, psZ, psX, psO = banks[4:8]
        ps_ks, ps_q, ps_v, ps_vs = (psY[:, i * P:(i + 1) * P] for i in range(4))
        ps_a, ps_rank, ps_tot = psY[:, 0:128], psY[:, 128:152], psY[:, 152:176]
        ps_lg = psY[:, 176:200]
        ps_k, ps_aT = psZ[:, 0:P], psZ[:, P:2 * P]
        ps_xf, ps_att = psX[:, 0:256], psX[:, 256:384]
        ps_self = psX[:, 384:400]

        FIRST_CONSTS = 8
        CONSTS = 18
        ALL_CONSTS = CONSTS + 10
        CHAIN_TYPES = 9
        STEPS = B + 3
        ACT_COND, DVE_COND = 6, 5
        LEAD = 6

        def pipeline(eng, step):
            for i in range(LEAD):
                step(i, i % 2, i // 2)
            with eng.Fori(LEAD // 2, B // 2) as n:
                for p in range(2):
                    step(2 * n + p, p, n)
            for i in range(B, STEPS):
                step(i, i % 2, i // 2)

        def known(i):
            return type(i) is int

        def active(i, lag):
            return not known(i) or 0 <= i - lag < B

        def upto(v):
            return min(v, B) if known(v) else v

        def atleast(eng, s, v):
            if not known(v) or v > 0:
                eng.wait_ge(s, v)

        def mixed(eng, k):
            eng.wait_ge(x2_ready if k > 0 else x2_first, max(k, 1))

        def carry(eng):
            eng.sem_inc(carried, 1)

        PE_STAGES = (0, 1, 2, 5, 6, 7, 12)
        ACT_STAGES = (0, 1, 3, 5, 6, 8)
        DVE_STAGES = (0, 2, 4, 7, 9, 10, 11, 12)

        def beside(cond, stages, c, k):
            for n, at in enumerate(stages):
                if at == c and k < NB:
                    cond(k, n)

        block = ctx.enter_context(nc.Block())

        @block.sync
        def _(sp):
            def load(i, p, n):
                if known(i) and i >= B:
                    return
                if not known(i) or i >= 2:
                    sp.wait_ge(x_in_ps, i - 1)
                sp.dma_start(xin[p][:, :], a["x"][bass.ds(i, 1)].rearrange("o t d -> (o t) d")).then_inc(s_in[p], 16)
                sp.dma_start(fin[p][:, :], a["fside_BxSxS_0"][bass.ds(i, 1)].rearrange("o t d -> (o t) d")).then_inc(s_in[p], 16)

            load(0, 0, 0)
            for dst, name in ((wq, "Wq"), (wk, "Wk")):
                sp.dma_start(dst[:, :], a[f"L0_cond_{name}"]).then_inc(w_att, 16)
            for n, ap in enumerate((a["L0_cond_b_prev"].rearrange("a b d -> d (a b)"),
                                    a["L0_cond_b_self"].rearrange("a b d -> d (a b)"),
                                    a["L0_cond_bk"].unsqueeze(1), a["L0_cond_bq"].unsqueeze(1))):
                sp.dma_start(cols[:, n:n + 1], ap).then_inc(w_att, 16)
            sp.dma_start(lens_i[:, :], a["itok_B_18_1004"].unsqueeze(0).broadcast_to([P, B])).then_inc(w_att, 16)
            sp.dma_start(wv[:, :], a["L0_cond_Wv"]).then_inc(w_att, 16)
            load(1, 1, 0)
            sp.dma_start(types_i[:, :], a["itok_B_0_2"].unsqueeze(0).broadcast_to([P, B])).then_inc(w_rest, 16)
            sp.dma_start(wo[:, :], a["L0_cond_Wo"]).then_inc(w_rest, 16)
            sp.dma_start(cols[:, 6:7], a["L0_cond_bv"].unsqueeze(1)).then_inc(w_rest, 16)
            sp.dma_start(cols[:, 4:5], a["L0_cond_bo"].unsqueeze(1)).then_inc(w_rest, 16)
            sp.dma_start(cols[0:A1, 5:6], a["L1_cond_b1"].unsqueeze(1)).then_inc(w_rest, 16)
            for dst, ap, n in ((boB, a["L0_cond_bo"], P), (gate0bB, a["L0_ffn_gate_b"], E0)):
                sp.dma_start(dst[:, :], ap.unsqueeze(0).broadcast_to([P, n])).then_inc(w_rest, 16)
            sp.dma_start(gate0[:, :], a["L0_ffn_gate_w"]).then_inc(w_rest, 16)
            sp.wait_ge(pool_const, FIRST_CONSTS)
            for part in range(RUNS * E0 // (P // 2)):
                sp.dma_start(ids_dram[(P // 2) * part:(P // 2) * (part + 1), :], zrow[0:P // 2, :]).then_inc(listed, 16)
            sp.dma_start(ids_dram[(P // 2) * (part + 1):, :], zrow[0:RUNS * E0 % (P // 2), :]).then_inc(listed, 16)
            for i in range(2, LEAD):
                load(i, i % 2, i // 2)
            sp.dma_start(w1c[:, :], a["L1_cond_W1"]).then_inc(w_l1, 16)
            sp.dma_start(vcol[:, :], a["L1_cond_v"].unsqueeze(1)).then_inc(w_l1, 16)
            sp.dma_start(gate1[:, :], a["L1_ffn_gate_w"]).then_inc(w_l1, 16)
            sp.dma_start(wg1[:, :].rearrange("d (e f) -> d e f", e=E1), a["L1_ffn_w_gate"].rearrange("e d f -> d e f")).then_inc(w_l1, 16)
            sp.dma_start(wu1[:, :].rearrange("d (e f) -> d e f", e=E1), a["L1_ffn_w_up"].rearrange("e d f -> d e f")).then_inc(w_l1, 16)
            sp.dma_start(wd1[:, :, :], a["L1_ffn_w_down"].rearrange("e f d -> (e f) d").rearrange("(c p) d -> p c d", p=P)).then_inc(w_l1, 16)
            sp.dma_start(wsg[:, :], a["L1_ffn_sw_gate"]).then_inc(w_l1, 16)
            sp.dma_start(wsu[:, :], a["L1_ffn_sw_up"]).then_inc(w_l1, 16)
            for c, (f, m) in enumerate(NSH):
                sp.dma_start(wsd[0:m, c, :], a["L1_ffn_sw_down"][f:f + m, :]).then_inc(w_l1, 16)
            def store(i):
                sp.wait_ge(a_ready, i - 2)
                sp.dma_start(at_dram[bass.ds(i - 3, 1)].rearrange("o t d -> (o t) d"),
                             a_all[:, bass.ds(i - 3, 1), :].rearrange("p o d -> p (o d)")).then_inc(a_stored, 16)

            for i in range(3, LEAD):
                store(i)
            sp.dma_start(b1_all, a["L0_ffn_b1"].rearrange("e (p c) -> p e c", c=C0)).then_inc(biases_in, 16)
            sp.dma_start(b2_all, a["L0_ffn_b2"].unsqueeze(0).broadcast_to([P, E0, P])).then_inc(biases_in, 16)
            with sp.Fori(LEAD // 2, B // 2) as n:
                for p in range(2):
                    load(2 * n + p, p, n)
                    store(2 * n + p)
            ys_t = ys_dram.rearrange("(j p) d -> p j d", p=P)
            for i in range(B, STEPS):
                store(i)
                for j in range((i - B) * ZERO_TILES, MAX_TILES, (STEPS - B) * ZERO_TILES):
                    sp.dma_start(ys_t[:, j:j + ZERO_TILES, :], zrow[:, :].unsqueeze(1).broadcast_to([P, ZERO_TILES, P])).then_inc(zeroed, 16)
            sp.wait_ge(plan_ready, 1)
            nl = sp.value_load(rounds[0:1, 0:1], min_val=MIN_TILES // RING - 1, max_val=MAX_TILES // RING - 1)
            w1_d, w2_d = a["L0_ffn_w1"], a["L0_ffn_w2"].rearrange("e (p c) d -> e p c d", c=C0)

            def load_tile(j, r, wait):
                if wait is not None:
                    sp.wait_ge(y_ready, wait)
                e = sp.value_load(table_i[0:1, bass.ds(j, 1)], min_val=0, max_val=E0 - 1)
                sp.dma_start(w1[r][:, :], w1_d[bass.ds(e, 1)].rearrange("o d f -> (o d) f")).then_inc(tile_in[r], 16)
                sp.dma_start(w2[r][:, :, :], w2_d[bass.ds(e, 1)].rearrange("o p c d -> (o p) c d")).then_inc(tile_in[r], 16)

            for r in ring:
                load_tile(r, r, None)
            with sp.Fori(1, nl + 1) as n:
                for r in ring:
                    load_tile(RING * n + r, r, RING * n + (r - RING + 1))
            for k in range(NB):
                if k >= 2:
                    mixed(sp, k - 2)
                sp.dma_start(xr[k % 2][:, :, :], a["x"][BLK * k:BLK * (k + 1)].rearrange("b t d -> t b d")).then_inc(xr_in[k % 2], 16)
            for k in range(NB):
                sp.wait_ge(ob_ready, k + 1)
                sp.dma_start(out[BLK * k:BLK * (k + 1)].rearrange("b t d -> t b d"), ob[k % 2][:, :, :]).then_inc(ob_out[k % 2], 16)
            for p in range(2):
                sp.wait_ge(ob_out[p], 16 * (NB // 2))

        @block.gpsimd
        def _(pool):
            g = nc.gpsimd

            def select(t, op, pattern, base, mult, fill):
                return g.affine_select(out=t, in_=t, compare_op=op, fill=fill, base=base, pattern=pattern,
                                       channel_multiplier=mult)

            steps = [0]

            def done(ins):
                steps[0] += 1
                ins.then_inc(pool_const, 1)
                pool.wait_ge(pool_const, steps[0])

            done(g.memset(ident[:, :], 0.0))
            done(select(ident[:, :], ALU.not_equal, [[-1, P]], 0, 1, 1.0))
            done(g.memset(ind[:, :], SCALE))
            done(select(ind[:, :], ALU.is_ge, [[-DH, H]], 0, 1, 0.0))
            done(select(ind[:, :], ALU.is_ge, [[DH, H]], DH - 1, -1, 0.0))
            done(g.iota(iota_p[:, :], pattern=[[0, 1]], base=0, channel_multiplier=1, allow_small_or_imprecise_dtypes=True))
            done(g.iota(iota_k[:, :], pattern=[[1, P]], base=0, channel_multiplier=0, allow_small_or_imprecise_dtypes=True))
            done(g.memset(zrow[:, :], 0.0))
            assert steps[0] == FIRST_CONSTS
            done(g.tensor_copy(identb[:, :], ident[:, :]))
            done(g.memset(onesb[:, :], 1.0))
            done(g.memset(before[:, :], 1.0))
            done(select(before[:, :], ALU.is_gt, [[1, P]], 0, -1, 0.0))
            done(g.iota(iota_e[:, :], pattern=[[1, E0]], base=0, channel_multiplier=0, allow_small_or_imprecise_dtypes=True))
            done(g.iota(region_of[:, :], pattern=[[REGION, E0]], base=0, channel_multiplier=0, allow_small_or_imprecise_dtypes=True))
            done(g.memset(held[:, :], 0.0))
            done(g.memset(ones_e[:, :], 1.0))
            for i in range(2):
                done(g.iota(tok[i][:, :], pattern=[[0, 1]], base=i * P, channel_multiplier=1, allow_small_or_imprecise_dtypes=True))
            assert steps[0] == CONSTS

            def second_layer_constants(i):
                if i == 0:
                    done(g.memset(prebias[:, :], 0.0))
                    done(select(prebias[:, :], ALU.is_ge, [[-1, P]], 0, 1, -BIG))
                    done(g.memset(postbias[:, :], 0.0))
                    done(select(postbias[:, :], ALU.is_ge, [[1, P]], 0, -1, -BIG))
                    done(g.memset(clozebias[:, :], 0.0))
                    done(select(clozebias[:, :], ALU.not_equal, [[-1, P]], 0, 1, -BIG))
                if i == 1:
                    done(g.memset(expert_of[:, :], 0.0))
                    for part in range(3):
                        v = expert_of[:, :].rearrange("p (e f) -> p e f", e=E1)
                        done(select(v, ALU.not_equal, [[-1, E1], [0, F1]], -E1 * part, 1, 1.0))
                    assert steps[0] == ALL_CONSTS

            def expand(i, p):
                if not active(i, 0):
                    return
                if known(i) and i == 0:
                    pool.wait_ge(dve_const, 2)
                pool.wait_ge(chain_q, 2 * i + 1)
                atleast(pool, a_in_ps, 4 * (i - 1))
                for g_ in range(NG):
                    rows = slice(32 * g_, 32 * g_ + 32)
                    g.tensor_tensor(qexp[p][rows, NJ * g_:NJ * (g_ + 1), :], qb[rows, :].unsqueeze(1).broadcast_to([32, NJ, P]),
                                    headmask[rows, :].unsqueeze(2).broadcast_to([32, NJ, P]), ALU.mult).then_inc(qexp_pool, 1)
                    pool.wait_ge(qexp_pool, 4 * i + (g_ + 1))

            def dispatch(i, p, n):
                expand(i, p)
                if known(i):
                    second_layer_constants(i)
                if not active(i, 3):
                    return
                pool.wait_ge(slots_ready, i - 2)
                if known(i) and i == 3:
                    pool.wait_ge(listed, 16 * (RUNS * E0 // (P // 2) + 1))
                carry(pool)
                for k in range(2):
                    g.indirect_dma_start(ids_dram.rearrange("r (t o) -> (r t) o", o=1), bass.IndirectOffsetOnAxis(ap=slots[1 - p][:, k:k + 1], axis=0),
                                         tok[1 - p][:, :], None).then_inc(scattered, 16)
                pool.wait_ge(scattered, 32 * (i - 2))
                carry(pool)
                g.tensor_scalar(tok[1 - p][:, :], tok[1 - p][:, :], float(2 * P), None, ALU.add).then_inc(tok_next, 1)
                pool.wait_ge(tok_next, i - 2)

            pipeline(pool, dispatch)

            pool.wait_ge(plan_ready, 1)
            pool.wait_ge(scattered, 32 * B)
            g.indirect_dma_start(tile_ids[:, :], None, ids_dram,
                                 bass.IndirectOffsetOnAxis(ap=tile_list[:, 0:1], axis=0)).then_inc(rows_in, 16)

            def gather_tile(j, r, wait):
                if wait is not None:
                    pool.wait_ge(xT_in_ps, wait)
                g.tensor_copy(row_r[r][:, :], tile_rows[:, bass.ds(j, 1)]).then_inc(copied, 1)
                pool.wait_ge(copied, j + 1)
                carry(pool)
                g.indirect_dma_start(xt[r][:, :], None, at_dram.rearrange("b t d -> (b t) d"),
                                     bass.IndirectOffsetOnAxis(ap=row_r[r][:, 0:1], axis=0)).then_inc(xt_in[r], 16)

            pool.wait_ge(rows_ready, 1)
            pool.wait_ge(a_stored, 16 * B)
            for r in ring:
                gather_tile(r, r, None)
            nl = pool.value_load(rounds[0:1, 0:1], min_val=MIN_TILES // RING - 1, max_val=MAX_TILES // RING - 1)
            with pool.Fori(1, nl + 1) as n:
                for r in ring:
                    gather_tile(RING * n + r, r, RING * n + (r - RING + 1))
            gather_tile(RING * nl + RING, 0, RING * nl + 1)

            for r in ring:
                pool.wait_ge(y_out[r], 16)
            pool.wait_ge(yslot_ready, 1)
            for r in ring:
                pool.wait_ge(y_out[r], nl * 16 + 16)
            carry(pool)
            for k in range(NB):
                if k >= 2:
                    mixed(pool, k - 2)
                for t in range(BLK):
                    for s, y in ((0, y1), (1, y2)):
                        n = 2 * (BLK * k + t) + s
                        g.indirect_dma_start(y[k % 2][:, t, :], None, ys_dram,
                                             bass.IndirectOffsetOnAxis(ap=yslot[:, n:n + 1], axis=0)).then_inc(gathered[k % 2], 16)
                if k > 0:
                    blk = slice(BLK * k, BLK * (k + 1))
                    pool.wait_ge(gathered[k % 2], 16 * 2 * BLK * (k // 2 + 1))
                    pool.wait_ge(xr_in[k % 2], 16 * (k // 2 + 1))
                    pool.wait_ge(a_ready, B)
                    gates = lambda t: t[:, blk].unsqueeze(2).broadcast_to([P, BLK, P])
                    for n, (o, x, y, op) in enumerate(((mix1p, y1[k % 2], gates(g1), ALU.mult), (mix2p, y2[k % 2], gates(g2), ALU.mult),
                                                       (mix1p, mix1p, xr[k % 2][:, :, :], ALU.add), (mix2p, mix2p, a_all[:, blk, :], ALU.add))):
                        g.tensor_tensor(o, x, y, op).then_inc(mix_step, 1)
                        pool.wait_ge(mix_step, 4 * (k - 1) + n + 1)
                    g.tensor_tensor(x2[:, blk, :], mix1p, mix2p, ALU.add).then_inc(x2_ready, 1)
                    pool.wait_ge(x2_ready, k)

        @block.tensor
        def _(pe):
            pe.wait_ge(w_att, 16 * 8)
            pe.wait_ge(pool_const, FIRST_CONSTS)
            for n, (w, c) in enumerate(((wk, 0), (wk, 1), (wq, 1))):
                mm_ = pe.matmul(psY[:, n:n + 1], w[:, :], cols[:, c:c + 1], start=True, stop=True)
            mm_.then_inc(cb_in_ps, 1)

            def scores(i, p, g):
                if not active(i, 1):
                    return
                if g == 0:
                    pe.wait_ge(kA_ready, i)
                pe.wait_ge(qexp_pool, 4 * (i - 1) + (g + 1))
                atleast(pe, sub_done, 4 * (i - 1) + (g - 1))
                for j in range(NJ):
                    m = pe.matmul(psA[g % 2][:, j * P:(j + 1) * P], qexp[1 - p][:, NJ * g + j, :], kA[1 - p][:, :], start=True, stop=True)
                m.then_inc(a_in_ps, 1)

            def turned_weights(i, p, g):
                if not active(i, 1):
                    return
                pe.wait_ge(exp_done, 4 * (i - 1) + (g + 1))
                atleast(pe, pT_ready, 4 * (i - 1) + (g - 1))
                for j in range(NJ):
                    m = pe.transpose(psT[g % 2][:, j * P:(j + 1) * P], ps[g % 2][:, j, :], ident[:, :])
                m.then_inc(pT_in_ps, 1)

            def weighted_values(i, p, g):
                if not active(i, 1):
                    return
                pe.wait_ge(pT_ready, 4 * (i - 1) + (g + 1))
                if g == 0:
                    atleast(pe, att_ready, i - 1)
                for j in range(NJ):
                    h = NJ * g + j
                    m = pe.matmul(psO[:, h * (DH + 1):(h + 1) * (DH + 1)], pT[g % 2][:, j * P:(j + 1) * P],
                                  v9[1 - p][:, h, :], start=True, stop=True)
                m.then_inc(pv_done, 1)

            def step(i, p, n):
                if known(i) and i == 2:
                    pe.wait_ge(w_rest, 16 * 8)
                if known(i) and i == 3:
                    pe.wait_ge(pool_const, CONSTS)
                scores(i, p, 0)
                if active(i, 0) or active(i, 2):
                    atleast(pe, self_read, upto(i))
                    if active(i, 0):
                        pe.wait_ge(s_in[p], 32 * (n + 1))
                        m = pe.transpose(ps_xf[:, 0:P], xin[p][:, :], ident[:, :])
                        m = pe.transpose(ps_xf[:, P:2 * P], fin[p][:, :], ident[:, :])
                    if active(i, 2):
                        pe.wait_ge(att_ready, i - 1)
                        m = pe.transpose(ps_att, att[p][:, :], ident[:, :])
                    m.then_inc(x_in_ps, 1)
                scores(i, p, 1)
                if active(i, 2):
                    pe.wait_ge(x_read, i + 1)
                    pe.wait_ge(z_read, upto(i))
                    pe.matmul(ps_aT, wo[:, :], attT[p][:, :], start=True, stop=True).then_inc(aT_in_ps, 1)
                turned_weights(i, p, 0)
                if active(i, 2) or active(i, 3):
                    pe.wait_ge(v_ready, upto(i))
                    atleast(pe, y_read, i - 2)
                    if active(i, 2):
                        pe.wait_ge(aT_ready, i - 1)
                        m = pe.matmul(ps_a, attT[p][:, :], wo[:, :], start=True, stop=True)
                        m = pe.matmul(ps_lg, aT[p][:, :], gate0[:, :], start=True, stop=True)
                    if active(i, 3):
                        pe.wait_ge(picks_ready, i - 2)
                        pe.matmul(ps_rank, before[:, :], picked[1 - p][:, :], start=True, stop=True)
                        m = pe.matmul(ps_tot, onesb[:, :], picked[1 - p][:, :], start=True, stop=True)
                    m.then_inc(y_in_ps, 1)
                scores(i, p, 2)
                weighted_values(i, p, 0)
                turned_weights(i, p, 1)
                scores(i, p, 3)
                weighted_values(i, p, 1)
                turned_weights(i, p, 2)
                if active(i, 0):
                    if known(i) and i == 0:
                        pe.wait_ge(cb_ready, 1)
                    pe.wait_ge(x_read, i + 1)
                    if known(i) and i == 1:
                        pe.wait_ge(v_ready, i)
                        pe.wait_ge(z_read, i)
                    atleast(pe, y_read, i - 1)
                    pe.matmul(ps_q, wq[:, :], xfT[p][:, P:2 * P], start=True, stop=True)
                    pe.matmul(ps_ks, wk[:, :], xfT[p][:, P:2 * P], start=True, stop=True)
                    pe.matmul(ps_v, xfT[p][:, 0:P], wv[:, :], start=True, stop=True)
                    pe.matmul(ps_vs, xfT[p][:, P:2 * P], wv[:, :], start=True, stop=True).then_inc(kqv_in_ps, 1)
                    atleast(pe, aT_ready, i - 1)
                    pe.matmul(ps_k, wk[:, :], xfT[p][:, 0:P], start=True, stop=True).then_inc(z_in_ps, 1)
                turned_weights(i, p, 3)
                weighted_values(i, p, 2)
                if active(i, 0):
                    pe.wait_ge(prod_ready, i + 1)
                    pe.matmul(ps_self, prod[:, :], ind[:, :], start=True, stop=True).then_inc(self_in_ps, 1)
                weighted_values(i, p, 3)

            pipeline(pe, step)

            pe.wait_ge(table_ready, 1)
            pe.wait_ge(y_read, STEPS - 2)
            pe.transpose(psY[0:1, 0:P], table[:, 0:1], ident[:, :]).then_inc(table_in_ps, 1)
            pe.wait_ge(x_read, STEPS - 1)
            pe.wait_ge(rows_in, 16)
            pe.transpose(psX[:, 0:P], tile_ids[:, :], ident[:, :]).then_inc(rows_in_ps, 1)
            pe.wait_ge(w_l1, 16 * 11)
            pe.transpose(psZ[:, 0:E1], gate1[:, :], ident[0:E1, 0:E1]).then_inc(gT_in_ps, 1)
            pe.wait_ge(plan_ready, 1)
            nl = pe.value_load(rounds[0:1, 0:1], min_val=MIN_TILES // RING - 1, max_val=MAX_TILES // RING - 1)

            def transpose_tile(j, r, n):
                pe.wait_ge(xt_in[r], 16 * (n + 1))
                pe.transpose(banks[4 + r % 2][:, 0:P], xt[r][:, :], ident[:, :]).then_inc(xT_in_ps, 1)

            def up(j, r, n, first):
                pe.wait_ge(tile_in[r], 32 * (n + 1))
                pe.wait_ge(xT_ready, j + 1)
                for c in range(C0):
                    if not first or r > 0:
                        pe.wait_ge(gelu_done, C0 * (j - 1) + (c + 1))
                    pe.matmul(banks[c][:, 0:P], w1[r][:, :].rearrange("d (f c) -> d c f", c=C0)[:, c, :],
                              xT[r % 2][:, :], start=True, stop=True).then_inc(hid_in_ps, 1)

            def down(j, r):
                for c in range(C0):
                    pe.wait_ge(gelu_done, C0 * j + (c + 1))
                    m = pe.matmul(banks[6 + r % 2][:, 0:P], hT[r % 2][:, c, :], w2[r][:, c, :], start=(c == 0), stop=(c == C0 - 1))
                m.then_inc(t_in_ps, 1)

            def round_of_tiles(n, first):
                for r in ring:
                    j = RING * n + r
                    up(j, r, n, first)
                    transpose_tile(j + 1, (r + 1) % RING, n + (r + 1) // RING)
                    if r > 0 or not first:
                        if not first or r >= 3:
                            pe.wait_ge(y_ready, j - 2)
                        down(j - 1, (r - 1) % RING)

            transpose_tile(0, 0, 0)
            round_of_tiles(0, True)
            with pe.Fori(1, nl + 1) as n:
                round_of_tiles(n, False)
            pe.wait_ge(y_ready, nl * RING + (RING - 2))
            down(nl * RING + (RING - 1), RING - 1)

            pc, pd = banks[6], banks[7]
            steps = [0]

            def signal(ins):
                steps[0] += 1
                ins.then_inc(c_pe, 1)

            def cond(k, stage):
                base_a, base_d = ACT_COND * k, DVE_COND * k
                if stage == 0:
                    mixed(pe, k)
                    for t in range(BLK):
                        m = pe.transpose(pc[:, t * P:(t + 1) * P], x2[:, BLK * k + t, :], ident[:, :])
                    signal(m)
                if stage == 1:
                    pe.wait_ge(c_act, base_a + 1)
                    signal(pe.matmul(pd[0:A1, :], w1c[:, :], x2T[:, :], start=True, stop=True))
                if stage == 2:
                    pe.wait_ge(c_act, base_a + 2)
                    signal(pe.matmul(pc[:, :], vB[:, :], th[:, :], start=True, stop=True))
                if stage == 3:
                    pe.wait_ge(c_dve, base_d + 3)
                    for t in range(BLK):
                        m = pe.transpose(pd[:, t * P:(t + 1) * P], pn[:, t, :], ident[:, :])
                    signal(m)
                if stage == 4:
                    pe.wait_ge(c_act, base_a + 4)
                    for t in range(BLK):
                        m = pe.matmul(pc[:, t * P:(t + 1) * P], x2[:, BLK * k + t, :], pnT[:, t * P:(t + 1) * P], start=True, stop=True)
                    signal(m)
                if stage == 5:
                    pe.wait_ge(c_act, base_a + 5)
                    for t in range(BLK):
                        m = pe.matmul(pd[:, t * E1:(t + 1) * E1], plT[k % 2][:, t * P:(t + 1) * P], gate1T[:, :], start=True, stop=True)
                    signal(m)
                if stage == 6:
                    pe.wait_ge(c_dve, base_d + 5)
                    for t in range(BLK):
                        m = pe.transpose(pc[:, :].bitcast(BF16)[0:3 * E1, t * P:(t + 1) * P], cparts[:, t, :], identb[:, :])
                    signal(m)

            def ffn(k):
                x = plT[k % 2]
                pe.wait_ge(cond_ready, k + 1)
                if k == 0:
                    pe.wait_ge(pool_const, ALL_CONSTS)
                for c in range(NC1):
                    n = NC1 * k + c
                    f, m = (c * P, P) if c < NE else NSH[c - NE]
                    wg, wu = (wg1, wu1) if c < NE else (wsg, wsu)
                    atleast(pe, h_ready, n - 1)
                    pe.matmul(banks[n % 2][0:m, :], wg[:, f:f + m], x[:, :], start=True, stop=True)
                    pe.matmul(banks[2 + n % 2][0:m, :], wu[:, f:f + m], x[:, :], start=True, stop=True).then_inc(gu_in_ps, 1)
                    if c < NE:
                        atleast(pe, h_ready, n)
                        pe.matmul(banks[4][:, :], expert_of[:, f:f + P], cT[k % 2][:, :], start=True, stop=True).then_inc(wt_in_ps, 1)
                    beside(cond, PE_STAGES, c, k + 1)
                atleast(pe, ob_ready, k)
                for t in range(BLK):
                    pe.wait_ge(h_ready, NC1 * (k + 1))
                    for c in range(NC1):
                        m = P if c < NE else NSH[c - NE][1]
                        wd = wd1[:, c, :] if c < NE else wsd[0:m, c - NE, :]
                        y = pe.matmul(banks[5][:, t * P:(t + 1) * P], h1[0:m, c, t * P:(t + 1) * P], wd, start=(c == 0), stop=(c == NC1 - 1))
                y.then_inc(out_acc, 1)

            pe.wait_ge(gT_ready, 1)
            pe.wait_ge(y_ready, nl * RING + RING)
            for n in range(len(PE_STAGES)):
                cond(0, n)
            for k in range(NB):
                ffn(k)

        @block.scalar
        def _(act):
            s = nc.scalar

            def weights(i, p, g):
                if not active(i, 1):
                    return
                act.wait_ge(sub_done, 4 * (i - 1) + (g + 1))
                s.activation(ps[g % 2][:, :, :], ps[g % 2][:, :, :], ACT.Exp).then_inc(exp_done, 1)

            def keep_turned(i, p, g):
                if not active(i, 1):
                    return
                act.wait_ge(pT_in_ps, 4 * (i - 1) + (g + 1))
                atleast(act, pv_done, 4 * (i - 1) + (g - 1))
                s.activation(pT[g % 2][:, :], psT[g % 2][:, :], ACT.Identity).then_inc(pT_ready, 1)

            def step(i, p, n):
                if active(i, 0) or active(i, 2):
                    act.wait_ge(x_in_ps, i + 1)
                    if active(i, 0):
                        atleast(act, kqv_in_ps, i - 1)
                        atleast(act, z_in_ps, i - 1)
                        m = s.activation(xfT[p][:, :], ps_xf, ACT.Identity)
                    if known(i) and i == 2:
                        act.wait_ge(w_rest, 16 * 8)
                    if active(i, 2):
                        atleast(act, y_in_ps, i - 3)
                        m = s.activation(attT[p][:, :], ps_att, ACT.Identity, bias=cols[:, 6:7])
                    m.then_inc(x_read, 1)
                weights(i, p, 0)
                if active(i, 2):
                    act.wait_ge(aT_in_ps, i - 1)
                    s.activation(aT[p][:, :], ps_aT, ACT.Identity, bias=cols[:, 4:5]).then_inc(aT_ready, 1)
                keep_turned(i, p, 0)
                weights(i, p, 1)
                keep_turned(i, p, 1)
                weights(i, p, 2)
                keep_turned(i, p, 2)
                weights(i, p, 3)
                if active(i, 0):
                    if known(i) and i == 0:
                        act.wait_ge(cb_ready, 1)
                    act.wait_ge(z_in_ps, i + 1)
                    atleast(act, kv_ready, i - 1)
                    s.activation(kT[p][:, :], ps_k, ACT.Identity, bias=cbias[:, 0:1]).then_inc(z_read, 1)
                if active(i, 1):
                    act.wait_ge(shift_ready, i)
                    atleast(act, att_ready, i - 2)
                    s.activation(ws[1 - p][:, :], sm[:, :], ACT.Exp).then_inc(ws_ready, 1)
                keep_turned(i, p, 3)
                if active(i, 0):
                    act.wait_ge(kv_ready, i + 1)
                    act.wait_ge(z_read, i + 1)
                    atleast(act, a_in_ps, 4 * (i - 1))
                    s.activation(kA[p][:, :], kv[:, :], ACT.Identity, bias=kT[p][:, 0:1]).then_inc(kA_ready, 1)

            pipeline(act, step)

            act.wait_ge(chain_l, 6 * B)
            s.activation(eg[:, :], gap[:, :], ACT.Exp).then_inc(gap_exp, 1)
            act.wait_ge(gap_exp, 1)
            s.activation(gelu_warm[:, :], eg[:, 0:1], ACT.Gelu)
            act.wait_ge(plan_ready, 1)
            nl = act.value_load(rounds[0:1, 0:1], min_val=MIN_TILES // RING - 1, max_val=MAX_TILES // RING - 1)
            ys_t = ys_dram.rearrange("(j p) d -> j p d", p=P)
            act.wait_ge(zeroed, 16 * (MAX_TILES // ZERO_TILES))

            def send(j, r):
                act.wait_ge(y_ready, j + 1)
                act.dma_start(ys_t[bass.ds(j, 1)].rearrange("o p d -> (o p) d"), yb[r][:, :]).then_inc(y_out[r], 16)

            def round_of_tiles(n, first):
                for r in ring:
                    j = RING * n + r
                    for c in range(C0):
                        act.wait_ge(hid_in_ps, C0 * j + (c + 1))
                        if c == 0:
                            act.wait_ge(b1_ready, j + 1)
                            if not first or r >= 2:
                                act.wait_ge(t_in_ps, RING * n + (r - 1))
                        s.activation(hT[r % 2][:, c, :], banks[c][:, 0:P], ACT.Gelu,
                                     bias=b1[r][:, c:c + 1]).then_inc(gelu_done, 1)
                    if r > 0 or not first:
                        send(j - 1, (r - 1) % RING)

            round_of_tiles(0, True)
            with act.Fori(1, nl + 1) as n:
                round_of_tiles(n, False)
            send(nl * RING + (RING - 1), RING - 1)

            pc, pd = banks[6], banks[7]

            def cond(k, stage):
                bp, bd = 7 * k, DVE_COND * k
                if stage == 0:
                    act.wait_ge(c_pe, bp + 1)
                    s.activation(x2T[:, :], pc[:, :], ACT.Identity).then_inc(c_act, 1)
                if stage == 1:
                    act.wait_ge(c_pe, bp + 2)
                    s.activation(th[:, :], pd[0:A1, :], ACT.Tanh, bias=cols[0:A1, 5:6]).then_inc(c_act, 1)
                if stage == 2:
                    act.wait_ge(c_dve, bd + 2)
                    for t in range(BLK):
                        m = s.activation(pe_[:, t, :], ms[:, t, :], ACT.Exp, bias=nm[:, t:t + 1], accum_out=psum_[:, t:t + 1])
                    m.then_inc(c_act, 1)
                if stage == 3:
                    act.wait_ge(c_pe, bp + 4)
                    s.activation(pnT[:, :], pd[:, :], ACT.Identity).then_inc(c_act, 1)
                if stage == 4:
                    act.wait_ge(c_pe, bp + 5)
                    atleast(act, out_acc, k - 1)
                    s.activation(plT[k % 2][:, :], pc[:, :], ACT.Identity).then_inc(c_act, 1)
                if stage == 5:
                    act.wait_ge(c_dve, bd + 4)
                    s.activation(e8[:, :, :].rearrange("p b e -> p (b e)"), ls8[:, :, :].rearrange("p b e -> p (b e)"), ACT.Exp).then_inc(c_act, 1)

            def ffn(k):
                for c in range(NC1):
                    n = NC1 * k + c
                    m = P if c < NE else NSH[c - NE][1]
                    act.wait_ge(gu_in_ps, n + 1)
                    atleast(act, h_ready, n - 1)
                    s.activation(sg[n % 2][0:m, :], banks[n % 2][0:m, :], ACT.Silu).then_inc(silu_done, 1)
                    beside(cond, ACT_STAGES, c, k + 1)

            for n in range(len(ACT_STAGES)):
                cond(0, n)
            for k in range(NB):
                ffn(k)

        @block.vector
        def _(dve):
            v = nc.vector

            class Chain:

                def __init__(self, s, per):
                    self.s, self.per, self.k, self.base = s, per, 0, 0

                def start(self, b):
                    self.base, self.k = self.per * b, 0

                def add(self, ins):
                    self.k += 1
                    assert self.k <= self.per
                    ins.then_inc(self.s, 1)

                def link(self, ins):
                    self.add(ins)
                    dve.wait_ge(self.s, self.base + self.k)

                def join(self):
                    dve.wait_ge(self.s, self.base + self.k)

            cc = Chain(chain_c, 22)
            cc.start(0)
            for t in qexp:
                v.memset(t[:, :, :], 0.0).then_inc(dve_const, 1)
            v.memset(ones_h[:, :, :], 1.0).then_inc(dve_const, 1)
            dve.wait_ge(dve_const, 3)
            dve.wait_ge(w_att, 16 * 8)
            dve.wait_ge(pool_const, FIRST_CONSTS)
            dve.wait_ge(cb_in_ps, 1)
            v.tensor_tensor(cbias[:, 0:1], psY[:, 0:1], cols[:, 2:3], ALU.add)
            v.tensor_tensor(cbias[:, 1:2], psY[:, 1:2], cols[:, 2:3], ALU.add)
            v.tensor_tensor(cbias[:, 2:3], psY[:, 2:3], cols[:, 3:4], ALU.add).then_inc(cb_ready, 1)
            dve.wait_ge(cb_ready, 1)
            cc.link(v.tensor_copy(lens[:, :], lens_i[:, :]))
            cc.add(v.tensor_scalar(nolen[:, :], lens[:, :], 1.0, -BIG, ALU.is_lt, ALU.mult))
            cc.add(v.tensor_scalar(keymask[:, :], lens[:, :], iota_p[:, 0:1], None, ALU.is_gt))
            cc.link(v.tensor_reduce(headmask[:, :], ind[:, :].rearrange("p (g j) -> p j g", g=NG), AX_X, ALU.add))

            def types_constants():
                dve.wait_ge(w_rest, 16 * 8)
                cc.link(v.tensor_copy(types[:, :], types_i[:, :]))
                cc.add(v.tensor_scalar(is_pre[:, :], types[:, :], 0.0, None, ALU.is_equal))
                cc.link(v.tensor_scalar(is_post[:, :], types[:, :], 1.0, None, ALU.is_equal))
                cc.link(v.tensor_tensor(tmp_b[:, :], is_pre[:, :], is_post[:, :], ALU.add))
                cc.link(v.tensor_scalar(is_cloze[:, :], tmp_b[:, :], -1.0, 1.0, ALU.mult, ALU.add))
                assert cc.k == CHAIN_TYPES
                cc.add(v.tensor_scalar(tmp_c[:, 0:1], iota_p[:, 0:1], 1.0, None, ALU.add))
                cc.link(v.tensor_scalar(tmp_c[:, 1:2], iota_p[:, 0:1], -1.0, float(P), ALU.mult, ALU.add))
                cc.link(v.tensor_scalar(count[:, :], is_cloze[:, :], float(P - 1), None, ALU.mult))
                cc.link(v.scalar_tensor_tensor(out=count[:, :], in0=is_pre[:, :], scalar=tmp_c[:, 0:1], in1=count[:, :], op0=ALU.mult, op1=ALU.add))
                cc.link(v.scalar_tensor_tensor(out=count[:, :], in0=is_post[:, :], scalar=tmp_c[:, 1:2], in1=count[:, :], op0=ALU.mult, op1=ALU.add))

            cq, cn, cm, cl, cr = (Chain(x, y) for x, y in ((chain_q, 2), (chain_n, 4), (chain_m, 9), (chain_l, 6), (chain_r, 4)))

            def below_maximum(i, p, g, between=None):
                if not active(i, 1):
                    return
                hs = slice(NJ * g, NJ * (g + 1))
                view = psA[g % 2][:, :].rearrange("p (j k) -> p j k", j=NJ)
                if g == 0:
                    cm.start(i - 1)
                dve.wait_ge(a_in_ps, 4 * (i - 1) + (g + 1))
                cm.add(v.tensor_reduce(mx[:, hs], view, AX_X, ALU.max))
                if between is not None:
                    between(0)
                cm.join()
                cm.add(v.tensor_tensor(top[:, hs], mx[:, hs], selfs[1 - p][:, hs], ALU.max))
                if between is not None:
                    between(1)
                cm.join()
                atleast(dve, pT_in_ps, 4 * (i - 1) + (g - 1))
                v.tensor_tensor(ps[g % 2][:, :, :], view, top[:, hs].unsqueeze(2).broadcast_to([P, NJ, P]), ALU.subtract).then_inc(sub_done, 1)

            def step(i, p, n):
                def slot_stage(stage):
                    if not active(i, 3):
                        return
                    sl = slotf[:, bass.ds(i - 3, 1), :].rearrange("p o k -> p (o k)")
                    if stage == 0:
                        cr.join()
                        cr.add(v.tensor_tensor(rsel[:, :, :], onehot[:, bass.ds(i - 3, 1), :, :].rearrange("p o k e -> p (o k) e"),
                                               rank[:, :].unsqueeze(1).broadcast_to([P, 2, E0]), ALU.mult))
                    if stage == 1:
                        cr.join()
                        cr.add(v.tensor_reduce(sl, rsel[:, :, :], AX_X, ALU.add))
                    if stage == 2:
                        cr.join()
                        atleast(dve, scattered, 32 * (i - 4))
                        carry(dve)
                        v.tensor_copy(slots[1 - p][:, :], sl).then_inc(slots_ready, 1)

                def pick_stage(stage):
                    if not active(i, 2):
                        return
                    b = i - 2
                    if stage == 0:
                        cl.join()
                        carry(dve)
                        cl.add(v.max(top8[:, :], lg[:, :]))
                    if stage == 1:
                        cl.join()
                        carry(dve)
                        cl.add(v.max_index(topi[:, :], top8[:, :], lg[:, :]))
                    if stage == 2:
                        cl.join()
                        cl.add(v.tensor_copy(topf[:, :], topi[:, 0:2]))
                    if stage == 3:
                        cl.join()
                        oh = onehot[:, bass.ds(b, 1), :, :].rearrange("p o k e -> p (o k) e")
                        cl.add(v.tensor_tensor(oh, iota_e[:, :].unsqueeze(1).broadcast_to([P, 2, E0]),
                                               topf[:, :].unsqueeze(2).broadcast_to([P, 2, E0]), ALU.is_equal))
                        cl.add(v.tensor_tensor(gap[:, bass.ds(b, 1)], top8[:, 1:2], top8[:, 0:1], ALU.subtract))
                    if stage == 4:
                        cl.join()
                        atleast(dve, y_in_ps, i - 2)
                        v.tensor_tensor(picked[p][:, :], onehot[:, bass.ds(b, 1), 0, :].rearrange("p o e -> p (o e)"),
                                        onehot[:, bass.ds(b, 1), 1, :].rearrange("p o e -> p (o e)"), ALU.add).then_inc(picks_ready, 1)

                if known(i) and i == 1:
                    types_constants()
                    dve.wait_ge(pool_const, CONSTS)
                below_maximum(i, p, 0)
                below_maximum(i, p, 1)
                if active(i, 2) or active(i, 3):
                    dve.wait_ge(y_in_ps, i - 1)
                if active(i, 2):
                    cl.start(i - 2)
                    v.tensor_tensor(a_all[:, bass.ds(i - 2, 1), :].rearrange("p o d -> p (o d)"), ps_a, boB[:, :], ALU.add).then_inc(a_ready, 1)
                    cl.add(v.tensor_tensor(lg[:, :], ps_lg, gate0bB[:, :], ALU.add))
                    if not active(i, 3):
                        v.tensor_copy(y_token[:, :], ps_lg[:, 0:1]).then_inc(y_read, 1)
                if active(i, 3):
                    cr.start(i - 3)
                    atleast(dve, y_read, i - 2)
                    cr.add(v.tensor_tensor(rank[:, :], ps_rank, held[:, :], ALU.add))
                    v.tensor_tensor(held[:, :], ps_tot, held[:, :], ALU.add).then_inc(y_read, 1)
                    cr.join()
                    cr.add(v.tensor_tensor(rank[:, :], rank[:, :], region_of[:, :], ALU.add))
                if active(i, 1):
                    below_maximum(i, p, 2, slot_stage)
                else:
                    slot_stage(0)
                    slot_stage(1)
                slot_stage(2)
                below_maximum(i, p, 3)
                if active(i, 1):
                    cm.link(v.scalar_tensor_tensor(out=mm[:, :], in0=mx[:, :], scalar=nolen[:, bass.ds(i - 1, 1)], in1=selfs[1 - p][:, :],
                                                   op0=ALU.add, op1=ALU.max))
                    atleast(dve, ws_ready, i - 1)
                    v.tensor_tensor(sm[:, :], selfs[1 - p][:, :], mm[:, :], ALU.subtract).then_inc(shift_ready, 1)
                if active(i, 0):
                    cq.start(i)
                    dve.wait_ge(kqv_in_ps, i + 1)
                    atleast(dve, qexp_pool, 4 * i)
                    cq.add(v.tensor_scalar(qb[:, :], ps_q, cbias[:, 2:3], None, ALU.add))
                pick_stage(0)
                if active(i, 0):
                    cq.join()
                    v.scalar_tensor_tensor(out=prod[:, :], in0=ps_ks, scalar=cbias[:, 1:2], in1=qb[:, :],
                                           op0=ALU.add, op1=ALU.mult).then_inc(prod_ready, 1)
                    dve.wait_ge(z_read, i + 1)
                    cq.add(v.tensor_scalar(kd[:, :], kT[p][:, :], kT[p][:, 0:1], None, ALU.subtract))
                pick_stage(1)
                if active(i, 0):
                    cq.join()
                    atleast(dve, kA_ready, i)
                    v.scalar_tensor_tensor(out=kv[:, :], in0=iota_k[:, :], scalar=lens[:, bass.ds(i, 1)], in1=kd[:, :],
                                           op0=ALU.is_lt, op1=ALU.mult).then_inc(kv_ready, 1)
                pick_stage(2)
                if active(i, 0):
                    atleast(dve, pv_done, 4 * (i - 1))
                    km = keymask[:, bass.ds(i, 1)]
                    v.tensor_scalar(v9[p][:, :, 0:DH], ps_v.rearrange("p (h d) -> p h d", h=H), km, None, ALU.mult)
                pick_stage(3)
                if active(i, 0):
                    v.tensor_scalar(v9[p][:, :, DH:DH + 1], ones_h[:, :, :], km, None, ALU.mult)
                    v.tensor_scalar(vs[p][:, :], ps_vs, 1.0, None, ALU.mult).then_inc(v_ready, 1)
                    dve.wait_ge(self_in_ps, i + 1)
                    v.tensor_copy(selfs[p][:, :], ps_self).then_inc(self_read, 1)
                    dve.wait_ge(self_read, i + 1)
                pick_stage(4)
                if active(i, 1):
                    cn.start(i - 1)
                    dve.wait_ge(ws_ready, i)
                    dve.wait_ge(v_ready, i)
                    wb = ws[1 - p][:, :].unsqueeze(2).broadcast_to([P, H, DH])
                    hd = lambda t: t[:, :].rearrange("p (h d) -> p h d", h=H)
                    cn.add(v.tensor_tensor(hd(t1), hd(vs[1 - p]), wb, ALU.mult))
                    dve.wait_ge(pv_done, 4 * i)
                    o = psO[:, 0:H * (DH + 1)].rearrange("p (h d) -> p h d", h=H)
                    cn.add(v.tensor_tensor(den[:, :], o[:, :, DH:DH + 1].rearrange("p h o -> p (h o)"), ws[1 - p][:, :], ALU.add))
                    cn.join()
                    cn.add(v.tensor_tensor(hd(t2), hd(t1), o[:, :, 0:DH], ALU.add))
                    cn.link(v.reciprocal(rec[:, :], den[:, :]))
                    atleast(dve, x_in_ps, i)
                    v.tensor_tensor(hd(att[1 - p]), hd(t2), rec[:, :].unsqueeze(2).broadcast_to([P, H, DH]), ALU.mult).then_inc(att_ready, 1)

            pipeline(dve, step)

            ct = Chain(chain_t, 40)
            ct.start(0)
            cr.start(B - 1)
            cr.k = 4
            cr.join()
            dve.wait_ge(y_read, STEPS - 2)
            ct.link(v.tensor_scalar(nti[:, :], held[:, :], float(P - 1), None, ALU.add))
            ct.link(v.tensor_scalar(nti[:, :], nti[:, :], 7, None, ALU.arith_shift_right))
            ct.link(v.tensor_copy(ntf[:, :], nti[:, :]))
            ct.link(v.tensor_tensor_scan(incl[:, :], ones_e[:, :], ntf[:, :], 0.0, ALU.mult, ALU.add))
            ct.add(v.tensor_tensor(excl[:, :], incl[:, :], ntf[:, :], ALU.subtract))
            ct.link(v.tensor_scalar(below[:, :], incl[:, :], iota_p[:, 0:1], None, ALU.is_le))
            ct.add(v.tensor_reduce(ej[:, :], below[:, :], AX_X, ALU.add))
            ct.link(v.tensor_tensor(under[:, :], below[:, :], incl[:, :], ALU.mult))
            ct.link(v.tensor_reduce(tj[:, :], under[:, :], AX_X, ALU.max))
            ct.link(v.tensor_tensor(tj[:, :], iota_p[:, :], tj[:, :], ALU.subtract))
            ct.link(v.scalar_tensor_tensor(out=tj[:, :], in0=ej[:, :], scalar=float(RUNS), in1=tj[:, :], op0=ALU.mult, op1=ALU.add))
            ct.add(v.tensor_scalar(table[:, 0:1], ej[:, :], float(E0 - 1), None, ALU.min))
            ct.add(v.tensor_scalar(tile_list[:, :], tj[:, :], float(E0 * RUNS - 1), None, ALU.min))
            ct.link(v.tensor_scalar(rounds_i[:, :], incl[:, E0 - 1:E0], -1.0, None, ALU.add))
            v.engine_nop().then_inc(table_ready, 1)
            ct.add(v.tensor_scalar(rounds[:, :], rounds_i[:, :], 2, None, ALU.arith_shift_right))
            dve.wait_ge(table_in_ps, 1)
            ct.link(v.tensor_copy(table_i[:, :], psY[0:1, 0:P]))
            v.engine_nop().then_inc(plan_ready, 1)
            dve.wait_ge(gap_exp, 1)
            ct.link(v.tensor_scalar(g1[:, :], eg[:, :], 1.0, None, ALU.add))
            ct.link(v.reciprocal(g1[:, :], g1[:, :]))
            ct.link(v.tensor_tensor(g2[:, :], g1[:, :], eg[:, :], ALU.mult))
            ct.link(v.scalar_tensor_tensor(out=ybase[:, :], in0=excl[:, :], scalar=float(P), in1=region_of[:, :], op0=ALU.mult, op1=ALU.subtract))
            ct.link(v.tensor_tensor(ysel[:, :, :, :].rearrange("p b k e -> p (b k) e"), onehot[:, :, :, :].rearrange("p b k e -> p (b k) e"),
                                    ybase[:, :].unsqueeze(1).broadcast_to([P, 2 * B, E0]), ALU.mult))
            ct.link(v.tensor_reduce(yoff[:, :, :].rearrange("p b k -> p (b k)"), ysel[:, :, :, :].rearrange("p b k e -> p (b k) e"), AX_X, ALU.add))
            ct.link(v.tensor_tensor(yslotf[:, :, :], slotf[:, :, :], yoff[:, :, :], ALU.add))
            ct.link(v.tensor_copy(yslot[:, :], yslotf[:, :, :].rearrange("p b k -> p (b k)")))
            v.engine_nop().then_inc(yslot_ready, 1)
            dve.wait_ge(rows_in_ps, 1)
            v.tensor_copy(tile_rows[:, :], psX[:, 0:P]).then_inc(rows_ready, 1)
            dve.wait_ge(gT_in_ps, 1)
            ct.add(v.tensor_copy(gate1T[:, :], psZ[:, 0:E1]))
            ct.link(v.tensor_scalar(vB[:, :], onesb[0:A1, :], vcol[:, 0:1], None, ALU.mult))
            v.engine_nop().then_inc(gT_ready, 1)

            nl = dve.value_load(rounds[0:1, 0:1], min_val=MIN_TILES // RING - 1, max_val=MAX_TILES // RING - 1)

            def take_xT(j, r, first):
                dve.wait_ge(xT_in_ps, j + 1)
                if not first or j >= 2:
                    dve.wait_ge(hid_in_ps, C0 * (j - 1))
                v.tensor_copy(xT[r % 2][:, :], banks[4 + r % 2][:, 0:P]).then_inc(xT_ready, 1)
                e = dve.value_load(table_i[0:1, bass.ds(j, 1)], min_val=0, max_val=E0 - 1)
                if not first or j >= RING:
                    dve.wait_ge(gelu_done, C0 * (j - RING + 1))
                carry(dve)
                v.tensor_scalar(b1[r][:, :], b1_all[:, bass.ds(e, 1), :].rearrange("p o c -> p (o c)"), 1.0, None, ALU.mult).then_inc(b1_ready, 1)
                v.tensor_scalar(b2[r][:, :], b2_all[:, bass.ds(e, 1), :].rearrange("p o d -> p (o d)"), 1.0, None, ALU.mult).then_inc(b2_ready, 1)

            def take_y(j, r, n):
                dve.wait_ge(t_in_ps, j + 1)
                dve.wait_ge(b2_ready, j + 1)
                atleast(dve, y_out[r], 16 * n)
                v.tensor_tensor(yb[r][:, :], banks[6 + r % 2][:, 0:P], b2[r][:, :], ALU.add).then_inc(y_ready, 1)

            def round_of_tiles(n):
                first = known(n) and n == 0
                for r in ring:
                    j = RING * n + r
                    take_xT(j + 1, (r + 1) % RING, first)
                    if r > 0 or not first:
                        take_y(j - 1, (r - 1) % RING, n - 1 if r == 0 else n)

            dve.wait_ge(biases_in, 32)
            take_xT(0, 0, True)
            round_of_tiles(0)
            round_of_tiles(1)
            with dve.Fori(2, nl + 1) as n:
                round_of_tiles(n)
            take_y(nl * RING + (RING - 1), RING - 1, nl)

            pc, pd = banks[6], banks[7]
            cx = Chain(chain_x, 1000)

            dve.wait_ge(pool_const, ALL_CONSTS)
            across = lambda t: t[:, :].unsqueeze(1).broadcast_to([P, B, P])
            along = lambda t: t[:, :].unsqueeze(2).broadcast_to([P, B, P])
            cx.link(v.tensor_tensor(poolbias[:, :, :], across(prebias), along(is_pre), ALU.mult))
            for mask, kind in ((postbias, is_post), (clozebias, is_cloze)):
                cx.link(v.tensor_tensor(term, across(mask), along(kind), ALU.mult))
                cx.link(v.tensor_tensor(poolbias[:, :, :], poolbias[:, :, :], term, ALU.add))

            def cond(k, stage):
                bp, ba = 7 * k, ACT_COND * k
                blk = slice(BLK * k, BLK * (k + 1))
                if stage == 0 and k > 0:
                    v.engine_nop().then_inc(c_dve, 1)
                if stage == 0 and k == 0:
                    dve.wait_ge(gathered[k % 2], 16 * 2 * BLK * (k // 2 + 1))
                    dve.wait_ge(xr_in[k % 2], 16 * (k // 2 + 1))
                    for t in range(BLK):
                        b = BLK * k + t
                        cx.add(v.scalar_tensor_tensor(out=mix1[:, t, :], in0=y1[k % 2][:, t, :], scalar=g1[:, b:b + 1], in1=xr[k % 2][:, t, :],
                                                      op0=ALU.mult, op1=ALU.add))
                    cx.join()
                    for t in range(BLK):
                        b = BLK * k + t
                        cx.add(v.scalar_tensor_tensor(out=mix2[:, t, :], in0=y2[k % 2][:, t, :], scalar=g2[:, b:b + 1], in1=mix1[:, t, :],
                                                      op0=ALU.mult, op1=ALU.add))
                    cx.join()
                    dve.wait_ge(a_ready, B)
                    v.tensor_tensor(x2[:, blk, :], mix2[:, :, :], a_all[:, blk, :], ALU.add).then_inc(x2_first, 1)
                    v.engine_nop().then_inc(c_dve, 1)
                if stage == 1:
                    dve.wait_ge(c_pe, bp + 3)
                    cx.link(v.tensor_tensor(ms[:, :, :], pc[:, :].rearrange("p (b l) -> p b l", b=BLK), poolbias[:, blk, :], ALU.add))
                    v.tensor_reduce(nm[:, :], ms[:, :, :], AX_X, ALU.max, negate=True).then_inc(c_dve, 1)
                if stage == 2:
                    dve.wait_ge(c_act, ba + 3)
                    cx.link(v.tensor_tensor(sc_[:, :], psum_[:, :], count[:, blk], ALU.mult))
                    cx.link(v.reciprocal(rs_[:, :], sc_[:, :]))
                    v.tensor_tensor(pn[:, :, :], pe_[:, :, :], rs_[:, :].unsqueeze(2).broadcast_to([P, BLK, P]), ALU.mult).then_inc(c_dve, 1)
                if stage == 3:
                    dve.wait_ge(c_pe, bp + 6)
                    cx.link(v.tensor_copy(l8[:, :, :].rearrange("p b e -> p (b e)"), pd[:, 0:BLK * E1]))
                    cx.link(v.tensor_reduce(nl8[:, :], l8[:, :, :], AX_X, ALU.max))
                    v.tensor_tensor(ls8[:, :, :], l8[:, :, :], nl8[:, :].unsqueeze(2).broadcast_to([P, BLK, E1]), ALU.subtract).then_inc(c_dve, 1)
                if stage == 4:
                    dve.wait_ge(c_act, ba + 6)
                    cx.link(v.tensor_reduce(z8[:, :], e8[:, :, :], AX_X, ALU.add))
                    cx.link(v.reciprocal(rz8[:, :], z8[:, :]))
                    cx.link(v.tensor_tensor(pr8[:, :, :], e8[:, :, :], rz8[:, :].unsqueeze(2).broadcast_to([P, BLK, E1]), ALU.mult))
                    for t in range(BLK):
                        cx.add(v.max(top1[:, t, :], pr8[:, t, :]))
                    cx.join()
                if stage == 5:
                    for t in range(BLK):
                        cx.add(v.max_index(topi1[:, t, :], top1[:, t, :], pr8[:, t, :]))
                    cx.join()
                    cx.link(v.tensor_copy(topf1[:, :, :], topi1[:, :, 0:2]))
                    for s in range(2):
                        cx.add(v.tensor_tensor(oh1[:, :, s, :], iota_e[:, 0:E1].unsqueeze(1).broadcast_to([P, BLK, E1]),
                                               topf1[:, :, s:s + 1].broadcast_to([P, BLK, E1]), ALU.is_equal))
                    cx.add(v.tensor_tensor(s8[:, :], top1[:, :, 0:1].rearrange("p b o -> p (b o)"), top1[:, :, 1:2].rearrange("p b o -> p (b o)"), ALU.add))
                    cx.join()
                if stage == 6:
                    cx.add(v.tensor_tensor(pick1[:, :, :], oh1[:, :, 0, :], oh1[:, :, 1, :], ALU.add))
                    cx.link(v.tensor_scalar(s8[:, :], s8[:, :], 1e-20, None, ALU.add))
                    cx.add(v.tensor_tensor(c8a[:, :, :], pick1[:, :, :], pr8[:, :, :], ALU.mult))
                    cx.link(v.reciprocal(r8[:, :], s8[:, :]))
                    cx.link(v.tensor_scalar(r8[:, :], r8[:, :], ROUTE_SCALE, None, ALU.mult))
                    cx.link(v.tensor_tensor(c8[:, :, :], c8a[:, :, :], r8[:, :].unsqueeze(2).broadcast_to([P, BLK, E1]), ALU.mult))
                    parts = [cparts[:, :, E1 * n:E1 * (n + 1)] for n in range(3)]
                    cx.link(v.tensor_copy(parts[0], c8[:, :, :]))
                    cx.link(v.tensor_tensor(c8r[:, :, :], c8[:, :, :], parts[0], ALU.subtract))
                    cx.link(v.tensor_copy(parts[1], c8r[:, :, :]))
                    cx.link(v.tensor_tensor(c8s[:, :, :], c8r[:, :, :], parts[1], ALU.subtract))
                    v.tensor_copy(parts[2], c8s[:, :, :]).then_inc(c_dve, 1)
                if stage == 7:
                    dve.wait_ge(c_pe, bp + 7)
                    atleast(dve, out_acc, k - 1)
                    v.tensor_copy(cT[k % 2][:, :], pc[:, :].bitcast(BF16)[0:3 * E1, 0:W]).then_inc(cond_ready, 1)

            def ffn(k):
                for c in range(NC1):
                    n = NC1 * k + c
                    m = P if c < NE else NSH[c - NE][1]
                    dve.wait_ge(silu_done, n + 1)
                    dve.wait_ge(gu_in_ps, n + 1)
                    atleast(dve, out_acc, k)
                    if c < NE:
                        atleast(dve, h_ready, n)
                        cf[0] += 1
                        v.tensor_tensor(hu[:, :], sg[n % 2][:, :], banks[2 + n % 2][:, :], ALU.mult).then_inc(chain_h, 1)
                        dve.wait_ge(chain_h, cf[0])
                        dve.wait_ge(wt_in_ps, NE * k + c + 1)
                        v.tensor_tensor(h1[:, c, :], hu[:, :], banks[4][:, :], ALU.mult).then_inc(h_ready, 1)
                    else:
                        v.tensor_tensor(h1[0:m, c, :], sg[n % 2][0:m, :], banks[2 + n % 2][0:m, :], ALU.mult).then_inc(h_ready, 1)
                    beside(cond, DVE_STAGES, c, k + 1)
                dve.wait_ge(out_acc, k + 1)
                if k >= 2:
                    dve.wait_ge(ob_out[k % 2], 16 * (k // 2))
                v.tensor_tensor(ob[k % 2][:, :, :], banks[5][:, :].rearrange("p (b d) -> p b d", b=BLK), x2[:, BLK * k:BLK * (k + 1), :],
                                ALU.add).then_inc(ob_ready, 1)

            cf = [0]
            for n in range(len(DVE_STAGES)):
                cond(0, n)
            for k in range(NB):
                ffn(k)


_INS = ['x', 'fside_BxSxS_0', 'itok_B_18_1004', 'itok_B_0_2', 'L0_cond_Wq', 'L0_cond_bq', 'L0_cond_Wk', 'L0_cond_bk', 'L0_cond_Wv',
        'L0_cond_bv', 'L0_cond_Wo', 'L0_cond_bo', 'L0_cond_b_prev', 'L0_cond_b_self', 'L0_ffn_gate_w', 'L0_ffn_gate_b', 'L0_ffn_w1',
        'L0_ffn_b1', 'L0_ffn_w2', 'L0_ffn_b2', 'L1_cond_W1', 'L1_cond_b1', 'L1_cond_v', 'L1_ffn_gate_w', 'L1_ffn_w_gate', 'L1_ffn_w_up',
        'L1_ffn_w_down', 'L1_ffn_sw_gate', 'L1_ffn_sw_up', 'L1_ffn_sw_down']


def kernel(**inputs):
    import numpy as _np
    import concourse.bacc as _bacc
    from concourse import mybir as _mybir
    from concourse.bass_utils import run_bass_kernel_spmd as _run

    nc = _bacc.Bacc("TRN2", target_bir_lowering=False, num_devices=1)
    arrays, aps = {}, {}
    for name in _INS:
        v = _np.ascontiguousarray(inputs[name])
        arrays[f"in_{name}_dram"] = v
        aps[name] = nc.dram_tensor(f"in_{name}_dram", v.shape, _mybir.dt.from_np(v.dtype), kind="ExternalInput").ap()
    out = nc.dram_tensor("out_0_dram", (B, P, P), F32, kind="ExternalOutput").ap()
    at = nc.dram_tensor("attention_output", (B, P, P), F32, kind="Internal").ap()
    ids = nc.dram_tensor("expert_tokens", (E0 * RUNS, P), F32, kind="Internal").ap()
    ys = nc.dram_tensor("expert_outputs", (YROWS, P), F32, kind="Internal").ap()
    attention_moe_kernel(nc, aps, out, at, ids, ys)
    r = _run(nc, [arrays], core_ids=[0])
    return r.results[0]["out_0_dram"]
```
